# Optimizing a Trainium2 kernel written in Bass

```python
import numpy as np
import jax
import jax.numpy as jnp

def _softmax(x, axis=-1):
    return jax.nn.softmax(x, axis=axis)

def _gelu(x):
    return jax.nn.gelu(x, approximate=True)

def _silu(x):
    return jax.nn.silu(x)

def _sigmoid(x):
    return jax.nn.sigmoid(x)

def _layernorm(x, axis=-1, eps=1e-05):
    m = jnp.mean(x, axis=axis, keepdims=True)
    v = jnp.var(x, axis=axis, keepdims=True)
    return (x - m) / jnp.sqrt(v + eps)

def _scatter_add(tgt, idx, src, axis=0):
    return tgt.at[idx].add(src)

def _segment_sum(src, seg, n):
    return jax.ops.segment_sum(src, seg, n)
kernel_name = 'mk_perceiver_d2_seqx_r4_c53f6c'

def setup_inputs(seed: int=0):
    np.random.seed(seed)
    _w = jnp.asarray

    def _rec_inputs():
        import jax
        import jax.numpy as jnp
        _rk = jax.random.key(seed)
        x = -0.000125 + 0.9999 * jax.random.normal(jax.random.fold_in(_rk, 1), (8, 64, 256), jnp.float32)
        _lenS = 64 - jax.random.randint(jax.random.fold_in(_rk, 7), (8,), 0, max(1, 64 // 4) + 1, jnp.int32)
        _lenS2 = 1601 - jax.random.randint(jax.random.fold_in(_rk, 8), (8,), 0, max(1, 1601 // 4) + 1, jnp.int32)
        _ctx_768P = jax.random.normal(jax.random.fold_in(_rk, 11), (8, 16, 192), jnp.float32)
        _ctx_768c = jax.random.dirichlet(jax.random.fold_in(_rk, 511), 0.3 * jnp.ones((16,), jnp.float32), (8, 1601))
        _ctx_768t = jnp.einsum('bsk,bkd->bsd', _ctx_768c, _ctx_768P)
        _ctx_768t = _ctx_768t * jax.lax.rsqrt(jnp.mean(jnp.square(_ctx_768t)) + 1e-12) * 0.953939
        ctx_768 = 0.00272024 + 0.999456 * (_ctx_768t + 0.3 * jax.random.normal(jax.random.fold_in(_rk, 611), (8, 1601, 192), jnp.float32))
        return (x, ctx_768)
    x, ctx_768 = _rec_inputs()

    def _L0_xattn_setup():
        import jax, jax.numpy as jnp
        import numpy as np
        HEADS = 16
        DIM_HEAD = 64
        SCALE = DIM_HEAD ** (-0.5)
        QUERY_DIM = 256
        CONTEXT_DIM = 192
        INNER_DIM = HEADS * DIM_HEAD
        key = jax.random.key(seed)
        ks = jax.random.split(key, 7)
        B, Nq, Nk = (8, 1024, 77)
        x = jax.random.normal(ks[0], (B, Nq, QUERY_DIM), dtype=jnp.float32)
        context = jax.random.normal(ks[1], (B, Nk, CONTEXT_DIM), dtype=jnp.float32)
        Wq = jax.random.normal(ks[2], (QUERY_DIM, INNER_DIM), dtype=jnp.float32) * QUERY_DIM ** (-0.5)
        Wk = jax.random.normal(ks[3], (CONTEXT_DIM, INNER_DIM), dtype=jnp.float32) * CONTEXT_DIM ** (-0.5)
        Wv = jax.random.normal(ks[4], (CONTEXT_DIM, INNER_DIM), dtype=jnp.float32) * CONTEXT_DIM ** (-0.5)
        Wo = jax.random.normal(ks[5], (INNER_DIM, QUERY_DIM), dtype=jnp.float32) * INNER_DIM ** (-0.5)
        bo = jnp.zeros((QUERY_DIM,), dtype=jnp.float32)
        return {'x': x, 'context': context, 'Wq': Wq, 'Wk': Wk, 'Wv': Wv, 'Wo': Wo, 'bo': bo}
    _L0_xattn_all = _L0_xattn_setup()
    _L0_xattn_in = {k: v for k, v in _L0_xattn_all.items() if k in ('Wq', 'Wk', 'Wv', 'Wo', 'bo')}
    del _L0_xattn_all

    def _L0_attn_setup():
        import jax, jax.numpy as jnp
        import numpy as np
        B, N, D, H = (4, 1024, 256, 16)
        HD = D // H
        EPS_NORM = 1e-12
        EPS_LN = 1e-05

        def _silu(x):
            return x * jax.nn.sigmoid(x)

        def _simple_gla(q, k, v, f):
            qT = jnp.moveaxis(q, 1, 0)
            kT = jnp.moveaxis(k, 1, 0)
            vT = jnp.moveaxis(v, 1, 0)
            fT = jnp.moveaxis(f, 1, 0)

            def step(S, inp):
                qt, kt, vt, ft = inp
                S = jnp.exp(ft)[..., None, None] * S + kt[..., :, None] * vt[..., None, :]
                o = jnp.einsum('bhk,bhkv->bhv', qt, S)
                return (S, o)
            S0 = jnp.zeros((q.shape[0], q.shape[2], q.shape[3], v.shape[3]), q.dtype)
            _, o = jax.lax.scan(step, S0, (qT, kT, vT, fT))
            return jnp.moveaxis(o, 0, 1)
        key = jax.random.key(seed)
        ks = jax.random.split(key, 9)
        s = 0.02
        return {'x': jax.random.normal(ks[0], (B, N, D), jnp.float32), 'Wq': jax.random.normal(ks[1], (D, D), jnp.float32) * s, 'Wk': jax.random.normal(ks[2], (D, D), jnp.float32) * s, 'Wv': jax.random.normal(ks[3], (D, D), jnp.float32) * s, 'Wf': jax.random.normal(ks[4], (H, D), jnp.float32) * s, 'Wg1': jax.random.normal(ks[5], (HD, D), jnp.float32) * s, 'Wg2': jax.random.normal(ks[6], (D, HD), jnp.float32) * s, 'ln_w': jnp.ones((D,), jnp.float32), 'Wo': jax.random.normal(ks[7], (D, D), jnp.float32) * s}
    _L0_attn_all = _L0_attn_setup()
    _L0_attn_in = {k: v for k, v in _L0_attn_all.items() if k in ('Wq', 'Wk', 'Wv', 'Wf', 'Wg1', 'Wg2', 'ln_w', 'Wo')}
    del _L0_attn_all

    def _L0_ffn_setup():
        import jax, jax.numpy as jnp
        import numpy as np
        B, S, H, I, E = (2, 1024, 256, 128, 8)
        key = jax.random.key(seed)
        ks = jax.random.split(key, 5)
        scale_h = 1.0 / np.sqrt(H)
        scale_i = 1.0 / np.sqrt(I)
        return {'hidden_states': jax.random.normal(ks[0], (B, S, H), dtype=jnp.float32), 'gate_w': jax.random.normal(ks[1], (E, H), dtype=jnp.float32) * scale_h, 'w_gate': jax.random.normal(ks[2], (E, I, H), dtype=jnp.float32) * scale_h, 'w_up': jax.random.normal(ks[3], (E, I, H), dtype=jnp.float32) * scale_h, 'w_down': jax.random.normal(ks[4], (E, H, I), dtype=jnp.float32) * scale_i}
    _L0_ffn_all = _L0_ffn_setup()
    _L0_ffn_in = {k: v for k, v in _L0_ffn_all.items() if k in ('gate_w', 'w_gate', 'w_up', 'w_down')}
    del _L0_ffn_all

    def _L1_xattn_setup():
        import jax, jax.numpy as jnp
        import numpy as np
        N_HEADS = 16
        key = jax.random.key(seed)
        ks = jax.random.split(key, 8)
        b, l, m = (8, 256, 256)
        d_embed, d_cross = (256, 192)
        s_q = 1.0 / np.sqrt(d_embed)
        s_kv = 1.0 / np.sqrt(d_cross)
        return {'x': jax.random.normal(ks[0], (b, l, d_embed), jnp.float32), 'y': jax.random.normal(ks[1], (b, m, d_cross), jnp.float32), 'Wq': jax.random.normal(ks[2], (d_embed, d_embed), jnp.float32) * s_q, 'bq': jax.random.normal(ks[3], (d_embed,), jnp.float32) * 0.01, 'Wkv': jax.random.normal(ks[4], (2 * d_embed, d_cross), jnp.float32) * s_kv, 'bkv': jax.random.normal(ks[5], (2 * d_embed,), jnp.float32) * 0.01, 'Wo': jax.random.normal(ks[6], (d_embed, d_embed), jnp.float32) * s_q, 'bo': jax.random.normal(ks[7], (d_embed,), jnp.float32) * 0.01}
    _L1_xattn_all = _L1_xattn_setup()
    _L1_xattn_in = {k: v for k, v in _L1_xattn_all.items() if k in ('Wq', 'bq', 'Wkv', 'bkv', 'Wo', 'bo')}
    del _L1_xattn_all

    def _L1_attn_setup():
        import jax, jax.numpy as jnp
        import numpy as np
        DIM = 256
        HEADS = 16
        HEAD_DIM = DIM // HEADS
        COLLAPSE_THRESHOLD = 0.27
        SHARPNESS = 15.0
        LN_EPS = 1e-05
        NORM_EPS = 1e-12

        def _layernorm(x, gamma, beta):
            mu = jnp.mean(x, axis=-1, keepdims=True)
            var = jnp.mean(jnp.square(x - mu), axis=-1, keepdims=True)
            return (x - mu) * jax.lax.rsqrt(var + LN_EPS) * gamma + beta

        def _l2_normalize(x):
            n = jnp.sqrt(jnp.sum(jnp.square(x), axis=-1, keepdims=True))
            return x / jnp.maximum(n, NORM_EPS)
        key = jax.random.key(seed)
        ks = jax.random.split(key, 9)
        B, T = (2, 512)
        s = 1.0 / np.sqrt(DIM)
        sh = 1.0 / np.sqrt(HEAD_DIM)
        return {'x': jax.random.normal(ks[0], (B, T, DIM), dtype=jnp.float32), 'w_q': jax.random.normal(ks[1], (DIM, DIM), dtype=jnp.float32) * s, 'w_k': jax.random.normal(ks[2], (DIM, DIM), dtype=jnp.float32) * s, 'w_v': jax.random.normal(ks[3], (DIM, DIM), dtype=jnp.float32) * s, 'g_q': jax.random.normal(ks[4], (HEAD_DIM,), dtype=jnp.float32) * sh, 'g_k': jax.random.normal(ks[5], (HEAD_DIM,), dtype=jnp.float32) * sh, 'w_o': jax.random.normal(ks[6], (DIM, DIM), dtype=jnp.float32) * s, 'b_o': jnp.zeros((DIM,), dtype=jnp.float32), 'gamma': jnp.ones((DIM,), dtype=jnp.float32), 'beta': jnp.zeros((DIM,), dtype=jnp.float32)}
    _L1_attn_all = _L1_attn_setup()
    _L1_attn_in = {k: v for k, v in _L1_attn_all.items() if k in ('w_q', 'w_k', 'w_v', 'g_q', 'g_k', 'w_o', 'b_o', 'gamma', 'beta')}
    del _L1_attn_all

    def _L1_ffn_setup():
        import jax, jax.numpy as jnp
        import numpy as np

        def _ste(w, w_q):
            return w + jax.lax.stop_gradient(w_q - w)

        def quantize_w8_per(w, axis):
            amax = jnp.clip(jnp.max(jnp.abs(w), axis=axis, keepdims=True), 1e-08, None)
            scale = 127.0 / amax
            w_q = jnp.clip(jnp.round(w * scale), -128.0, 127.0) / scale
            return _ste(w, w_q)

        def quantize_a16(x):
            amax = jnp.clip(jnp.max(jnp.abs(x)), 1e-08, None)
            scale = 32767.0 / amax
            x_q = jnp.clip(jnp.round(x * scale), -32768.0, 32767.0) / scale
            return _ste(x, x_q)
        key = jax.random.key(seed)
        k1, k2, k3 = jax.random.split(key, 3)
        d_model, d_ff = (256, 1024)
        x = jax.random.normal(k1, (4, 512, d_model), dtype=jnp.float32)
        W_in = jax.random.normal(k2, (d_model, d_ff), dtype=jnp.float32) / np.sqrt(d_model)
        b_in = jnp.zeros((d_ff,), dtype=jnp.float32)
        W_out = jax.random.normal(k3, (d_ff, d_model), dtype=jnp.float32) / np.sqrt(d_ff)
        b_out = jnp.zeros((d_model,), dtype=jnp.float32)
        return {'x': x, 'W_in': W_in, 'b_in': b_in, 'W_out': W_out, 'b_out': b_out}
    _L1_ffn_all = _L1_ffn_setup()
    _L1_ffn_in = {k: v for k, v in _L1_ffn_all.items() if k in ('W_in', 'b_in', 'W_out', 'b_out')}
    del _L1_ffn_all
    return {'x': x, 'ctx_768': ctx_768, 'L0_xattn_Wq': _L0_xattn_in['Wq'], 'L0_xattn_Wk': _L0_xattn_in['Wk'], 'L0_xattn_Wv': _L0_xattn_in['Wv'], 'L0_xattn_Wo': _L0_xattn_in['Wo'], 'L0_xattn_bo': _L0_xattn_in['bo'], 'L0_attn_Wq': _L0_attn_in['Wq'], 'L0_attn_Wk': _L0_attn_in['Wk'], 'L0_attn_Wv': _L0_attn_in['Wv'], 'L0_attn_Wf': _L0_attn_in['Wf'], 'L0_attn_Wg1': _L0_attn_in['Wg1'], 'L0_attn_Wg2': _L0_attn_in['Wg2'], 'L0_attn_ln_w': _L0_attn_in['ln_w'], 'L0_attn_Wo': _L0_attn_in['Wo'], 'L0_ffn_gate_w': _L0_ffn_in['gate_w'], 'L0_ffn_w_gate': _L0_ffn_in['w_gate'], 'L0_ffn_w_up': _L0_ffn_in['w_up'], 'L0_ffn_w_down': _L0_ffn_in['w_down'], 'L1_xattn_Wq': _L1_xattn_in['Wq'], 'L1_xattn_bq': _L1_xattn_in['bq'], 'L1_xattn_Wkv': _L1_xattn_in['Wkv'], 'L1_xattn_bkv': _L1_xattn_in['bkv'], 'L1_xattn_Wo': _L1_xattn_in['Wo'], 'L1_xattn_bo': _L1_xattn_in['bo'], 'L1_attn_w_q': _L1_attn_in['w_q'], 'L1_attn_w_k': _L1_attn_in['w_k'], 'L1_attn_w_v': _L1_attn_in['w_v'], 'L1_attn_g_q': _L1_attn_in['g_q'], 'L1_attn_g_k': _L1_attn_in['g_k'], 'L1_attn_w_o': _L1_attn_in['w_o'], 'L1_attn_b_o': _L1_attn_in['b_o'], 'L1_attn_gamma': _L1_attn_in['gamma'], 'L1_attn_beta': _L1_attn_in['beta'], 'L1_ffn_W_in': _L1_ffn_in['W_in'], 'L1_ffn_b_in': _L1_ffn_in['b_in'], 'L1_ffn_W_out': _L1_ffn_in['W_out'], 'L1_ffn_b_out': _L1_ffn_in['b_out']}

def reference(x, ctx_768, L0_xattn_Wq, L0_xattn_Wk, L0_xattn_Wv, L0_xattn_Wo, L0_xattn_bo, L0_attn_Wq, L0_attn_Wk, L0_attn_Wv, L0_attn_Wf, L0_attn_Wg1, L0_attn_Wg2, L0_attn_ln_w, L0_attn_Wo, L0_ffn_gate_w, L0_ffn_w_gate, L0_ffn_w_up, L0_ffn_w_down, L1_xattn_Wq, L1_xattn_bq, L1_xattn_Wkv, L1_xattn_bkv, L1_xattn_Wo, L1_xattn_bo, L1_attn_w_q, L1_attn_w_k, L1_attn_w_v, L1_attn_g_q, L1_attn_g_k, L1_attn_w_o, L1_attn_b_o, L1_attn_gamma, L1_attn_beta, L1_ffn_W_in, L1_ffn_b_in, L1_ffn_W_out, L1_ffn_b_out):
    import jax
    import jax.numpy as jnp

    def _L0_xattn_ref(x, context, Wq, Wk, Wv, Wo, bo):
        import jax, jax.numpy as jnp
        import numpy as np
        HEADS = 16
        DIM_HEAD = 64
        SCALE = DIM_HEAD ** (-0.5)
        QUERY_DIM = 256
        CONTEXT_DIM = 192
        INNER_DIM = HEADS * DIM_HEAD
        B, Nq, _ = x.shape
        Nk = context.shape[1]
        q = x @ Wq
        k = context @ Wk
        v = context @ Wv
        q = q.reshape(B, Nq, HEADS, DIM_HEAD).transpose(0, 2, 1, 3)
        k = k.reshape(B, Nk, HEADS, DIM_HEAD).transpose(0, 2, 1, 3)
        v = v.reshape(B, Nk, HEADS, DIM_HEAD).transpose(0, 2, 1, 3)
        sim = jnp.einsum('bhid,bhjd->bhij', q, k) * SCALE
        attn = jax.nn.softmax(sim, axis=-1)
        out = jnp.einsum('bhij,bhjd->bhid', attn, v)
        out = out.transpose(0, 2, 1, 3).reshape(B, Nq, INNER_DIM)
        return out @ Wo + bo

    def _L0_attn_ref(x, Wq, Wk, Wv, Wf, Wg1, Wg2, ln_w, Wo):
        import jax, jax.numpy as jnp
        import numpy as np
        B, N, D, H = (4, 1024, 256, 16)
        HD = D // H
        EPS_NORM = 1e-12
        EPS_LN = 1e-05

        def _silu(x):
            return x * jax.nn.sigmoid(x)

        def _simple_gla(q, k, v, f):
            qT = jnp.moveaxis(q, 1, 0)
            kT = jnp.moveaxis(k, 1, 0)
            vT = jnp.moveaxis(v, 1, 0)
            fT = jnp.moveaxis(f, 1, 0)

            def step(S, inp):
                qt, kt, vt, ft = inp
                S = jnp.exp(ft)[..., None, None] * S + kt[..., :, None] * vt[..., None, :]
                o = jnp.einsum('bhk,bhkv->bhv', qt, S)
                return (S, o)
            S0 = jnp.zeros((q.shape[0], q.shape[2], q.shape[3], v.shape[3]), q.dtype)
            _, o = jax.lax.scan(step, S0, (qT, kT, vT, fT))
            return jnp.moveaxis(o, 0, 1)
        b, n, d = x.shape
        q = _silu(x @ Wq.T).reshape(b, n, H, HD)
        k = _silu(x @ Wk.T).reshape(b, n, H, HD)
        v = _silu(x @ Wv.T).reshape(b, n, H, HD)
        f = jax.nn.log_sigmoid(x @ Wf.T)
        k = k / jnp.maximum(jnp.linalg.norm(k, axis=-1, keepdims=True), EPS_NORM)
        o = _simple_gla(q, k, v, f).reshape(b, n, d)
        gate = jax.nn.sigmoid(x @ Wg1.T @ Wg2.T)
        o = o * gate
        mu = jnp.mean(o, axis=-1, keepdims=True)
        xc = o - mu
        var = jnp.mean(xc * xc, axis=-1, keepdims=True)
        o = xc / jnp.sqrt(var + EPS_LN) * ln_w
        return o @ Wo.T

    def _L0_ffn_ref(hidden_states, gate_w, w_gate, w_up, w_down):
        import jax, jax.numpy as jnp
        import numpy as np
        B, S, H, I, E = (2, 1024, 256, 128, 8)
        b, s, h = hidden_states.shape
        x = hidden_states.reshape(-1, h)
        logits = x @ gate_w.T
        top_v = jnp.max(logits, axis=-1)
        sel = jnp.argmax(logits, axis=-1)
        rw = jax.nn.sigmoid(top_v)
        out = jnp.zeros_like(x)
        n_exp = gate_w.shape[0]
        for e in range(n_exp):
            mask = (sel == e).astype(x.dtype)
            xs = x * (rw * mask)[:, None]
            g = xs @ w_gate[e].T
            u = xs @ w_up[e].T
            out = out + u * jax.nn.silu(g) @ w_down[e].T
        return out.reshape(b, s, h)

    def _L1_xattn_ref(x, y, Wq, bq, Wkv, bkv, Wo, bo):
        import jax, jax.numpy as jnp
        import numpy as np
        N_HEADS = 16
        b, l, d = x.shape
        m = y.shape[1]
        h = N_HEADS
        dh = d // h
        q = (jnp.einsum('bld,ed->ble', x, Wq) + bq).reshape(b, l, h, dh)
        kv = (jnp.einsum('bmc,ec->bme', y, Wkv) + bkv).reshape(b, m, h, 2 * dh)
        k, v = (kv[..., :dh], kv[..., dh:])
        scale = 1.0 / jnp.sqrt(jnp.asarray(dh, x.dtype))
        att = jax.nn.softmax(jnp.einsum('blhd,bmhd->blmh', q, k) * scale, axis=2)
        out = jnp.einsum('blmh,bmhd->blhd', att, v).reshape(b, l, d)
        return jnp.einsum('bld,ed->ble', out, Wo) + bo

    def _L1_attn_ref(x, w_q, w_k, w_v, g_q, g_k, w_o, b_o, gamma, beta):
        import jax, jax.numpy as jnp
        import numpy as np
        DIM = 256
        HEADS = 16
        HEAD_DIM = DIM // HEADS
        COLLAPSE_THRESHOLD = 0.27
        SHARPNESS = 15.0
        LN_EPS = 1e-05
        NORM_EPS = 1e-12

        def _layernorm(x, gamma, beta):
            mu = jnp.mean(x, axis=-1, keepdims=True)
            var = jnp.mean(jnp.square(x - mu), axis=-1, keepdims=True)
            return (x - mu) * jax.lax.rsqrt(var + LN_EPS) * gamma + beta

        def _l2_normalize(x):
            n = jnp.sqrt(jnp.sum(jnp.square(x), axis=-1, keepdims=True))
            return x / jnp.maximum(n, NORM_EPS)
        B, T, D = x.shape
        x_norm = _layernorm(x, gamma, beta)
        q = (x_norm @ w_q).reshape(B, T, HEADS, HEAD_DIM).transpose(0, 2, 1, 3)
        k = (x_norm @ w_k).reshape(B, T, HEADS, HEAD_DIM).transpose(0, 2, 1, 3)
        v = (x @ w_v).reshape(B, T, HEADS, HEAD_DIM).transpose(0, 2, 1, 3)
        q = _l2_normalize(q)
        k = _l2_normalize(k)
        align = jnp.einsum('bhqd,bhkd->bhqk', q, k)
        resonance = 0.5 + 0.5 * jnp.tanh((align - COLLAPSE_THRESHOLD) * SHARPNESS)
        gate_q = 0.25 + 0.75 * jax.nn.sigmoid(jnp.einsum('bhtd,d->bht', q, g_q))
        gate_k = 0.25 + 0.75 * jax.nn.sigmoid(jnp.einsum('bhtd,d->bht', k, g_k))
        modulation = resonance * gate_q[..., :, None] * gate_k[..., None, :]
        fused = jnp.einsum('bhqk,bhkd->bhqd', modulation, v)
        fused = fused.transpose(0, 2, 1, 3).reshape(B, T, HEADS * HEAD_DIM)
        return fused @ w_o + b_o

    def _L1_ffn_ref(x, W_in, b_in, W_out, b_out):
        import jax, jax.numpy as jnp
        import numpy as np

        def _ste(w, w_q):
            return w + jax.lax.stop_gradient(w_q - w)

        def quantize_w8_per(w, axis):
            amax = jnp.clip(jnp.max(jnp.abs(w), axis=axis, keepdims=True), 1e-08, None)
            scale = 127.0 / amax
            w_q = jnp.clip(jnp.round(w * scale), -128.0, 127.0) / scale
            return _ste(w, w_q)

        def quantize_a16(x):
            amax = jnp.clip(jnp.max(jnp.abs(x)), 1e-08, None)
            scale = 32767.0 / amax
            x_q = jnp.clip(jnp.round(x * scale), -32768.0, 32767.0) / scale
            return _ste(x, x_q)
        W_in_sim = quantize_w8_per(W_in, axis=0)
        W_out_sim = quantize_w8_per(W_out, axis=1)
        x_sim = quantize_a16(x)
        hidden = jax.nn.gelu(x_sim @ W_in_sim + b_in, approximate=False)
        hidden_sim = quantize_a16(hidden)
        out = hidden_sim @ W_out_sim + b_out
        return out
    x = x + _L0_xattn_ref(_layernorm(x, axis=-1), ctx_768, L0_xattn_Wq, L0_xattn_Wk, L0_xattn_Wv, L0_xattn_Wo, L0_xattn_bo)
    x = x + _L0_attn_ref(_layernorm(x, axis=-1), L0_attn_Wq, L0_attn_Wk, L0_attn_Wv, L0_attn_Wf, L0_attn_Wg1, L0_attn_Wg2, L0_attn_ln_w, L0_attn_Wo)
    x = x + _L0_ffn_ref(_layernorm(x, axis=-1), L0_ffn_gate_w, L0_ffn_w_gate, L0_ffn_w_up, L0_ffn_w_down)
    x = x + _L1_xattn_ref(_layernorm(x, axis=-1), ctx_768, L1_xattn_Wq, L1_xattn_bq, L1_xattn_Wkv, L1_xattn_bkv, L1_xattn_Wo, L1_xattn_bo)
    x = x + _L1_attn_ref(_layernorm(x, axis=-1), L1_attn_w_q, L1_attn_w_k, L1_attn_w_v, L1_attn_g_q, L1_attn_g_k, L1_attn_w_o, L1_attn_b_o, L1_attn_gamma, L1_attn_beta)
    x = x + _L1_ffn_ref(_layernorm(x, axis=-1), L1_ffn_W_in, L1_ffn_b_in, L1_ffn_W_out, L1_ffn_b_out)
    return x

_drawn_inputs = setup_inputs


def setup_inputs(seed=0):
    import zlib

    import numpy as np

    out = dict(_drawn_inputs(seed))
    spreads = {'L0_xattn_bo': (0.0, 0.1),
     'L0_attn_ln_w': (1.0, 0.2),
     'L1_attn_b_o': (0.0, 0.1),
     'L1_attn_gamma': (1.0, 0.2),
     'L1_attn_beta': (0.0, 0.1),
     'L1_ffn_b_in': (0.0, 0.38),
     'L1_ffn_b_out': (0.0, 0.1)}
    factors = {'L0_attn_Wg1': 3.088,
     'L0_attn_Wg2': 3.015,
     'L1_xattn_bq': 8.0,
     'L1_xattn_bkv': 3.716,
     'L1_xattn_bo': 3.474}
    for name, (base, spread) in spreads.items():
        noise = np.random.default_rng([zlib.crc32(name.encode()), seed]).standard_normal(out[name].shape)
        drawn = base * np.exp(spread * noise) if base else spread * noise
        out[name] = jnp.asarray(drawn.astype(out[name].dtype))
    for name, factor in factors.items():
        out[name] = (out[name] * factor).astype(out[name].dtype)
    return out
```

```python
from contextlib import ExitStack

import numpy as np
import concourse.bass as bass
from concourse import mybir
from concourse.alu_op_type import AluOpType as ALU

F32 = mybir.dt.float32
BF16 = mybir.dt.bfloat16
ACT = mybir.ActivationFunctionType
AX_X = mybir.AxisListType.X

P = 128
B, NQ, D = 8, 64, 256
TOK = B * NQ
TT = TOK // P
KC = D // P
M, DC = 1601, 192
DB = DC - P
MC = -(-M // P)
ML = M - (MC - 1) * P
H = 16
PAIRS = H // 2
BANK = 512
SEG = [(j * BANK, min(BANK, M - j * BANK)) for j in range(-(-M // BANK))]
TGRP = [(g, range(4 * g, min(4 * g + 4, MC))) for g in range(-(-MC // 4))]
NG = len(TGRP)
E, I = 8, 128
FF = 1024
FC = FF // P


class Shared:
    pass


class Parts:
    def __init__(self, sb, tag, natural):
        if natural:
            self.nh, self.nl = (sb(f"{tag}_{n}", [P, MC, DC], BF16) for n in ("nh", "nl"))
        self.ah, self.al, self.bh, self.bl = (sb(f"{tag}_{n}", [P, M + 1], BF16) for n in ("ah", "al", "bh", "bl"))


def names(nc, ctx):
    def sb(name, shape, dt=F32):
        return ctx.enter_context(nc.sbuf_tensor(name, shape, dt))

    def ps(name, shape, dt=F32):
        return ctx.enter_context(nc.psum_tensor(name, shape, dt))

    def sem(name):
        return ctx.enter_context(nc.semaphore(name))

    return sb, ps, sem


def chained(eng, sem):
    done = [0]

    def link(ins):
        done[0] += 1
        ins.then_inc(sem, 1)
        eng.wait_ge(sem, done[0])

    return link


def load_inputs(nc, m, d):
    with ExitStack() as ctx:
        with nc.Block() as block:
            @block.sync
            def _(sp):
                sp.dma_start(m.x[:, :, :], d["x"]).then_inc(m.x_loaded, 16)
                sp.dma_start(m.ident[:, :], d["ident"]).then_inc(m.const_loaded, 16)
                sp.dma_start(m.maskneg[:, :], d["maskneg"]).then_inc(m.const_loaded, 16)
                sp.dma_start(m.mask05[:, :], d["mask05"]).then_inc(m.const_loaded, 16)
                sp.dma_start(m.small[:, :], d["small"]).then_inc(m.const_loaded, 16)
                sp.dma_start(m.wv0[:, :, :], d["wv0"]).then_inc(m.w0_loaded, 16)
                sp.dma_start(m.wo0[:, :, :], d["wo0"]).then_inc(m.w0_loaded, 16)
                sp.dma_start(m.bo0[:, :], d["bo0"]).then_inc(m.w0_loaded, 16)


def layer_norm(nc, m, tag, src, dst, dstT, affine=None):
    with ExitStack() as ctx:
        sb, ps, sem = names(nc, ctx)
        stats = sb(f"{tag}_stats", [P, TT, 6])
        mv = sb(f"{tag}_meanvar", [P, TT, 2])
        std = sb(f"{tag}_std", [P, TT])
        rstd = sb(f"{tag}_rstd", [P, TT])
        pT = ps(f"{tag}_pT", [P, KC, BANK])
        stats_done, mv_done, std_done, rstd_done, normed, scaled, done, turned, copied = (
            sem(f"{tag}_{n}") for n in
            ("stats_done", "mv_done", "std_done", "rstd_done", "normed", "scaled", "done", "turned", "copied"))
        with nc.Block() as block:
            @block.vector
            def _(dve):
                dve.wait_ge(m.x_loaded, 16)
                for t in range(TT):
                    dve.bn_stats(stats[:, t, :], src[:, t, :]).then_inc(stats_done, 1)
                for t in range(TT):
                    dve.wait_ge(stats_done, t + 1)
                    dve.bn_aggr(mv[:, t, :], stats[:, t, :]).then_inc(mv_done, 1)
                dve.wait_ge(std_done, 1)
                dve.reciprocal(rstd[:, :], std[:, :]).then_inc(rstd_done, 1)
                dve.wait_ge(rstd_done, 1)
                for t in range(TT):
                    o = dve.tensor_scalar(dst[:, t, :], src[:, t, :], mv[:, t, 0:1], rstd[:, t:t + 1],
                                          ALU.subtract, ALU.mult)
                    o.then_inc(normed if affine else done, 1)
                if affine:
                    dve.wait_ge(m.late_loaded, m.late_n)
                    for t in range(TT):
                        dve.wait_ge(normed, t + 1)
                        dve.tensor_tensor(dst[:, t, :], dst[:, t, :], affine[0], ALU.mult).then_inc(
                            scaled if affine[1] is not None else done, 1)
                    if affine[1] is not None:
                        for t in range(TT):
                            dve.wait_ge(scaled, t + 1)
                            dve.tensor_tensor(dst[:, t, :], dst[:, t, :], affine[1], ALU.add).then_inc(done, 1)
                if dstT is not None:
                    dve.wait_ge(turned, KC * TT)
                    dve.tensor_copy(dstT[:, 1, :], pT[:, 1, :]).then_inc(copied, 1)

            @block.scalar
            def _(act):
                act.wait_ge(mv_done, TT)
                act.wait_ge(m.const_loaded, m.const_n)
                act.activation(std[:, :], mv[:, :, 1], ACT.Sqrt, bias=m.eps).then_inc(std_done, 1)
                if dstT is not None:
                    act.wait_ge(turned, TT)
                    act.activation(dstT[:, 0, :], pT[:, 0, :], ACT.Copy).then_inc(copied, 1)

            if dstT is not None:
                @block.tensor
                def _(pe):
                    pe.wait_ge(m.const_loaded, m.const_n)
                    pe.wait_ge(done, TT)
                    for c in range(KC):
                        for t in range(TT):
                            pe.transpose(pT[:, c, P * t:P * t + P], dst[:, t, P * c:P * c + P],
                                         m.ident[:, :]).then_inc(turned, 1)


def l0x_queries(nc, m, d):
    with ExitStack() as ctx:
        sb, ps, sem = names(nc, ctx)
        wq = sb("wq0", [P, KC, 1024])
        wk = sb("wk0", [P, PAIRS, D])
        wkh = sb("wk0h", [P, PAIRS, D], BF16)
        wkl = sb("wk0l", [P, PAIRS, D], BF16)
        qzh = sb("qzh", [P, 2, 2, TOK], BF16)
        qzl = sb("qzl", [P, 2, 2, TOK], BF16)
        pQ = ps("pQ", [P, 2, BANK])
        pK = ps("pK", [P, 4, BANK])
        w_in, wkh_done, wkl_done, zeroed, q_mm, q_hi, q_lo, qk_mm, qk_hi, qk_lo = (
            sem(n) for n in ("q0_w_in", "q0_wkh", "q0_wkl", "q0_zeroed", "q0_q_mm", "q0_q_hi", "q0_q_lo",
                             "q0_qk_mm", "q0_qk_hi", "q0_qk_lo"))
        with nc.Block() as block:
            @block.sync
            def _(sp):
                sp.dma_start(wq[:, :, :], d["wq0"]).then_inc(w_in, 16)
                sp.dma_start(wk[:, :, :], d["wk0"]).then_inc(w_in, 16)

            @block.gpsimd
            def _(pool):
                pool.memset(qzh[:, :, :, :], 0.0).then_inc(zeroed, 1)
                pool.memset(qzl[:, :, :, :], 0.0).then_inc(zeroed, 1)
                pool.wait_ge(w_in, 32)
                pool.tensor_copy(wkh[:, :, :], wk[:, :, :]).then_inc(wkh_done, 1)
                pool.wait_ge(wkh_done, 1)
                pool.tensor_tensor(wkl[:, :, :], wk[:, :, :], wkh[:, :, :], ALU.subtract).then_inc(wkl_done, 1)

            @block.tensor
            def _(pe):
                pe.wait_ge(w_in, 32)
                for p in range(PAIRS + 1):
                    if p < PAIRS:
                        if p >= 2:
                            pe.wait_ge(q_lo, 2 * (p - 1))
                        for c in range(KC):
                            mm = pe.matmul(pQ[:, p % 2, :], wq[:, c, P * p:P * p + P], m.xnT[:, c, :],
                                           start=(c == 0), stop=(c == KC - 1))
                        mm.then_inc(q_mm, 1)
                    if p >= 1:
                        r = (p - 1) % 2
                        pe.wait_ge(q_lo, 2 * p)
                        pe.wait_ge(wkl_done, 1)
                        for n in range(4 * (p - 1), 4 * p):
                            h, part = (n % 4) // 2, n % 2
                            if n >= 4:
                                pe.wait_ge(qk_lo, n - 3)
                            w = slice(P * part, P * part + P)
                            for a, (wt, q) in enumerate(((wkh, qzh), (wkh, qzl), (wkl, qzh))):
                                mm = pe.matmul(pK[:, n % 4, :], wt[:, p - 1, w], q[:, r, h, :],
                                               start=(a == 0), stop=(a == 2))
                            mm.then_inc(qk_mm, 1)

            def qu_out(n):
                p, h, part = n // 4, (n % 4) // 2, n % 2
                s = slice(NQ * h, NQ * h + NQ)
                return part, (m.quA[:, 0, :, p, s], m.quA[:, 1, :, p, s], m.quB[:, :, p, s])

            @block.scalar
            def _(act):
                act.wait_ge(zeroed, 2)
                for p in range(PAIRS + 1):
                    if p < PAIRS:
                        act.wait_ge(q_mm, p + 1)
                        if p >= 2:
                            act.wait_ge(qk_mm, 4 * (p - 1))
                        for h in range(2):
                            s = slice(64 * h, 64 * h + 64)
                            act.activation(qzh[s, p % 2, h, :], pQ[s, p % 2, :], ACT.Copy).then_inc(q_hi, 1)
                    if p >= 1:
                        for n in range(4 * (p - 1), 4 * p):
                            part, (ah, al, b) = qu_out(n)
                            act.wait_ge(qk_mm, n + 1)
                            src = pK[:, n % 4, :].rearrange("p (b i) -> p b i", b=B)
                            act.activation(b if part else ah, src, ACT.Copy).then_inc(qk_hi, 1)

            @block.vector
            def _(dve):
                for p in range(PAIRS + 1):
                    if p < PAIRS:
                        for h in range(2):
                            s = slice(64 * h, 64 * h + 64)
                            dve.wait_ge(q_hi, 2 * p + h + 1)
                            dve.tensor_tensor(qzl[s, p % 2, h, :], pQ[s, p % 2, :], qzh[s, p % 2, h, :],
                                              ALU.subtract).then_inc(q_lo, 1)
                    if p >= 1:
                        for n in range(4 * (p - 1), 4 * p):
                            part, (ah, al, b) = qu_out(n)
                            dve.wait_ge(qk_hi, n + 1)
                            src = pK[:, n % 4, :].rearrange("p (b i) -> p b i", b=B)
                            if part:
                                dve.tensor_tensor(b[64:128], src[64:128], b[64:128], ALU.subtract).then_inc(qk_lo, 1)
                            else:
                                dve.tensor_tensor(al, src, ah, ALU.subtract).then_inc(qk_lo, 1)


def l0x_attention(nc, m, d):
    SCALE = 64 ** -0.5
    T2 = 2 * PAIRS
    with ExitStack() as ctx:
        sb, ps, sem = names(nc, ctx)
        stN = sb("stN", [P, MC, DC])
        stA = sb("stA", [P, M])
        stB = sb("stB", [P, M])
        hl = [Parts(sb, f"ctx{n}", True) for n in range(2)]
        prob = sb("prob", [P, M])
        pth = sb("pth", [P, MC, P], BF16)
        ptl = sb("ptl", [P, MC, P], BF16)
        mx = sb("mx", [P, 2])
        nmax = sb("nmax", [P, 2])
        rsum = sb("rsum", [P, 2])
        rinv = sb("rinv", [P, 2])
        u = sb("u", [P, D])
        pS = ps("pS", [P, 4 * BANK])
        pT = ps("pT", [P, 2, BANK])
        pU = ps("pU", [P, D])
        pV = ps("pV", [P, 2, P])
        (ctx_in, begun, split, s_done, exp_done, t_done, hi_done, lo_done, av_done, mx_done, nmax_done, rinv_done,
         u_done, ut_done, uhi_done, ulo_done) = (sem("a0_" + n) for n in (
             "ctx_in", "begun", "split", "s_done", "exp_done", "t_done", "hi_done", "lo_done", "av_done", "mx_done",
             "nmax_done", "rinv_done", "u_done", "ut_done", "uhi_done", "ulo_done"))
        NS = 6

        with nc.Block() as block:
            @block.sync
            def _(sp):
                with sp.Fori(0, B) as b:
                    sp.wait_ge(split, 1 + b * NS)
                    sp.dma_start(stN[:, :, :], d["ctxn"][bass.ds(b, 1)].rearrange("o p c f -> (o p) c f")).then_inc(ctx_in, 16)
                    sp.dma_start(stA[:, :], d["ctxT"][bass.ds(b, 1), 0:P].rearrange("o p c -> (o p) c")).then_inc(ctx_in, 16)
                    for s in (0, 64):
                        sp.dma_start(stB[s:s + 64, :], d["ctxT"][bass.ds(b, 1), P:DC].rearrange("o p c -> (o p) c")).then_inc(ctx_in, 16)

            def split_batch(pool, b, o):
                pool.wait_ge(ctx_in, (b + 1) * 64)
                pool.sem_inc(begun, 1)
                parts = ((o.ah[:, 0:M], o.al[:, 0:M], stA[:, :]), (o.bh[:, 0:M], o.bl[:, 0:M], stB[:, :]),
                         (o.nh[:, :, :], o.nl[:, :, :], stN[:, :, :]))
                for hi, _, src in parts:
                    pool.tensor_copy(hi, src).then_inc(split, 1)
                for n, (hi, lo, src) in enumerate(parts):
                    pool.wait_ge(split, 1 + b * NS + n + 1)
                    pool.tensor_tensor(lo, src, hi, ALU.subtract).then_inc(split, 1)

            @block.gpsimd
            def _(pool):
                for s in (split,):
                    pool.sem_inc(s, 1)
                for par in range(2):
                    split_batch(pool, par, hl[par])
                with pool.Fori(1, B // 2) as i:
                    b = i * 2
                    for par in range(2):
                        pool.wait_ge(av_done, 1 + b * PAIRS + (par - 1) * PAIRS)
                        split_batch(pool, b + par, hl[par])

            @block.tensor
            def _(pe):
                for s in (s_done, t_done, av_done, ut_done):
                    pe.sem_inc(s, 1)
                with pe.Fori(0, B // 2) as i:
                    b = i * 2
                    k0 = b * PAIRS

                    def scores(t, j):
                        par, p = t // PAIRS, t % PAIRS
                        c = hl[par]
                        s, w = SEG[j]
                        qa = [m.quA[:, n, bass.ds(b + par, 1), p, :].rearrange("p o r -> p (o r)") for n in (0, 1)]
                        qb = m.quB[:, bass.ds(b + par, 1), p, :].rearrange("p o r -> p (o r)")
                        if j == 0:
                            pe.wait_ge(exp_done, 1 + k0 + t)
                            if p == 0:
                                pe.wait_ge(split, 1 + (b + par + 1) * NS)
                        for a, (q, k) in enumerate(((qa[0], c.ah), (qa[0], c.al), (qa[1], c.ah), (qb, c.bh), (qb, c.bl))):
                            mm = pe.matmul(pS[:, s:s + w], q, k[:, s:s + w], start=(a == 0), stop=(a == 4))
                        if j in (1, 3):
                            mm.then_inc(s_done, 1)

                    def turn_probs(t, g):
                        n = 4 * t + g
                        if g == 0:
                            pe.wait_ge(exp_done, 1 + k0 + t + 1)
                        pe.wait_ge(lo_done, 1 + k0 * NG + max(n - 1, 0))
                        for c in TGRP[g][1]:
                            w = min(P, M - P * c)
                            mm = pe.transpose(pT[0:w, n % 2, P * (c % 4):P * (c % 4) + P],
                                              prob[:, P * c:P * c + w], m.ident[:, :])
                        mm.then_inc(t_done, 1)

                    def values(t):
                        c = hl[t // PAIRS]
                        pe.wait_ge(u_done, 1 + (k0 + t) * 2)
                        for n in range(MC):
                            w = min(P, M - P * n)
                            if n % 4 == 0:
                                pe.wait_ge(lo_done, 1 + (k0 + t) * NG + n // 4 + 1)
                            for a, (pr, cx) in enumerate(((pth, c.nh), (pth, c.nl), (ptl, c.nh))):
                                mm = pe.matmul(pU[:, 0:DC], pr[0:w, n, :], cx[0:w, n, :],
                                               start=(n == 0 and a == 0), stop=(n == MC - 1 and a == 2))
                        mm.then_inc(av_done, 1)

                    def turn_result(t):
                        pe.wait_ge(u_done, 1 + (k0 + t + 1) * 2)
                        pe.wait_ge(ulo_done, 1 + (k0 + t) * 2)
                        for n in range(2):
                            pe.transpose(pV[:, n, :], u[:, P * n:P * n + P], m.ident[:, :]).then_inc(ut_done, 1)

                    for t in range(T2 + 2):
                        for j in range(4):
                            if t < T2:
                                scores(t, j)
                            if 1 <= t <= T2:
                                turn_probs(t - 1, j)
                        if t >= 2:
                            turn_result(t - 2)
                        if 1 <= t <= T2:
                            values(t - 1)

            @block.scalar
            def _(act):
                for s in (exp_done, hi_done, uhi_done):
                    act.sem_inc(s, 1)
                with act.Fori(0, B // 2) as i:
                    b = i * 2
                    k0 = b * PAIRS
                    for t in range(T2 + 2):
                        if 1 <= t <= T2:
                            act.wait_ge(av_done, 1 + k0 + t - 1)
                            for g, cs in TGRP:
                                n = 4 * (t - 1) + g
                                w = min(P, M - P * cs[0])
                                act.wait_ge(t_done, 1 + (k0 + t - 1) * NG + g + 1)
                                act.activation(pth[0:w, cs[0]:cs[-1] + 1, :], pT[0:w, n % 2, 0:P * len(cs)].rearrange(
                                    "p (c r) -> p c r", r=P), ACT.Copy).then_inc(hi_done, 1)
                        if t < T2:
                            act.wait_ge(nmax_done, 1 + k0 + t + 1)
                            act.wait_ge(t_done, 1 + (k0 + t) * NG)
                            act.activation(prob[:, :], pS[:, 0:M], ACT.Exp, bias=nmax[:, t % 2:t % 2 + 1], scale=SCALE,
                                           accum_out=rsum[:, t % 2:t % 2 + 1]).then_inc(exp_done, 1)
                        if t >= 2:
                            par, p = (t - 2) // PAIRS, (t - 2) % PAIRS
                            for n in range(2):
                                act.wait_ge(ut_done, 1 + (k0 + t - 1) * 2)
                                o = m.quB[:, bass.ds(b + par, 1), p, :] if n else m.quA[:, 0, bass.ds(b + par, 1), p, :]
                                act.activation(o.rearrange("p o r -> p (o r)"), pV[:, n, :], ACT.Copy).then_inc(uhi_done, 1)

            @block.vector
            def _(dve):
                for s in (lo_done, mx_done, nmax_done, rinv_done, u_done, ulo_done):
                    dve.sem_inc(s, 1)
                with dve.Fori(0, B // 2) as i:
                    b = i * 2
                    k0 = b * PAIRS

                    def low_probs(t, g):
                        cs = TGRP[g][1]
                        n = 4 * t + g
                        w = min(P, M - P * cs[0])
                        dve.wait_ge(hi_done, 1 + (k0 + t) * NG + g + 1)
                        dve.tensor_tensor(ptl[0:w, cs[0]:cs[-1] + 1, :], pT[0:w, n % 2, 0:P * len(cs)].rearrange(
                            "p (c r) -> p c r", r=P), pth[0:w, cs[0]:cs[-1] + 1, :], ALU.subtract).then_inc(lo_done, 1)

                    def maxima(t, half):
                        a, z = (0, 2 * BANK) if half == 0 else (2 * BANK, M)
                        dve.wait_ge(s_done, 1 + (k0 + t) * 2 + half + 1)
                        dve.tensor_reduce(mx[:, half:half + 1], pS[:, a:z], AX_X, ALU.max, negate=True).then_inc(mx_done, 1)

                    for t in range(T2 + 2):
                        for half in range(2):
                            if 1 <= t <= T2:
                                low_probs(t - 1, 2 * half)
                                low_probs(t - 1, 2 * half + 1)
                            if t < T2:
                                maxima(t, half)
                        if t < T2:
                            dve.wait_ge(mx_done, 1 + (k0 + t + 1) * 2)
                            dve.tensor_scalar(nmax[:, t % 2:t % 2 + 1], mx[:, 0:1], mx[:, 1:2], SCALE, ALU.min,
                                              ALU.mult).then_inc(nmax_done, 1)
                        if t >= 2:
                            par, p = (t - 2) // PAIRS, (t - 2) % PAIRS
                            ah, al = (m.quA[:, n, bass.ds(b + par, 1), p, :].rearrange("p o r -> p (o r)") for n in (0, 1))
                            bb = m.quB[64:128, bass.ds(b + par, 1), p, :].rearrange("p o r -> p (o r)")
                            dve.wait_ge(uhi_done, 1 + (k0 + t - 1) * 2)
                            dve.tensor_tensor(al, pV[:, 0, :], ah, ALU.subtract).then_inc(ulo_done, 1)
                            dve.tensor_tensor(bb, pV[64:128, 1, :], bb, ALU.subtract).then_inc(ulo_done, 1)
                        if 1 <= t <= T2:
                            s = (t - 1) % 2
                            dve.wait_ge(exp_done, 1 + k0 + t)
                            dve.reciprocal(rinv[:, s:s + 1], rsum[:, s:s + 1]).then_inc(rinv_done, 1)
                            dve.wait_ge(rinv_done, 1 + k0 + t)
                            dve.wait_ge(av_done, 1 + k0 + t)
                            dve.wait_ge(ut_done, 1 + (k0 + t - 1) * 2)
                            dve.tensor_scalar(u[:, 0:DC], pU[:, 0:DC], rinv[:, s:s + 1], None, ALU.mult).then_inc(u_done, 1)
                            dve.tensor_scalar(u[:, DC:D], pU[:, P:DC], rinv[:, s:s + 1], None, ALU.mult).then_inc(u_done, 1)


def l0x_output(nc, m, d):
    with ExitStack() as ctx:
        sb, ps, sem = names(nc, ctx)
        wvh, wvl = (sb(n, [P, 2, 1024], BF16) for n in ("wv0h", "wv0l"))
        woh, wol = (sb(n, [P, PAIRS, D], BF16) for n in ("wo0h", "wo0l"))
        oh, ol = (sb(n, [P, PAIRS, TOK], BF16) for n in ("o0h", "o0l"))
        pO = ps("pO", [P, 2, BANK])
        pX = ps("pX", [P, TT, BANK])
        whi, wlo, o_mm, o_hi, o_lo, x_mm, x_done = (
            sem("o0_" + n) for n in ("whi", "wlo", "o_mm", "o_hi", "o_lo", "x_mm", "x_done"))
        with nc.Block() as block:
            @block.tensor
            def _(pe):
                for p in range(PAIRS + 1):
                    if p < PAIRS:
                        if p == 0:
                            pe.wait_ge(wlo, 1)
                        if p >= 2:
                            pe.wait_ge(o_lo, p - 1)
                        ops = ((wvh, 0, 0), (wvh, 0, 1), (wvl, 0, 0), (wvh, 1, 2), (wvl, 1, 2))
                        for a, (w, part, q) in enumerate(ops):
                            for h in range(2):
                                s = slice(NQ * h, NQ * h + NQ)
                                mov = m.quB[:, :, p, s] if q == 2 else m.quA[:, q, :, p, s]
                                mm = pe.matmul(pO[64 * h:64 * h + 64, p % 2, :].rearrange("p (b i) -> p b i", b=B),
                                               w[:, part, P * p + 64 * h:P * p + 64 * h + 64], mov,
                                               start=(a == 0), stop=(a == 4))
                        mm.then_inc(o_mm, 1)
                    if p >= 1:
                        pe.wait_ge(o_lo, p)
                        if p == 1:
                            pe.wait_ge(wlo, 2)
                        for t in range(TT):
                            s = slice(P * t, P * t + P)
                            for a, (o, w) in enumerate(((oh, woh), (oh, wol), (ol, woh))):
                                pe.matmul(pX[:, t, 0:D], o[:, p - 1, s], w[:, p - 1, :],
                                          start=(p == 1 and a == 0), stop=False)
                for t in range(TT):
                    pe.matmul(pX[:, t, 0:D], m.ones_row, m.bo0[:, :], start=False, stop=True).then_inc(x_mm, 1)

            @block.scalar
            def _(act):
                act.wait_ge(m.w0_loaded, 48)
                act.activation(wvh[:, :, :], m.wv0[:, :, :], ACT.Copy).then_inc(whi, 1)
                act.activation(woh[:, :, :], m.wo0[:, :, :], ACT.Copy).then_inc(whi, 1)
                for p in range(PAIRS):
                    act.wait_ge(o_mm, p + 1)
                    act.activation(oh[:, p, :], pO[:, p % 2, :], ACT.Copy).then_inc(o_hi, 1)

            @block.vector
            def _(dve):
                dve.wait_ge(whi, 1)
                dve.tensor_tensor(wvl[:, :, :], m.wv0[:, :, :], wvh[:, :, :], ALU.subtract).then_inc(wlo, 1)
                dve.wait_ge(whi, 2)
                dve.tensor_tensor(wol[:, :, :], m.wo0[:, :, :], woh[:, :, :], ALU.subtract).then_inc(wlo, 1)
                for p in range(PAIRS):
                    dve.wait_ge(o_hi, p + 1)
                    dve.tensor_tensor(ol[:, p, :], pO[:, p % 2, :], oh[:, p, :], ALU.subtract).then_inc(o_lo, 1)
                for t in range(TT):
                    dve.wait_ge(x_mm, t + 1)
                    dve.tensor_tensor(m.x[:, t, :], m.x[:, t, :], pX[:, t, 0:D], ALU.add).then_inc(x_done, 1)


def project(nc, m, tag, srcT, w, bias_row, src=None):
    with ExitStack() as ctx:
        sb, ps, sem = names(nc, ctx)
        pX = ps(f"{tag}_pX", [P, TT, BANK])
        pT = ps(f"{tag}_pT", [P, KC, BANK])
        turned, copied, x_mm, x_done = (sem(f"{tag}_{n}") for n in ("turned", "copied", "x_mm", "x_done"))
        with nc.Block() as block:
            @block.tensor
            def _(pe):
                if src is not None:
                    for c in range(KC):
                        for t in range(TT):
                            pe.transpose(pT[:, c, P * t:P * t + P], src[:, t, P * c:P * c + P],
                                         m.ident[:, :]).then_inc(turned, 1)
                for c in range(KC):
                    if src is not None:
                        pe.wait_ge(copied, c + 1)
                    for t in range(TT):
                        mm = pe.matmul(pX[:, t, 0:D], srcT[:, c, P * t:P * t + P], w[:, c, :], start=(c == 0),
                                       stop=(c == KC - 1 and bias_row is None))
                        if c == KC - 1 and bias_row is not None:
                            mm = pe.matmul(pX[:, t, 0:D], m.ones_row, bias_row, start=False, stop=True)
                        if c == KC - 1:
                            mm.then_inc(x_mm, 1)

            if src is not None:
                @block.scalar
                def _(act):
                    for c in range(KC):
                        act.wait_ge(turned, TT * (c + 1))
                        act.activation(srcT[:, c, :], pT[:, c, :], ACT.Copy).then_inc(copied, 1)

            @block.vector
            def _(dve):
                for t in range(TT):
                    dve.wait_ge(x_mm, t + 1)
                    dve.tensor_tensor(m.x[:, t, :], m.x[:, t, :], pX[:, t, 0:D], ALU.add).then_inc(x_done, 1)


def heads16(nc, m, tag, qT, kT, vhl, o, decay):
    with ExitStack() as ctx:
        sb, ps, sem = names(nc, ctx)
        qm = sb(f"{tag}_qm", [P, KC, 8, TOK])
        arg = sb(f"{tag}_arg", [P, 2, BANK])
        ex = sb(f"{tag}_ex", [P, 2, BANK])
        wt = sb(f"{tag}_wt", [P, 2, BANK])
        wh = sb(f"{tag}_wh", [P, 2, BANK], BF16)
        wl = sb(f"{tag}_wl", [P, 2, BANK], BF16)
        o2 = sb(f"{tag}_o2", [P, TT, H, 16])
        pA = ps(f"{tag}_pA", [P, 2, BANK])
        pD = ps(f"{tag}_pD", [P, 2, BANK])
        pO = ps(f"{tag}_pO", [P, TT, H, 32])
        qm_dve, qm_pool, a_mm, d_mm, arg_done, ex_done, wt_done, wh_done, wl_done, av_mm, o2_done, o_done = (
            sem(f"{tag}_{n}") for n in ("qm_dve", "qm_pool", "a_mm", "d_mm", "arg_done", "ex_done", "wt_done",
                                        "wh_done", "wl_done", "av_mm", "o2_done", "o_done"))
        G = 4 * TT
        hmask = m.small[:, SMALL["hmask"]:SMALL["hmask"] + 8]
        with nc.Block() as block:
            @block.tensor
            def _(pe):
                for g in range(G + 1):
                    if g < G:
                        t, q = g // 4, g % 4
                        s = slice(P * t, P * t + P)
                        if g == 0:
                            pe.wait_ge(qm_dve, 8)
                            pe.wait_ge(qm_pool, 8)
                        if decay is not None:
                            if g >= 2:
                                pe.wait_ge(arg_done, g - 1)
                            F, nF = decay
                            pe.matmul(pD[:, g % 2, :], nF[:, s], m.late["onehot"][:, 4 * q:4 * q + 4, :].rearrange(
                                "p h r -> p (h r)"), start=True, stop=False)
                            for h in range(4):
                                mm = pe.matmul(pD[:, g % 2, P * h:P * h + P], m.late["onehot"][:, 4 * q + h, :], F[:, s],
                                               start=False, stop=(h == 3))
                            mm.then_inc(d_mm, 1)
                        if g >= 2:
                            pe.wait_ge(wt_done if decay is not None else ex_done, g - 1)
                        c = q // 2
                        pe.matmul(pA[:, g % 2, :].rearrange("p (h r) -> p h r", h=4), kT[:, c, s],
                                  qm[:, c, 4 * (q % 2):4 * (q % 2) + 4, s], start=True, stop=True).then_inc(a_mm, 1)
                    if g >= 1:
                        t, q = (g - 1) // 4, (g - 1) % 4
                        pe.wait_ge(wh_done, g)
                        pe.wait_ge(wl_done, g)
                        for h in range(4):
                            n, s = 4 * q + h, slice(P * h, P * h + P)
                            pe.matmul(pO[:, t, n, :], wh[:, (g - 1) % 2, s], vhl[:, t, n, :], start=True, stop=False)
                            mm = pe.matmul(pO[:, t, n, 0:16], wl[:, (g - 1) % 2, s], vhl[:, t, n, 0:16],
                                           start=False, stop=True)
                        mm.then_inc(av_mm, 1)

            @block.scalar
            def _(act):
                def cast(g):
                    act.wait_ge(wt_done, g + 1)
                    if g >= 2:
                        act.wait_ge(av_mm, g - 1)
                    act.activation(wh[:, g % 2, :], wt[:, g % 2, :], ACT.Copy).then_inc(wh_done, 1)

                for g in range(G):
                    if decay is not None:
                        act.wait_ge(arg_done, g + 1)
                        if g >= 2:
                            act.wait_ge(wt_done, g - 1)
                        act.activation(ex[:, g % 2, :], arg[:, g % 2, :], ACT.Exp).then_inc(ex_done, 1)
                    else:
                        act.wait_ge(a_mm, g + 1)
                        if g >= 2:
                            act.wait_ge(wt_done, g - 1)
                        act.activation(ex[:, g % 2, :], pA[:, g % 2, :], ACT.Tanh, bias=m.tanh_bias,
                                       scale=15.0).then_inc(ex_done, 1)
                    if g >= 1:
                        cast(g - 1)
                cast(G - 1)
                for t in range(TT):
                    act.wait_ge(av_mm, 4 * (t + 1))
                    act.activation(o2[:, t, :, :], pO[:, t, :, 16:32], ACT.Copy).then_inc(o2_done, 1)

            @block.vector
            def _(dve):
                for n in range(8):
                    dve.tensor_scalar(qm[:, 0, n, :], qT[:, 0, :], hmask[:, n:n + 1], None, ALU.mult).then_inc(qm_dve, 1)
                for g in range(G + 1):
                    if decay is not None and g < G:
                        dve.wait_ge(d_mm, g + 1)
                        if g >= 2:
                            dve.wait_ge(ex_done, g - 1)
                        dve.tensor_tensor(arg[:, g % 2, :], pD[:, g % 2, :], m.maskneg[:, :], ALU.min).then_inc(arg_done, 1)
                    if g >= 1:
                        r = (g - 1) % 2
                        dve.wait_ge(ex_done, g)
                        if g >= 3:
                            dve.wait_ge(wl_done, g - 2)
                            dve.wait_ge(wh_done, g - 2)
                        if decay is not None:
                            dve.wait_ge(a_mm, g)
                            dve.tensor_tensor(wt[:, r, :], pA[:, r, :], ex[:, r, :], ALU.mult).then_inc(wt_done, 1)
                        else:
                            dve.scalar_tensor_tensor(wt[:, r, :], ex[:, r, :], 1.0, m.mask05[:, :], ALU.add,
                                                     ALU.mult).then_inc(wt_done, 1)
                for t in range(TT):
                    dve.wait_ge(o2_done, t + 1)
                    dve.tensor_tensor(o[:, t, :].rearrange("p (h e) -> p h e", h=H), pO[:, t, :, 0:16], o2[:, t, :, :],
                                      ALU.add).then_inc(o_done, 1)

            @block.gpsimd
            def _(pool):
                for n in range(8):
                    pool.tensor_scalar(qm[:, 1, n, :], qT[:, 1, :], hmask[:, n:n + 1], None, ALU.mult).then_inc(qm_pool, 1)
                for g in range(G):
                    pool.wait_ge(wh_done, g + 1)
                    if g >= 2:
                        pool.wait_ge(av_mm, g - 1)
                    pool.tensor_tensor(wl[:, g % 2, :], wt[:, g % 2, :], wh[:, g % 2, :], ALU.subtract).then_inc(wl_done, 1)


def l0_gla(nc, m, d):
    with ExitStack() as ctx:
        sb, ps, sem = names(nc, ctx)
        qT = sb("gl_qT", [P, KC, TOK])
        kv = sb("gl_kv", [P, TT, 2 * D])
        sq = sb("gl_sq", [P, TT, D])
        ssq = sb("gl_ssq", [P, TT, H])
        nrm = sb("gl_nrm", [P, TT, H])
        inv = sb("gl_inv", [P, TT, H])
        kn = sb("gl_kn", [P, TT, D])
        kT = sb("gl_kT", [P, KC, TOK])
        vhl = sb("gl_vhl", [P, TT, H, 32], BF16)
        g1 = sb("gl_g1", [16, TOK])
        gate = sb("gl_gate", [P, TT, D])
        o = sb("gl_o", [P, TT, D])
        F = sb("gl_F", [96, TOK], BF16)
        nF = sb("gl_nF", [96, TOK], BF16)
        with ExitStack() as c2:
            sb2, ps2, sem2 = names(nc, c2)
            fa = sb2("gl_fa", [96, TOK])
            fe = sb2("gl_fe", [96, TOK])
            fl = sb2("gl_fl", [96, TOK])
            fs = sb2("gl_fs", [96, TOK])
            fc = sb2("gl_fc", [96, TOK])
            fr = sb2("gl_fr", [96, TOK])
            f1 = sb2("gl_f1", [96, TOK], BF16)
            pq = ps2("gl_pq", [P, KC, BANK])
            pkv = ps2("gl_pkv", [P, TT, BANK])
            pf = ps2("gl_pf", [P, BANK])
            pg = ps2("gl_pg", [P, BANK])
            (q_mm, kv_mm, f_mm, g1_mm, q_done, kv_done, fabs, fexp, fln, g1_done, gt_mm, gate_done, sq_done, ssq_done,
             nrm_done, inv_done, kn_done, kt_mm, kt_done, fchain, v_hi, v_lo) = (sem2("gl_" + n) for n in (
                 "q_mm", "kv_mm", "f_mm", "g1_mm", "q_done", "kv_done", "fabs", "fexp", "fln", "g1_done", "gt_mm",
                 "gate_done", "sq_done", "ssq_done", "nrm_done", "inv_done", "kn_done", "kt_mm", "kt_done", "fchain",
                 "v_hi", "v_lo"))
            with nc.Block() as block:
                @block.tensor
                def _(pe):
                    pe.wait_ge(m.late_loaded, m.late_n)
                    for t in range(TT):
                        for c in range(KC):
                            mm = pe.matmul(pkv[:, t, :], m.xnT[:, c, P * t:P * t + P], m.late["gl_wkv"][:, c, :],
                                           start=(c == 0), stop=(c == KC - 1))
                        mm.then_inc(kv_mm, 1)
                    for c in range(KC):
                        mm = pe.matmul(pf[0:96, :], m.late["gl_wf"][:, c, :], m.xnT[:, c, :], start=(c == 0), stop=(c == KC - 1))
                    mm.then_inc(f_mm, 1)
                    for c in range(KC):
                        mm = pe.matmul(pg[0:16, :], m.late["gl_g1"][:, c, :], m.xnT[:, c, :], start=(c == 0), stop=(c == KC - 1))
                    mm.then_inc(g1_mm, 1)
                    for n in range(KC):
                        for c in range(KC):
                            mm = pe.matmul(pq[:, n, :], m.late["gl_wq"][:, c, P * n:P * n + P], m.xnT[:, c, :],
                                           start=(c == 0), stop=(c == KC - 1))
                        mm.then_inc(q_mm, 1)
                    pe.wait_ge(g1_done, 1)
                    pe.wait_ge(q_done, 2)
                    for t in range(TT):
                        pe.matmul(pq[:, t // 2, D * (t % 2):D * (t % 2) + D], g1[:, P * t:P * t + P], m.late["gl_g2"][:, :],
                                  start=True, stop=True).then_inc(gt_mm, 1)
                    pe.wait_ge(kn_done, 1)
                    for c in range(KC):
                        for t in range(TT):
                            mm = pe.transpose(pkv[:, c, P * t:P * t + P], kn[:, t, P * c:P * c + P], m.ident[:, :])
                        mm.then_inc(kt_mm, 1)

                @block.scalar
                def _(act):
                    for t in range(TT):
                        act.wait_ge(kv_mm, t + 1)
                        act.activation(kv[:, t, :], pkv[:, t, :], ACT.Silu).then_inc(kv_done, 1)
                    for n in range(KC):
                        act.wait_ge(q_mm, n + 1)
                        act.activation(qT[:, n, :], pq[:, n, :], ACT.Silu).then_inc(q_done, 1)
                    act.wait_ge(g1_mm, 1)
                    act.activation(g1[:, :], pg[0:16, :], ACT.Copy).then_inc(g1_done, 1)
                    act.wait_ge(f_mm, 1)
                    act.activation(fa[:, :], pf[0:96, :], ACT.Abs).then_inc(fabs, 1)
                    act.wait_ge(ssq_done, 1)
                    act.activation(nrm[:, :, :], ssq[:, :, :], ACT.Sqrt).then_inc(nrm_done, 1)
                    act.wait_ge(gt_mm, TT)
                    for n in range(2):
                        act.activation(gate[:, 2 * n:2 * n + 2, :], pq[:, n, :].rearrange("p (t f) -> p t f", t=2),
                                       ACT.Sigmoid).then_inc(gate_done, 1)
                    act.wait_ge(fabs, 1)
                    act.activation(fe[:, :], fa[:, :], ACT.Exp, scale=-1.0).then_inc(fexp, 1)
                    act.wait_ge(fexp, 1)
                    act.activation(fl[:, :], fe[:, :], ACT.Ln, bias=m.one[0:96, :]).then_inc(fln, 1)
                    act.wait_ge(kt_mm, 1)
                    act.activation(kT[:, 0, :], pkv[:, 0, :], ACT.Copy).then_inc(kt_done, 1)

                @block.vector
                def _(dve):
                    k4 = kv[:, :, 0:D]
                    dve.wait_ge(kv_done, TT)
                    dve.tensor_tensor(sq[:, :, :], k4, k4, ALU.mult).then_inc(sq_done, 1)
                    dve.wait_ge(sq_done, 1)
                    dve.tensor_reduce(ssq[:, :, :], sq[:, :, :].rearrange("p t (h e) -> p t h e", h=H), AX_X,
                                      ALU.add).then_inc(ssq_done, 1)
                    dve.wait_ge(nrm_done, 1)
                    dve.tensor_scalar(nrm[:, :, :], nrm[:, :, :], 1e-12, None, ALU.max).then_inc(inv_done, 1)
                    dve.wait_ge(inv_done, 1)
                    dve.reciprocal(inv[:, :, :], nrm[:, :, :]).then_inc(inv_done, 1)
                    dve.wait_ge(inv_done, 2)
                    dve.tensor_tensor(kn[:, :, :].rearrange("p t (h e) -> p t h e", h=H),
                                      k4.rearrange("p t (h e) -> p t h e", h=H),
                                      inv[:, :, :].unsqueeze(3).broadcast_to([P, TT, H, 16]), ALU.mult).then_inc(kn_done, 1)
                    dve.wait_ge(fln, 1)
                    link = chained(dve, fchain)
                    link(dve.scalar_tensor_tensor(fs[:, :], pf[0:96, :], 0.0, fl[:, :], ALU.min, ALU.subtract))
                    link(dve.tensor_tensor_scan(fc[:, :], m.late["scanmask"][0:96, :], fs[:, :], 0.0, ALU.mult, ALU.add))
                    link(dve.tensor_copy(f1[:, :], fc[:, :]))
                    link(dve.tensor_tensor(fr[:, :], fc[:, :], f1[:, :], ALU.subtract))
                    link(dve.tensor_copy(F[:, :], fr[:, :]))
                    link(dve.tensor_tensor(fa[:, :], fr[:, :], F[:, :], ALU.subtract))
                    link(dve.tensor_copy(F[0:32, :], f1[0:32, :]))
                    link(dve.tensor_copy(F[64:96, :], fa[64:96, :]))
                    link(dve.tensor_scalar(nF[:, :], F[:, :], -1.0, None, ALU.mult))
                    dve.wait_ge(kt_mm, 2)
                    dve.tensor_copy(kT[:, 1, :], pkv[:, 1, :]).then_inc(kt_done, 1)

                @block.gpsimd
                def _(pool):
                    v4 = kv[:, :, D:2 * D].rearrange("p t (h e) -> p t h e", h=H)
                    pool.wait_ge(kv_done, TT)
                    for t in range(TT):
                        pool.tensor_copy(vhl[:, t, :, 0:16], v4[:, t]).then_inc(v_hi, 1)
                    for t in range(TT):
                        pool.wait_ge(v_hi, t + 1)
                        pool.tensor_tensor(vhl[:, t, :, 16:32], v4[:, t], vhl[:, t, :, 0:16], ALU.subtract).then_inc(v_lo, 1)
        heads16(nc, m, "gh", qT, kT, vhl, o, (F, nF))
        with ExitStack() as c2:
            _, _, sem2 = names(nc, c2)
            gated = sem2("gl_gated")
            with nc.Block() as block:
                @block.vector
                def _(dve):
                    dve.tensor_tensor(o[:, :, :], o[:, :, :], gate[:, :, :], ALU.mult).then_inc(gated, 1)
        layer_norm(nc, m, "lng", o, kn, kT, (m.late["gl_lnw"][:, :], None))
        project(nc, m, "gp", kT, m.late["gl_wo"], None)


def l0_moe(nc, m, d):
    with ExitStack() as ctx:
        sb, ps, sem = names(nc, ctx)
        mask = sb("mo_mask", [P, TT, E])
        xs = sb("mo_xs", [P, TT, D])
        xsT = sb("mo_xsT", [P, KC, TOK])
        with ExitStack() as c2:
            sb2, ps2, sem2 = names(nc, c2)
            lg = sb2("mo_lg", [P, TT, E])
            top = sb2("mo_top", [P, TT])
            rw = sb2("mo_rw", [P, TT])
            eq = sb2("mo_eq", [P, TT, E])
            cand = sb2("mo_cand", [P, TT, E])
            best = sb2("mo_best", [P, TT])
            pL = ps2("mo_pL", [P, TT * E])
            pT = ps2("mo_pT", [P, KC, BANK])
            l_mm, chain, rw_done, xs_done, turned, copied = (
                sem2("mo_" + n) for n in ("l_mm", "chain", "rw_done", "xs_done", "turned", "copied"))
            with nc.Block() as block:
                @block.tensor
                def _(pe):
                    pe.wait_ge(m.late_loaded, m.late_n)
                    for t in range(TT):
                        for c in range(KC):
                            mm = pe.matmul(pL[:, E * t:E * t + E], m.xnT[:, c, P * t:P * t + P], m.late["mo_gate"][:, c, :],
                                           start=(c == 0), stop=(c == KC - 1))
                    mm.then_inc(l_mm, 1)
                    pe.wait_ge(xs_done, TT)
                    for c in range(KC):
                        for t in range(TT):
                            mm = pe.transpose(pT[:, c, P * t:P * t + P], xs[:, t, P * c:P * c + P], m.ident[:, :])
                        mm.then_inc(turned, 1)

                @block.scalar
                def _(act):
                    act.wait_ge(chain, 2)
                    act.activation(rw[:, :], top[:, :], ACT.Sigmoid).then_inc(rw_done, 1)
                    act.wait_ge(turned, 1)
                    act.activation(xsT[:, 0, :], pT[:, 0, :], ACT.Copy).then_inc(copied, 1)

                @block.vector
                def _(dve):
                    dve.wait_ge(l_mm, 1)
                    def wide(a):
                        return a[:, :].unsqueeze(2).broadcast_to([P, TT, E])
                    desc = m.small[:, SMALL["desc"]:SMALL["desc"] + E].unsqueeze(1).broadcast_to([P, TT, E])
                    link = chained(dve, chain)
                    link(dve.tensor_copy(lg[:, :, :], pL[:, :].rearrange("p (t e) -> p t e", e=E)))
                    link(dve.tensor_reduce(top[:, :], lg[:, :, :], AX_X, ALU.max))
                    link(dve.tensor_tensor(eq[:, :, :], lg[:, :, :], wide(top), ALU.is_equal))
                    link(dve.tensor_tensor(cand[:, :, :], eq[:, :, :], desc, ALU.mult))
                    link(dve.tensor_reduce(best[:, :], cand[:, :, :], AX_X, ALU.max))
                    link(dve.tensor_tensor(mask[:, :, :], cand[:, :, :], wide(best), ALU.is_equal))
                    dve.wait_ge(rw_done, 1)
                    for t in range(TT):
                        dve.tensor_scalar(xs[:, t, :], m.xn[:, t, :], rw[:, t:t + 1], None, ALU.mult).then_inc(xs_done, 1)
                    dve.wait_ge(turned, 2)
                    dve.tensor_copy(xsT[:, 1, :], pT[:, 1, :]).then_inc(copied, 1)
        sg = sb("mo_sg", [P, 2, TOK])
        hT = sb("mo_hT", [P, 2, TOK])
        pG = ps("mo_pG", [P, 2, BANK])
        pU = ps("mo_pU", [P, 2, BANK])
        pD = ps("mo_pD", [P, TT, BANK])
        g_mm, u_mm, sg_done, h_done, d_mm, x_done = (
            sem("mo_" + n) for n in ("g_mm", "u_mm", "sg_done", "h_done", "d_mm", "x_done"))
        with nc.Block() as block:
            @block.tensor
            def _(pe):
                for e in range(E + 1):
                    if e < E:
                        if e >= 2:
                            pe.wait_ge(h_done, e - 1)
                        for w, o, s in ((m.late["mo_wg"], pG, g_mm), (m.late["mo_wu"], pU, u_mm)):
                            for c in range(KC):
                                mm = pe.matmul(o[:, e % 2, :], w[:, e, c, :], xsT[:, c, :], start=(c == 0),
                                               stop=(c == KC - 1))
                            mm.then_inc(s, 1)
                    if e >= 1:
                        pe.wait_ge(h_done, e)
                        for t in range(TT):
                            if e >= 2:
                                pe.wait_ge(x_done, TT * (e - 2) + t + 1)
                            pe.matmul(pD[:, t, 0:D], hT[:, (e - 1) % 2, P * t:P * t + P], m.late["mo_wd"][:, e - 1, :],
                                      start=True, stop=True).then_inc(d_mm, 1)

            @block.scalar
            def _(act):
                for e in range(E):
                    act.wait_ge(g_mm, e + 1)
                    if e >= 2:
                        act.wait_ge(h_done, e - 1)
                    act.activation(sg[:, e % 2, :], pG[:, e % 2, :], ACT.Silu).then_inc(sg_done, 1)

            @block.vector
            def _(dve):
                for e in range(E + 1):
                    if e < E:
                        dve.wait_ge(u_mm, e + 1)
                        dve.wait_ge(sg_done, e + 1)
                        if e >= 2:
                            dve.wait_ge(d_mm, TT * (e - 1))
                        dve.tensor_tensor(hT[:, e % 2, :], pU[:, e % 2, :], sg[:, e % 2, :], ALU.mult).then_inc(h_done, 1)
                    if e >= 1:
                        for t in range(TT):
                            n = TT * (e - 1) + t
                            dve.wait_ge(d_mm, n + 1)
                            if e >= 2:
                                dve.wait_ge(x_done, n - TT + 1)
                            dve.scalar_tensor_tensor(m.x[:, t, :], pD[:, t, 0:D], mask[:, t, e - 1:e], m.x[:, t, :],
                                                     ALU.mult, ALU.add).then_inc(x_done, 1)


def l1x_tiles(nc, m, d, qbh, qbl, wh, wl, wB, oT):
    SCALE = 16 ** -0.5
    with ExitStack() as ctx:
        sb, ps, sem = names(nc, ctx)
        stA = sb("x1_stA", [P, M])
        stB = sb("x1_stB", [P, M])
        hl = [Parts(sb, f"x1_ctx{n}", False) for n in range(2)]
        kh = sb("x1_kh", [P, KC, M + 1], BF16)
        kl = sb("x1_kl", [P, KC, M + 1], BF16)
        vhl = sb("x1_vhl", [P, MC, PAIRS, 64], BF16)
        prob = sb("x1_prob", [P, M])
        pth = sb("x1_pth", [P, MC, P], BF16)
        ptl = sb("x1_ptl", [P, MC, P], BF16)
        mx = sb("x1_mx", [P, 2])
        nmax = sb("x1_nmax", [P, 2])
        rsum = sb("x1_rsum", [P, 2])
        rinv = sb("x1_rinv", [P, 2])
        u = sb("x1_u", [P, 2, PAIRS, 32])
        pS = ps("x1_pS", [P, 4 * BANK])
        pT = ps("x1_pT", [P, 2, BANK])
        pU = ps("x1_pU", [P, 64])
        pF = ps("x1_pF", [P, KC, NQ])
        (ctx_in, begun, split, k_mm, k_hi, k_lo, v_mm, v_hi, v_lo, s_done, exp_done, t_done, hi_done, lo_done, av_done,
         mx_done, nmax_done, rinv_done, u_done, f_mm, f_done) = (sem("x1_" + n) for n in (
             "ctx_in", "begun", "split", "k_mm", "k_hi", "k_lo", "v_mm", "v_hi", "v_lo", "s_done", "exp_done", "t_done",
             "hi_done", "lo_done", "av_done", "mx_done", "nmax_done", "rinv_done", "u_done", "f_mm", "f_done"))
        NS = 4
        NK = KC * len(SEG)
        VG = [range(2 * n, min(2 * n + 2, MC)) for n in range(-(-MC // 2))]
        NV = len(VG)
        rowmask = m.small[:, SMALL["rowmask"]:SMALL["rowmask"] + 64].rearrange("p (a c) -> p a c", a=2)
        fold = m.small[:, SMALL["fold"]:SMALL["fold"] + NQ]

        with nc.Block() as block:
            @block.sync
            def _(sp):
                with sp.Fori(0, B) as b:
                    sp.wait_ge(split, 1 + b * NS)
                    sp.dma_start(stA[:, :], d["ctxT"][bass.ds(b, 1), 0:P].rearrange("o p c -> (o p) c")).then_inc(ctx_in, 16)
                    for s in (0, 64):
                        sp.dma_start(stB[s:s + 64, :], d["ctxT"][bass.ds(b, 1), P:DC].rearrange("o p c -> (o p) c")).then_inc(ctx_in, 16)

            def split_batch(pool, b, o):
                pool.wait_ge(ctx_in, (b + 1) * 48)
                pool.sem_inc(begun, 1)
                parts = ((o.ah[:, 0:M], o.al[:, 0:M], stA[:, :]), (o.bh[:, 0:M], o.bl[:, 0:M], stB[:, :]))
                for hi, _, src in parts:
                    pool.tensor_copy(hi, src).then_inc(split, 1)
                for n, (hi, lo, src) in enumerate(parts):
                    pool.wait_ge(split, 1 + b * NS + n + 1)
                    pool.tensor_tensor(lo, src, hi, ALU.subtract).then_inc(split, 1)

            @block.gpsimd
            def _(pool):
                for s in (split,):
                    pool.sem_inc(s, 1)
                for par in range(2):
                    split_batch(pool, par, hl[par])
                with pool.Fori(1, B // 2) as i:
                    b = i * 2
                    for par in range(2):
                        pool.wait_ge(v_mm, 1 + (b + par - 1) * NV)
                        split_batch(pool, b + par, hl[par])

            def batches(eng, body):
                with eng.Fori(0, B // 2) as i:
                    for par in range(2):
                        body(i * 2 + par, hl[par])

            @block.tensor
            def _(pe):
                for s in (s_done, t_done, av_done, k_mm, v_mm, f_mm):
                    pe.sem_inc(s, 1)
                def body(b, c):
                    k0 = b * PAIRS

                    def keys():
                        pe.wait_ge(split, 1 + (b + 1) * NS)
                        pe.wait_ge(exp_done, 1 + k0)
                        for n in range(KC):
                            w = slice(P * n, P * n + P)
                            for j, (s, z) in enumerate(SEG):
                                if n:
                                    pe.wait_ge(k_lo, 1 + b * NK + j + 1)
                                for a, (st, mv) in enumerate(((wh[:, 0, w], c.ah), (wh[:, 0, w], c.al), (wl[:, 0, w], c.ah),
                                                              (wB[:, w], c.bh), (wB[:, w], c.bl))):
                                    mm = pe.matmul(pS[:, s:s + z], st, mv[:, s:s + z], start=(a == 0), stop=(a == 4))
                                mm.then_inc(k_mm, 1)

                    def vals():
                        for n, cs in enumerate(VG):
                            if n >= 2:
                                pe.wait_ge(v_lo, 1 + b * NV + n - 1)
                            else:
                                pe.wait_ge(lo_done, 1 + k0 * NG)
                                pe.wait_ge(v_lo, 1 + b * NV)
                            for ch in cs:
                                r = min(P, M - P * ch)
                                s = slice(P * ch, P * ch + r)
                                w = slice(D, 2 * D)
                                o = pT[0:r, n % 2, D * (ch % 2):D * (ch % 2) + D]
                                for a, (st, mv) in enumerate(((c.ah, wh[:, 0, w]), (c.ah, wl[:, 0, w]), (c.al, wh[:, 0, w]),
                                                              (c.bh, wB[:, w]), (c.bl, wB[:, w]))):
                                    mm = pe.matmul(o, st[:, s], mv, start=(a == 0), stop=(a == 4))
                            mm.then_inc(v_mm, 1)

                    def scores(t, j):
                        s, w = SEG[j]
                        q = [a[:, bass.ds(b, 1), t, :].rearrange("p o r -> p (o r)") for a in (qbh, qbl)]
                        if j == 0:
                            pe.wait_ge(exp_done, 1 + k0 + t)
                            if t == 0:
                                pe.wait_ge(k_lo, 1 + (b + 1) * NK)
                        for a, (st, mv) in enumerate(((q[0], kh), (q[0], kl), (q[1], kh))):
                            mm = pe.matmul(pS[:, s:s + w], st, mv[:, t // 4, s:s + w], start=(a == 0), stop=(a == 2))
                        if j in (1, 3):
                            mm.then_inc(s_done, 1)

                    def turn_probs(t, g):
                        n = 4 * t + g
                        if g == 0:
                            pe.wait_ge(exp_done, 1 + k0 + t + 1)
                            if t == 0:
                                pe.wait_ge(v_lo, 1 + (b + 1) * NV)
                        pe.wait_ge(lo_done, 1 + k0 * NG + max(n - 1, 0))
                        for ch in TGRP[g][1]:
                            w = min(P, M - P * ch)
                            mm = pe.transpose(pT[0:w, n % 2, P * (ch % 4):P * (ch % 4) + P], prob[:, P * ch:P * ch + w],
                                              m.ident[:, :])
                        mm.then_inc(t_done, 1)

                    def values(t):
                        pe.wait_ge(u_done, 1 + k0 + t)
                        for n in range(MC):
                            w = min(P, M - P * n)
                            if n % 4 == 0:
                                pe.wait_ge(lo_done, 1 + (k0 + t) * NG + n // 4 + 1)
                            pe.matmul(pU[:, 0:64], pth[0:w, n, :], vhl[0:w, n, t, :], start=(n == 0), stop=False)
                            mm = pe.matmul(pU[:, 0:32], ptl[0:w, n, :], vhl[0:w, n, t, 0:32], start=False,
                                           stop=(n == MC - 1))
                        mm.then_inc(av_done, 1)

                    def fold_rows():
                        pe.wait_ge(u_done, 1 + k0 + PAIRS)
                        pe.wait_ge(f_done, 1 + b * KC)
                        for n in range(KC):
                            for a in range(2):
                                mm = pe.matmul(pF[:, n, :], u[:, a, 4 * n:4 * n + 4, :].rearrange("p a c -> p (a c)"), fold,
                                               start=(a == 0), stop=(a == 1))
                        mm.then_inc(f_mm, 1)

                    keys()
                    vals()
                    for t in range(PAIRS + 1):
                        for j in range(4):
                            if t < PAIRS:
                                scores(t, j)
                            if t >= 1:
                                turn_probs(t - 1, j)
                        if t >= 1:
                            values(t - 1)
                    fold_rows()

                batches(pe, body)

            @block.scalar
            def _(act):
                for s in (exp_done, hi_done, k_hi, v_hi, f_done):
                    act.sem_inc(s, 1)
                def body(b, c):
                    k0 = b * PAIRS
                    act.wait_ge(s_done, 1 + k0 * 2)
                    for n in range(KC):
                        for j, (s, w) in enumerate(SEG):
                            act.wait_ge(k_mm, 1 + b * NK + 4 * n + j + 1)
                            act.activation(kh[:, n, s:s + w], pS[:, s:s + w], ACT.Identity,
                                           bias=m.late["x1_bk"][:, n:n + 1]).then_inc(k_hi, 1)
                    act.wait_ge(av_done, 1 + k0)
                    for n, cs in enumerate(VG):
                        r = min(P, M - P * cs[0])
                        act.wait_ge(v_mm, 1 + b * NV + n + 1)
                        act.activation(vhl[0:r, cs[0]:cs[-1] + 1, :, 0:32], pT[0:r, n % 2, 0:D * len(cs)].rearrange(
                            "p (c a e) -> p c a e", a=PAIRS, e=32), ACT.Copy).then_inc(v_hi, 1)
                    for t in range(PAIRS + 1):
                        if t >= 1:
                            act.wait_ge(av_done, 1 + k0 + t - 1)
                            for g, cs in TGRP:
                                n = 4 * (t - 1) + g
                                w = min(P, M - P * cs[0])
                                act.wait_ge(t_done, 1 + (k0 + t - 1) * NG + g + 1)
                                act.activation(pth[0:w, cs[0]:cs[-1] + 1, :], pT[0:w, n % 2, 0:P * len(cs)].rearrange(
                                    "p (c r) -> p c r", r=P), ACT.Copy).then_inc(hi_done, 1)
                        if t < PAIRS:
                            act.wait_ge(nmax_done, 1 + k0 + t + 1)
                            act.wait_ge(t_done, 1 + (k0 + t) * NG)
                            act.activation(prob[:, :], pS[:, 0:M], ACT.Exp, bias=nmax[:, t % 2:t % 2 + 1], scale=SCALE,
                                           accum_out=rsum[:, t % 2:t % 2 + 1]).then_inc(exp_done, 1)
                    act.wait_ge(f_mm, 1 + b + 1)
                    for n in range(KC):
                        act.activation(oT[:, n, bass.ds(b * NQ, NQ)], pF[:, n, :], ACT.Identity,
                                       bias=m.late["x1_bv"][:, n:n + 1]).then_inc(f_done, 1)

                batches(act, body)

            @block.vector
            def _(dve):
                for s in (lo_done, mx_done, nmax_done, rinv_done, u_done, k_lo, v_lo):
                    dve.sem_inc(s, 1)
                def body(b, c):
                    k0 = b * PAIRS
                    for n in range(KC):
                        for j, (s, w) in enumerate(SEG):
                            dve.wait_ge(k_hi, 1 + b * NK + 4 * n + j + 1)
                            dve.scalar_tensor_tensor(kl[:, n, s:s + w], pS[:, s:s + w], m.late["x1_bk"][:, n:n + 1], kh[:, n, s:s + w],
                                                     ALU.add, ALU.subtract).then_inc(k_lo, 1)
                    for n, cs in enumerate(VG):
                        r = min(P, M - P * cs[0])
                        dve.wait_ge(v_hi, 1 + b * NV + n + 1)
                        dve.tensor_tensor(vhl[0:r, cs[0]:cs[-1] + 1, :, 32:64], pT[0:r, n % 2, 0:D * len(cs)].rearrange(
                            "p (c a e) -> p c a e", a=PAIRS, e=32), vhl[0:r, cs[0]:cs[-1] + 1, :, 0:32],
                            ALU.subtract).then_inc(v_lo, 1)

                    def low_probs(t, g):
                        cs = TGRP[g][1]
                        n = 4 * t + g
                        w = min(P, M - P * cs[0])
                        dve.wait_ge(hi_done, 1 + (k0 + t) * NG + g + 1)
                        dve.tensor_tensor(ptl[0:w, cs[0]:cs[-1] + 1, :], pT[0:w, n % 2, 0:P * len(cs)].rearrange(
                            "p (c r) -> p c r", r=P), pth[0:w, cs[0]:cs[-1] + 1, :], ALU.subtract).then_inc(lo_done, 1)

                    def maxima(t, half):
                        a, z = (0, 2 * BANK) if half == 0 else (2 * BANK, M)
                        dve.wait_ge(s_done, 1 + (k0 + t) * 2 + half + 1)
                        dve.tensor_reduce(mx[:, half:half + 1], pS[:, a:z], AX_X, ALU.max, negate=True).then_inc(mx_done, 1)

                    for t in range(PAIRS + 1):
                        for half in range(2):
                            if t >= 1:
                                low_probs(t - 1, 2 * half)
                                low_probs(t - 1, 2 * half + 1)
                            if t < PAIRS:
                                maxima(t, half)
                        if t < PAIRS:
                            dve.wait_ge(mx_done, 1 + (k0 + t + 1) * 2)
                            dve.tensor_scalar(nmax[:, t % 2:t % 2 + 1], mx[:, 0:1], mx[:, 1:2], SCALE, ALU.min,
                                              ALU.mult).then_inc(nmax_done, 1)
                        if t >= 1:
                            s = (t - 1) % 2
                            dve.wait_ge(exp_done, 1 + k0 + t)
                            dve.reciprocal(rinv[:, s:s + 1], rsum[:, s:s + 1]).then_inc(rinv_done, 1)
                            dve.wait_ge(rinv_done, 1 + k0 + t)
                            dve.wait_ge(av_done, 1 + k0 + t)
                            dve.wait_ge(f_mm, 1 + b)
                            dve.scalar_tensor_tensor(u[:, :, t - 1, :], pU[:, :].rearrange("p (a c) -> p a c", a=2),
                                                     rinv[:, s:s + 1], rowmask, ALU.mult, ALU.mult).then_inc(u_done, 1)

                batches(dve, body)


def l1x(nc, m, d):
    with ExitStack() as ctx:
        sb, ps, sem = names(nc, ctx)
        qbh = sb("x1_qbh", [P, B, PAIRS, P], BF16)
        qbl = sb("x1_qbl", [P, B, PAIRS, P], BF16)
        wh = sb("x1_wh", [P, 2, 2 * D], BF16)
        wl = sb("x1_wl", [P, 2, 2 * D], BF16)
        wB = sb("x1_wB", [P, 2 * D], BF16)
        oT = sb("x1_oT", [P, KC, TOK])
        with ExitStack() as c2:
            sb2, ps2, sem2 = names(nc, c2)
            qT = sb2("x1_qT", [P, KC, TOK])
            qm = sb2("x1_qm", [P, 2, 8, TOK])
            pq = ps2("x1_pq", [P, KC, BANK])
            q_mm, q_done, qm_done, qbh_done, qbl_done, whi, wlo = (
                sem2("x1_" + n) for n in ("q_mm", "q_done", "qm_done", "qbh_done", "qbl_done", "whi", "wlo"))
            with nc.Block() as block:
                @block.tensor
                def _(pe):
                    pe.wait_ge(m.late_loaded, m.late_n)
                    for n in range(KC):
                        for c in range(KC):
                            mm = pe.matmul(pq[:, n, :], m.late["x1_wq"][:, c, P * n:P * n + P], m.xnT[:, c, :], start=(c == 0),
                                           stop=(c == KC - 1))
                        mm.then_inc(q_mm, 1)

                def q_out(q, n, h):
                    return q[:, :, 4 * n + h // 2, NQ * (h % 2):NQ * (h % 2) + NQ]

                def by_batch(a):
                    return a.rearrange("p (b i) -> p b i", b=B)

                @block.scalar
                def _(act):
                    for n in range(KC):
                        act.wait_ge(q_mm, n + 1)
                        act.activation(qT[:, n, :], pq[:, n, :], ACT.Identity, bias=m.late["x1_bq"][:, n:n + 1]).then_inc(q_done, 1)
                    act.activation(wh[:, :, :], m.late["x1_wkv"][:, :, :], ACT.Copy).then_inc(whi, 1)
                    for k in range(16):
                        n, h = k // 8, k % 8
                        act.wait_ge(qm_done, k + 1)
                        act.activation(q_out(qbh, n, h), by_batch(qm[:, n, h, :]), ACT.Copy).then_inc(qbh_done, 1)

                @block.vector
                def _(dve):
                    hmask = m.small[:, SMALL["hmask"]:SMALL["hmask"] + 8]
                    for k in range(16):
                        n, h = k // 8, k % 8
                        dve.wait_ge(q_done, n + 1)
                        dve.tensor_scalar(qm[:, n, h, :], qT[:, n, :], hmask[:, h:h + 1], None, ALU.mult).then_inc(qm_done, 1)
                    for k in range(16):
                        n, h = k // 8, k % 8
                        dve.wait_ge(qbh_done, k + 1)
                        dve.tensor_tensor(q_out(qbl, n, h), by_batch(qm[:, n, h, :]), q_out(qbh, n, h),
                                          ALU.subtract).then_inc(qbl_done, 1)

                @block.gpsimd
                def _(pool):
                    pool.wait_ge(m.late_loaded, m.late_n)
                    pool.wait_ge(whi, 1)
                    pool.tensor_tensor(wl[:, :, :], m.late["x1_wkv"][:, :, :], wh[:, :, :], ALU.subtract).then_inc(wlo, 1)
                    pool.tensor_copy(wB[0:64, :], wh[0:64, 1, :]).then_inc(wlo, 1)
                    pool.wait_ge(wlo, 1)
                    pool.tensor_copy(wB[64:128, :], wl[64:128, 1, :]).then_inc(wlo, 1)

        l1x_tiles(nc, m, d, qbh, qbl, wh, wl, wB, oT)
        project(nc, m, "xp", oT, m.late["x1_wo"], m.late["x1_bo"][:, :])


def l1_attn(nc, m, d):
    with ExitStack() as ctx:
        sb, ps, sem = names(nc, ctx)
        x2 = sb("a1_x2", [P, TT, D])
        x2T = sb("a1_x2T", [P, KC, TOK])
        layer_norm(nc, m, "ln4b", m.xn, x2, x2T, (m.late["a1_gamma"][:, :], m.late["a1_beta"][:, :]))
        qk = sb("a1_qk", [P, TT, 2 * D])
        kT = sb("a1_kT", [P, KC, TOK])
        qT = sb("a1_qT", [P, KC, TOK])
        vhl = sb("a1_vhl", [P, TT, H, 32], BF16)
        gates = sb("a1_gates", [P, TT, 2 * H])
        o = sb("a1_o", [P, TT, D])
        with ExitStack() as c2:
            sb2, ps2, sem2 = names(nc, c2)
            sq = sb2("a1_sq", [P, TT, 2 * D])
            ss = sb2("a1_ss", [P, TT, 2 * H])
            nrm = sb2("a1_nrm", [P, TT, 2 * H])
            vg = sb2("a1_vg", [P, TT, D])
            pqk = ps2("a1_pqk", [P, TT, BANK])
            pv = ps2("a1_pv", [P, TT, BANK])
            qk_mm, v_mm, qk_done, chain, nrm_done, sig_done, turned, copied, v_hi, v_lo, freed = (
                sem2("a1_" + n) for n in ("qk_mm", "v_mm", "qk_done", "chain", "nrm_done", "sig_done", "turned",
                                          "copied", "v_hi", "v_lo", "freed"))

            def by_head(a, n):
                return a.rearrange("p t (h e) -> p t h e", h=n)

            with nc.Block() as block:
                @block.tensor
                def _(pe):
                    for t in range(TT):
                        s = slice(P * t, P * t + P)
                        for c in range(KC):
                            mm = pe.matmul(pqk[:, t, :], x2T[:, c, s], m.late["a1_wqk"][:, c, :], start=(c == 0), stop=(c == KC - 1))
                        mm.then_inc(qk_mm, 1)
                    for t in range(TT):
                        s = slice(P * t, P * t + P)
                        for c in range(KC):
                            mm = pe.matmul(pv[:, t, 0:D], m.xnT[:, c, s], m.late["a1_wv"][:, c, :], start=(c == 0), stop=(c == KC - 1))
                        mm.then_inc(v_mm, 1)
                    pe.wait_ge(chain, 5)
                    for n in range(4):
                        for t in range(TT):
                            mm = pe.transpose(pqk[:, n, P * t:P * t + P], qk[:, t, P * n:P * n + P], m.ident[:, :])
                        mm.then_inc(turned, 1)

                @block.scalar
                def _(act):
                    for t in range(TT):
                        act.wait_ge(qk_mm, t + 1)
                        act.activation(qk[:, t, :], pqk[:, t, :], ACT.Copy).then_inc(qk_done, 1)
                    act.wait_ge(chain, 2)
                    act.activation(nrm[:, :, :], ss[:, :, :], ACT.Sqrt).then_inc(nrm_done, 1)
                    act.wait_ge(chain, 7)
                    act.activation(gates[:, :, :], ss[:, :, :], ACT.Sigmoid).then_inc(sig_done, 1)
                    for n in range(4):
                        act.wait_ge(turned, n + 1)
                        o_ = (qT if n < 2 else kT)[:, n % 2, :]
                        act.activation(o_, pqk[:, n, :], ACT.Copy).then_inc(copied, 1)

                @block.vector
                def _(dve):
                    dve.wait_ge(qk_done, TT)
                    inv = nrm
                    q4 = by_head(qk[:, :, :], 2 * H)
                    link = chained(dve, chain)
                    link(dve.tensor_tensor(sq[:, :, :], qk[:, :, :], qk[:, :, :], ALU.mult))
                    link(dve.tensor_reduce(ss[:, :, :], by_head(sq[:, :, :], 2 * H), AX_X, ALU.add))
                    dve.wait_ge(nrm_done, 1)
                    link(dve.tensor_scalar(nrm[:, :, :], nrm[:, :, :], 1e-12, None, ALU.max))
                    link(dve.reciprocal(inv[:, :, :], nrm[:, :, :]))
                    link(dve.tensor_tensor(q4, q4, inv[:, :, :].unsqueeze(3).broadcast_to([P, TT, 2 * H, 16]), ALU.mult))
                    link(dve.tensor_tensor(sq[:, :, :], qk[:, :, :],
                         m.late["a1_g"][:, :].unsqueeze(1).broadcast_to([P, TT, 2 * D]), ALU.mult))
                    link(dve.tensor_reduce(ss[:, :, :], by_head(sq[:, :, :], 2 * H), AX_X, ALU.add))
                    dve.wait_ge(sig_done, 1)
                    dve.wait_ge(v_mm, TT)
                    link(dve.tensor_scalar(gates[:, :, :], gates[:, :, :], 0.75, 0.25, ALU.mult, ALU.add))
                    link(dve.tensor_tensor(
                         by_head(vg[:, :, :], H), pv[:, :, 0:D].rearrange("p t (h e) -> p t h e", h=H),
                         gates[:, :, H:2 * H].unsqueeze(3).broadcast_to([P, TT, H, 16]), ALU.mult))

                @block.gpsimd
                def _(pool):
                    pool.wait_ge(chain, 9)
                    v4 = by_head(vg[:, :, :], H)
                    for t in range(TT):
                        pool.tensor_copy(vhl[:, t, :, 0:16], v4[:, t]).then_inc(v_hi, 1)
                    for t in range(TT):
                        pool.wait_ge(v_hi, t + 1)
                        pool.tensor_tensor(vhl[:, t, :, 16:32], v4[:, t], vhl[:, t, :, 0:16], ALU.subtract).then_inc(v_lo, 1)
        heads16(nc, m, "ah", qT, kT, vhl, o, None)
        with ExitStack() as c2:
            _, _, sem2 = names(nc, c2)
            gated = sem2("a1_gated")
            with nc.Block() as block:
                @block.vector
                def _(dve):
                    o4 = o[:, :, :].rearrange("p t (h e) -> p t h e", h=H)
                    dve.tensor_tensor(o4, o4, gates[:, :, 0:H].unsqueeze(3).broadcast_to([P, TT, H, 16]),
                                      ALU.mult).then_inc(gated, 1)
        project(nc, m, "ap", kT, m.late["a1_wo"], m.late["a1_bo"][:, :], src=o)


MAGIC = 1.5 * 2 ** 23


def l1_ffn(nc, m, d):
    with ExitStack() as ctx:
        sb, ps, sem = names(nc, ctx)
        wq = sb("ff_wq", [P, KC, FF], BF16)
        wo = sb("ff_wo_sim", [P, FC, D])
        am = sb("ff_am", [P, 2, FC])
        rs = sb("ff_rs", [P, 2, FC])
        dq = sb("ff_dq", [P, 2, FC])
        with ExitStack() as c2:
            sb2, ps2, sem2 = names(nc, c2)
            w1 = sb2("ff_w1", [P, FC, D])
            w2 = sb2("ff_w2", [P, FC, D])
            w1q = sb2("ff_w1q", [P, FC, D], BF16)
            idb = sb2("ff_idb", [P, P], BF16)
            pW = ps2("ff_pW", [P, 4, 2 * BANK], BF16)
            chain, pchain, id_done, w_t, w_c = (sem2("ff_" + n) for n in ("chain", "pchain", "id_done", "w_t", "w_c"))
            with nc.Block() as block:
                @block.vector
                def _(dve):
                    dve.wait_ge(m.late_loaded, m.late_n)
                    def wide(a, n):
                        return a[:, n, :].unsqueeze(2).broadcast_to([P, FC, D])
                    link = chained(dve, chain)
                    link(dve.tensor_reduce(am[:, 0, :], m.late["ff_w_in"][:, :, :], AX_X, ALU.max, apply_absolute_value=True))
                    link(dve.tensor_reduce(am[:, 1, :], m.late["ff_w_out"][:, :, :], AX_X, ALU.max, apply_absolute_value=True))
                    link(dve.tensor_scalar(am[:, :, :], am[:, :, :], 1e-8, None, ALU.max))
                    link(dve.reciprocal(rs[:, :, :], am[:, :, :]))
                    link(dve.tensor_scalar(rs[:, :, :], rs[:, :, :], 127.0, None, ALU.mult))
                    link(dve.tensor_scalar(dq[:, :, :], am[:, :, :], 1 / 127.0, None, ALU.mult))
                    link(dve.tensor_tensor(w1[:, :, :], m.late["ff_w_in"][:, :, :], wide(rs, 0), ALU.mult))
                    link(dve.tensor_scalar(w1[:, :, :], w1[:, :, :], 127.0, -128.0, ALU.min, ALU.max))
                    link(dve.tensor_scalar(w1q[:, :, :], w1[:, :, :], MAGIC, MAGIC, ALU.add, ALU.subtract))
                    for n in range(4):
                        dve.wait_ge(w_t, n + 1)
                        dve.tensor_copy(wq[:, n // 2, BANK * (n % 2):BANK * (n % 2) + BANK], pW[:, n, 0:BANK]).then_inc(w_c, 1)

                @block.gpsimd
                def _(pool):
                    pool.tensor_copy(idb[:, :], m.ident[:, :]).then_inc(id_done, 1)
                    pool.wait_ge(chain, 6)
                    def wide(a, n):
                        return a[:, n, :].unsqueeze(2).broadcast_to([P, FC, D])
                    link = chained(pool, pchain)
                    link(pool.tensor_tensor(w2[:, :, :], m.late["ff_w_out"][:, :, :], wide(rs, 1), ALU.mult))
                    link(pool.tensor_scalar(w2[:, :, :], w2[:, :, :], 127.0, -128.0, ALU.min, ALU.max))
                    link(pool.tensor_scalar(w2[:, :, :], w2[:, :, :], MAGIC, MAGIC, ALU.add, ALU.subtract))
                    link(pool.tensor_tensor(wo[:, :, :], w2[:, :, :], wide(dq, 1), ALU.mult))

                @block.tensor
                def _(pe):
                    pe.wait_ge(id_done, 1)
                    pe.wait_ge(chain, 9)
                    for n in range(4):
                        for a in range(4):
                            mm = pe.transpose(pW[:, n, P * a:P * a + P],
                                              w1q[:, 4 * (n % 2) + a, P * (n // 2):P * (n // 2) + P], idb[:, :])
                        mm.then_inc(w_t, 1)
        xq = sb("ff_xq", [P, TT, D])
        xh = sb("ff_xh", [P, KC, TOK], BF16)
        xl = sb("ff_xl", [P, KC, TOK], BF16)
        hid = sb("ff_hid", [P, FC, TOK])
        cols = sb("ff_cols", [P, 8])
        hmax = sb("ff_hmax", [P, FC])
        top = sb("ff_top", [1, 2])
        sc = sb("ff_sc", [P, 2, 2])
        dqx = sb("ff_dqx", [P, FC])
        pM = ps("ff_pM", [P, BANK])
        pXT = ps("ff_pXT", [P, KC, BANK])
        pH = ps("ff_pH", [P, 2, BANK])
        chain, m_mm, turned, xhi, h_mm, h_done, hm_done, x_mm = (
            sem("fg_" + n) for n in ("chain", "m_mm", "turned", "xhi", "h_mm", "h_done", "hm_done", "x_mm"))
        steps = [0]

        def largest(dve, link, column, k):
            dve.wait_ge(m_mm, 2 * k + 1)
            link(dve.tensor_reduce(top[0:1, k:k + 1], pM[0:1, 0:P], AX_X, ALU.max))
            link(dve.tensor_scalar(top[0:1, k:k + 1], top[0:1, k:k + 1], 1e-8, None, ALU.max))
            dve.wait_ge(m_mm, 2 * k + 2)
            link(dve.tensor_copy(cols[:, 2 + k:3 + k], pM[:, P:P + 1]))
            link(dve.reciprocal(sc[:, k, 0:1], cols[:, 2 + k:3 + k]))
            link(dve.tensor_scalar(sc[:, k, 0:1], sc[:, k, 0:1], 32767.0, None, ALU.mult))
            link(dve.tensor_scalar(sc[:, k, 1:2], cols[:, 2 + k:3 + k], 1 / 32767.0, None, ALU.mult))

        C_AMAX, C_TOP, C_XQ = 1, 3, 10
        with nc.Block() as block:
            @block.vector
            def _(dve):
                def link(ins):
                    steps[0] += 1
                    ins.then_inc(chain, 1)
                    dve.wait_ge(chain, steps[0])

                link(dve.tensor_reduce(cols[:, 0:1], m.xn[:, :, :].rearrange("p t f -> p (t f)"), AX_X, ALU.max,
                                       apply_absolute_value=True))
                largest(dve, link, 0, 0)
                link(dve.tensor_scalar(xq[:, :, :], m.xn[:, :, :], sc[:, 0, 0:1], 32767.0, ALU.mult, ALU.min))
                link(dve.tensor_scalar(xq[:, :, :], xq[:, :, :], -32768.0, MAGIC, ALU.max, ALU.add))
                link(dve.tensor_scalar(xq[:, :, :], xq[:, :, :], MAGIC, None, ALU.subtract))
                assert steps[0] == C_XQ
                link(dve.tensor_scalar(dqx[:, :], dq[:, 0, :], sc[:, 0, 1:2], None, ALU.mult))
                for c in range(KC):
                    dve.wait_ge(xhi, c + 1)
                    link(dve.tensor_tensor(xl[:, c, :], pXT[:, c, :], xh[:, c, :], ALU.subtract))
                link(dve.tensor_tensor(m.x[:, :, :], m.x[:, :, :], m.late["ff_b_out"][:, :].unsqueeze(1).broadcast_to([P, TT, D]),
                                       ALU.add))
                for n in range(FC):
                    dve.wait_ge(h_done, n + 1)
                    dve.tensor_reduce(hmax[:, n:n + 1], hid[:, n, :], AX_X, ALU.max, apply_absolute_value=True).then_inc(
                        hm_done, 1)
                dve.wait_ge(hm_done, FC)
                link(dve.tensor_reduce(cols[:, 1:2], hmax[:, :], AX_X, ALU.max))

            @block.scalar
            def _(act):
                for c in range(KC):
                    act.wait_ge(turned, c + 1)
                    act.activation(xh[:, c, :], pXT[:, c, :], ACT.Copy).then_inc(xhi, 1)
                act.wait_ge(chain, C_XQ + 1)
                for n in range(FC):
                    act.wait_ge(h_mm, n + 1)
                    act.activation(hid[:, n, :], pH[:, n % 2, :], ACT.Gelu, bias=m.late["ff_b_in"][:, n:n + 1],
                                   scale=dqx[:, n:n + 1]).then_inc(h_done, 1)

            @block.tensor
            def _(pe):
                pe.wait_ge(chain, C_AMAX)
                pe.transpose(pM[0:1, 0:P], cols[:, 0:1], m.ident[:, :]).then_inc(m_mm, 1)
                pe.wait_ge(chain, C_TOP)
                pe.matmul(pM[:, P:P + 1], m.ones_row, top[0:1, 0:1], start=True, stop=True).then_inc(m_mm, 1)
                pe.wait_ge(chain, C_XQ)
                for c in range(KC):
                    for t in range(TT):
                        mm = pe.transpose(pXT[:, c, P * t:P * t + P], xq[:, t, P * c:P * c + P], m.ident[:, :])
                    mm.then_inc(turned, 1)
                pe.wait_ge(chain, C_XQ + 1 + KC)
                for n in range(FC):
                    if n >= 2:
                        pe.wait_ge(h_done, n - 1)
                    for a in range(4):
                        c, xx = a // 2, (xh, xl)[a % 2]
                        mm = pe.matmul(pH[:, n % 2, :], wq[:, c, P * n:P * n + P], xx[:, c, :], start=(a == 0), stop=(a == 3))
                    mm.then_inc(h_mm, 1)
        pX = ps("ff_pX", [P, 2, BANK])
        chain2, x_done, fq = (sem("fh_" + n) for n in ("chain", "x_done", "fq"))
        with nc.Block() as block:
            @block.vector
            def _(dve):
                done = [0]

                def link(ins):
                    done[0] += 1
                    ins.then_inc(chain2, 1)
                    dve.wait_ge(chain2, done[0])

                largest(dve, link, 1, 1)
                for n in range(FC):
                    link(dve.tensor_scalar(hid[:, n, :], hid[:, n, :], sc[:, 1, 0:1], 32767.0, ALU.mult, ALU.min))
                    link(dve.tensor_scalar(hid[:, n, :], hid[:, n, :], -32768.0, MAGIC, ALU.max, ALU.add))
                    link(dve.tensor_scalar(hid[:, n, :], hid[:, n, :], MAGIC, None, ALU.subtract))
                for t in range(TT):
                    dve.wait_ge(x_mm, t + 1)
                    dve.scalar_tensor_tensor(m.x[:, t, :], (pX if t < 2 else pXT)[:, t % 2, 0:D], sc[:, 1, 1:2], m.x[:, t, :],
                                             ALU.mult, ALU.add).then_inc(x_done, 1)

            @block.tensor
            def _(pe):
                pe.transpose(pM[0:1, 0:P], cols[:, 1:2], m.ident[:, :]).then_inc(m_mm, 1)
                pe.wait_ge(chain2, 2)
                pe.matmul(pM[:, P:P + 1], m.ones_row, top[0:1, 1:2], start=True, stop=True).then_inc(m_mm, 1)
                for n in range(FC):
                    pe.wait_ge(chain2, 6 + 3 * (n + 1))
                    for t in range(TT):
                        mm = pe.matmul((pX if t < 2 else pXT)[:, t % 2, 0:D], hid[:, n, P * t:P * t + P], wo[:, n, :],
                                       start=(n == 0), stop=(n == FC - 1))
                        if n == FC - 1:
                            mm.then_inc(x_mm, 1)


LATE = {
    "gl_wq": [P, KC, D], "gl_wkv": [P, KC, 2 * D], "gl_wf": [P, KC, 96], "gl_g1": [P, KC, 16], "gl_g2": [16, D],
    "gl_lnw": [P, D], "gl_wo": [P, KC, D], "scanmask": [P, TOK],
    "x1_wq": [P, KC, D], "x1_bq": [P, KC], "x1_wkv": [P, 2, 2 * D], "x1_bk": [P, KC], "x1_bv": [P, KC],
    "x1_wo": [P, KC, D], "x1_bo": [1, D],
    "a1_wqk": [P, KC, 2 * D], "a1_wv": [P, KC, D], "a1_wo": [P, KC, D], "a1_bo": [1, D], "a1_gamma": [P, D],
    "a1_beta": [P, D], "a1_g": [P, 2 * D],
    "ff_w_in": [P, FC, D], "ff_w_out": [P, FC, D], "ff_b_in": [P, FC], "ff_b_out": [P, D],
    "mo_gate": [P, KC, E], "mo_wg": [P, E, KC, I], "mo_wu": [P, E, KC, I], "mo_wd": [P, E, D],
}


def late_weights(nc, m, d, sb, sb_moe):
    onehot = sb("onehot", [96, H, P], BF16)
    tiles = {name: (sb_moe if name[:2] == "mo" else sb)("w_" + name, shape) for name, shape in LATE.items()}
    m.late = {"onehot": onehot, **tiles}
    m.late_n = 16 * len(LATE)
    with nc.Block() as block:
        @block.sync
        def _(sp):
            sp.wait_ge(m.w0_loaded, 48)
            for name, shape in LATE.items():
                t = tiles[name]
                sp.dma_start(t[:, :] if len(shape) == 2 else t[:, :, :] if len(shape) == 3 else t[:, :, :, :],
                             d[name]).then_inc(m.late_loaded, 16)

        @block.gpsimd
        def _(pool):
            one = m.small[0:96, SMALL["onehot"]:SMALL["onehot"] + H]
            pool.wait_ge(m.const_loaded, m.const_n)
            pool.wait_ge(m.w0_loaded, 48)
            pool.tensor_copy(onehot[:, :, :], one.unsqueeze(2).broadcast_to([96, H, P])).then_inc(m.onehot_made, 1)


def clear_semaphores(nc):
    done = sorted(nc.released_uncleared_semaphores)
    runs, start = [], None
    for n, s in enumerate(done):
        start = s if start is None else start
        if n + 1 == len(done) or done[n + 1] != s + 1:
            runs.append(range(start, s + 1))
            start = None
    with nc.Block() as block:
        @block.gpsimd
        def _(pool):
            for r in runs:
                pool.sem_clear(r)


def build(nc, d, out):
    with ExitStack() as ctx:
        sb, ps, sem = names(nc, ctx)
        m = Shared()
        m.x_loaded, m.const_loaded, m.w0_loaded, m.late_loaded, m.onehot_made, m.stored = (
            sem(n) for n in ("x_loaded", "const_loaded", "w0_loaded", "late_loaded", "onehot_made", "stored"))
        m.x = sb("x", [P, TT, D])
        m.xn = sb("xn", [P, TT, D])
        m.xnT = sb("xnT", [P, KC, TOK])
        m.ident = sb("ident", [P, P])
        m.maskneg = sb("maskneg", [P, BANK])
        m.mask05 = sb("mask05", [P, BANK])
        m.small = sb("small", [P, SMALL["n"]])
        m.eps = m.small[:, SMALL["eps"]:SMALL["eps"] + 1]
        m.one = m.small[:, SMALL["ones"]:SMALL["ones"] + 1]
        m.tanh_bias = m.small[:, SMALL["tanh"]:SMALL["tanh"] + 1]
        m.ones_row = m.small[0:1, SMALL["ones"]:SMALL["ones"] + P]
        m.const_n = 64
        with ExitStack() as c2:
            sb2, _, _ = names(nc, c2)
            m.wv0 = sb2("wv0", [P, 2, 1024])
            m.wo0 = sb2("wo0", [P, PAIRS, D])
            m.bo0 = sb2("bo0", [1, D])
            load_inputs(nc, m, d)
            m.quA = sb2("quA", [P, 2, B, PAIRS, P], BF16)
            m.quB = sb2("quB", [P, B, PAIRS, P], BF16)
            layer_norm(nc, m, "ln0", m.x, m.xn, m.xnT)
            l0x_queries(nc, m, d)
            l0x_attention(nc, m, d)
            l0x_output(nc, m, d)
        with ExitStack() as c2:
            sb2, _, _ = names(nc, c2)
            with ExitStack() as c3:
                late_weights(nc, m, d, sb2, names(nc, c3)[0])
                layer_norm(nc, m, "ln1", m.x, m.xn, m.xnT)
                l0_gla(nc, m, d)
                layer_norm(nc, m, "ln2", m.x, m.xn, m.xnT)
                l0_moe(nc, m, d)
            clear_semaphores(nc)
            layer_norm(nc, m, "ln3", m.x, m.xn, m.xnT)
            l1x(nc, m, d)
            layer_norm(nc, m, "ln4", m.x, m.xn, m.xnT)
            l1_attn(nc, m, d)
            layer_norm(nc, m, "ln5", m.x, m.xn, None)
            l1_ffn(nc, m, d)
        with nc.Block() as block:
            @block.sync
            def _(sp):
                sp.wait_ge(m.w0_loaded, 48)
                sp.wait_ge(m.late_loaded, m.late_n)
                sp.dma_start(out, m.x[:, :, :]).then_inc(m.stored, 16)
                sp.wait_ge(m.stored, 16)


SMALL = {"eps": 0, "ones": 1, "hmask": 129, "desc": 137, "tanh": 145, "rowmask": 146, "fold": 210, "onehot": 274, "n": 290}


def layouts(v):
    f = np.float32
    c = np.ascontiguousarray

    def rows(w, n=P):
        w = np.asarray(w)
        return c(w.reshape(-1, n, w.shape[1]).transpose(1, 0, 2))

    a = {}
    a["x"] = rows(v["x"].reshape(TOK, D))
    ctx = v["ctx_768"]
    pad = np.zeros((B, MC * P, DC), f)
    pad[:, :M] = ctx
    a["ctxn"] = c(pad.reshape(B, MC, P, DC).transpose(0, 2, 1, 3))
    a["ctxT"] = c(ctx.transpose(0, 2, 1))
    a["wq0"] = rows(v["L0_xattn_Wq"])
    wkT = v["L0_xattn_Wk"].T
    a["wk0"] = rows(np.concatenate([wkT, wkT[:, P:]], axis=1))
    wv = v["L0_xattn_Wv"]
    a["wv0"] = c(np.stack([wv[:P], np.concatenate([wv[P:], wv[P:]])], axis=1))
    a["wo0"] = rows(v["L0_xattn_Wo"])
    a["bo0"] = c(v["L0_xattn_bo"][None])
    a["ident"] = np.eye(P, dtype=f)
    s, t = np.arange(P)[:, None], np.arange(P)[None]
    same = s // NQ == t // NQ
    a["maskneg"] = np.tile(np.where(same & (s <= t), 0, -1e30).astype(f), (1, 4))
    a["mask05"] = np.tile(np.where(same, 0.5, 0).astype(f), (1, 4))
    small = np.zeros((P, SMALL["n"]), f)
    small[:, SMALL["eps"]] = 1e-5
    small[:, SMALL["ones"]:SMALL["ones"] + P] = 1
    small[:, SMALL["hmask"]:SMALL["hmask"] + 8] = np.arange(P)[:, None] // 16 == np.arange(8)
    small[:, SMALL["desc"]:SMALL["desc"] + E] = E - np.arange(E)
    small[:, SMALL["tanh"]] = -15.0 * 0.27
    r = np.arange(P)[:, None]
    small[:, SMALL["rowmask"]:SMALL["rowmask"] + 64] = r // NQ == np.arange(64) % 32 // 16
    small[:, SMALL["fold"]:SMALL["fold"] + NQ] = r % NQ == np.arange(NQ)
    small[:, SMALL["onehot"]:SMALL["onehot"] + H] = r % 32 == np.arange(H)
    a["small"] = small

    gl = {n: v["L0_attn_" + n] for n in ("Wq", "Wk", "Wv", "Wf", "Wg1", "Wg2", "ln_w", "Wo")}
    a["gl_wq"] = rows(gl["Wq"].T)
    a["gl_wkv"] = rows(np.concatenate([gl["Wk"].T, gl["Wv"].T], axis=1))
    wf = np.zeros((D, 96), f)
    for n in range(3):
        wf[:, 32 * n:32 * n + 16] = gl["Wf"].T
    a["gl_wf"] = rows(wf)
    a["gl_g1"] = rows(gl["Wg1"].T)
    a["gl_g2"] = c(gl["Wg2"].T)
    a["gl_lnw"] = c(np.broadcast_to(gl["ln_w"], (P, D)))
    a["gl_wo"] = rows(gl["Wo"].T)
    a["scanmask"] = np.tile((np.arange(TOK) % NQ != 0).astype(f), (P, 1))
    a["mo_gate"] = rows(v["L0_ffn_gate_w"].T)
    for n, w in (("mo_wg", "w_gate"), ("mo_wu", "w_up")):
        a[n] = c(v["L0_ffn_" + w].reshape(E, I, KC, P).transpose(3, 0, 2, 1))
    a["mo_wd"] = c(v["L0_ffn_w_down"].transpose(2, 0, 1))

    def cols(b, n=P):
        return c(np.asarray(b).reshape(-1, n).T)

    x1 = {n: v["L1_xattn_" + n] for n in ("Wq", "bq", "Wkv", "bkv", "Wo", "bo")}
    ik = (np.arange(H)[:, None] * 32 + np.arange(16)).ravel()
    a["x1_wq"] = rows(x1["Wq"].T)
    a["x1_bq"] = cols(x1["bq"])
    wkv = x1["Wkv"][np.concatenate([ik, ik + 16])].T
    a["x1_wkv"] = c(np.stack([wkv[:P], np.concatenate([wkv[P:], wkv[P:]])], axis=1))
    a["x1_bk"] = cols(x1["bkv"][ik])
    a["x1_bv"] = cols(x1["bkv"][ik + 16])
    a["x1_wo"] = rows(x1["Wo"].T)
    a["x1_bo"] = c(x1["bo"][None])
    a1 = {n: v["L1_attn_" + n] for n in ("w_q", "w_k", "w_v", "g_q", "g_k", "w_o", "b_o", "gamma", "beta")}
    a["a1_wqk"] = rows(np.concatenate([a1["w_q"], a1["w_k"]], axis=1))
    a["a1_wv"] = rows(a1["w_v"])
    a["a1_wo"] = rows(a1["w_o"])
    a["a1_bo"] = c(a1["b_o"][None])
    for n in ("gamma", "beta"):
        a["a1_" + n] = c(np.broadcast_to(a1[n], (P, D)))
    a["a1_g"] = c(np.broadcast_to(np.concatenate([np.tile(a1["g_q"], H), np.tile(a1["g_k"], H)]), (P, 2 * D)))
    a["ff_w_in"] = rows(v["L1_ffn_W_in"].T)
    a["ff_w_out"] = rows(v["L1_ffn_W_out"])
    a["ff_b_in"] = cols(v["L1_ffn_b_in"])
    a["ff_b_out"] = c(np.broadcast_to(v["L1_ffn_b_out"], (P, D)))
    return a


def kernel(**inputs):
    import concourse.bacc as _bacc
    from concourse.bass_utils import run_bass_kernel_spmd as _run

    arrays = layouts({k: np.asarray(v) for k, v in inputs.items()})
    nc = _bacc.Bacc("TRN2", target_bir_lowering=False, num_devices=1)
    d = {n: nc.dram_tensor(f"in_{n}", a.shape, mybir.dt.from_np(a.dtype), kind="ExternalInput").ap()
         for n, a in arrays.items()}
    out = nc.dram_tensor("out_x", (P, TT, D), F32, kind="ExternalOutput").ap()
    build(nc, d, out)
    r = _run(nc, [{f"in_{n}": a for n, a in arrays.items()}], core_ids=[0])
    y = np.asarray(r.results[0]["out_x"])
    return y.transpose(1, 0, 2).reshape(B, NQ, D)
```

```python
from contextlib import ExitStack

import numpy as np
import concourse.bass as bass
from concourse import mybir
from concourse.alu_op_type import AluOpType as ALU

F32 = mybir.dt.float32
BF16 = mybir.dt.bfloat16
ACT = mybir.ActivationFunctionType
AX_X = mybir.AxisListType.X

P = 128
B, NQ, D = 8, 64, 256
TOK = B * NQ
TT = TOK // P
KC = D // P
M, DC = 1601, 192
DB = DC - P
MC = -(-M // P)
ML = M - (MC - 1) * P
H = 16
PAIRS = H // 2
BANK = 512
SEG = [(j * BANK, min(BANK, M - j * BANK)) for j in range(-(-M // BANK))]
TGRP = [(g, range(4 * g, min(4 * g + 4, MC))) for g in range(-(-MC // 4))]
NG = len(TGRP)
E, I = 8, 128
FF = 1024
FC = FF // P


class Shared:
    pass


class Parts:
    def __init__(self, sb, tag, natural):
        if natural:
            self.nh, self.nl = (sb(f"{tag}_{n}", [P, MC, DC], BF16) for n in ("nh", "nl"))
        self.ah, self.al, self.bh, self.bl = (sb(f"{tag}_{n}", [P, M + 1], BF16) for n in ("ah", "al", "bh", "bl"))


def names(nc, ctx):
    def sb(name, shape, dt=F32):
        return ctx.enter_context(nc.sbuf_tensor(name, shape, dt))

    def ps(name, shape, dt=F32):
        return ctx.enter_context(nc.psum_tensor(name, shape, dt))

    def sem(name):
        return ctx.enter_context(nc.semaphore(name))

    return sb, ps, sem


def chained(eng, sem):
    done = [0]

    def link(ins):
        done[0] += 1
        ins.then_inc(sem, 1)
        eng.wait_ge(sem, done[0])

    return link


def load_inputs(nc, m, d):
    with ExitStack() as ctx:
        with nc.Block() as block:
            @block.sync
            def _(sp):
                sp.dma_start(m.x[:, :, :], d["x"]).then_inc(m.x_loaded, 16)
                sp.dma_start(m.ident[:, :], d["ident"]).then_inc(m.const_loaded, 16)
                sp.dma_start(m.maskneg[:, :], d["maskneg"]).then_inc(m.const_loaded, 16)
                sp.dma_start(m.mask05[:, :], d["mask05"]).then_inc(m.const_loaded, 16)
                sp.dma_start(m.small[:, :], d["small"]).then_inc(m.const_loaded, 16)
                sp.dma_start(m.wv0[:, :, :], d["wv0"]).then_inc(m.w0_loaded, 16)
                sp.dma_start(m.wo0[:, :, :], d["wo0"]).then_inc(m.w0_loaded, 16)
                sp.dma_start(m.bo0[:, :], d["bo0"]).then_inc(m.w0_loaded, 16)


def layer_norm(nc, m, tag, src, dst, dstT, affine=None):
    with ExitStack() as ctx:
        sb, ps, sem = names(nc, ctx)
        stats = sb(f"{tag}_stats", [P, TT, 6])
        mv = sb(f"{tag}_meanvar", [P, TT, 2])
        std = sb(f"{tag}_std", [P, TT])
        rstd = sb(f"{tag}_rstd", [P, TT])
        pT = ps(f"{tag}_pT", [P, KC, BANK])
        stats_done, mv_done, std_done, rstd_done, normed, scaled, done, turned, copied = (
            sem(f"{tag}_{n}") for n in
            ("stats_done", "mv_done", "std_done", "rstd_done", "normed", "scaled", "done", "turned", "copied"))
        with nc.Block() as block:
            @block.vector
            def _(dve):
                dve.wait_ge(m.x_loaded, 16)
                for t in range(TT):
                    dve.bn_stats(stats[:, t, :], src[:, t, :]).then_inc(stats_done, 1)
                for t in range(TT):
                    dve.wait_ge(stats_done, t + 1)
                    dve.bn_aggr(mv[:, t, :], stats[:, t, :]).then_inc(mv_done, 1)
                dve.wait_ge(std_done, 1)
                dve.reciprocal(rstd[:, :], std[:, :]).then_inc(rstd_done, 1)
                dve.wait_ge(rstd_done, 1)
                for t in range(TT):
                    o = dve.tensor_scalar(dst[:, t, :], src[:, t, :], mv[:, t, 0:1], rstd[:, t:t + 1],
                                          ALU.subtract, ALU.mult)
                    o.then_inc(normed if affine else done, 1)
                if affine:
                    dve.wait_ge(m.late_loaded, m.late_n)
                    for t in range(TT):
                        dve.wait_ge(normed, t + 1)
                        dve.tensor_tensor(dst[:, t, :], dst[:, t, :], affine[0], ALU.mult).then_inc(
                            scaled if affine[1] is not None else done, 1)
                    if affine[1] is not None:
                        for t in range(TT):
                            dve.wait_ge(scaled, t + 1)
                            dve.tensor_tensor(dst[:, t, :], dst[:, t, :], affine[1], ALU.add).then_inc(done, 1)
                if dstT is not None:
                    dve.wait_ge(turned, KC * TT)
                    dve.tensor_copy(dstT[:, 1, :], pT[:, 1, :]).then_inc(copied, 1)

            @block.scalar
            def _(act):
                act.wait_ge(mv_done, TT)
                act.wait_ge(m.const_loaded, m.const_n)
                act.activation(std[:, :], mv[:, :, 1], ACT.Sqrt, bias=m.eps).then_inc(std_done, 1)
                if dstT is not None:
                    act.wait_ge(turned, TT)
                    act.activation(dstT[:, 0, :], pT[:, 0, :], ACT.Copy).then_inc(copied, 1)

            if dstT is not None:
                @block.tensor
                def _(pe):
                    pe.wait_ge(m.const_loaded, m.const_n)
                    pe.wait_ge(done, TT)
                    for c in range(KC):
                        for t in range(TT):
                            pe.transpose(pT[:, c, P * t:P * t + P], dst[:, t, P * c:P * c + P],
                                         m.ident[:, :]).then_inc(turned, 1)


NSPLIT0 = 6


def context0(nc, ctx):
    sb, _, sem = names(nc, ctx)
    c = Shared()
    c.stN = sb("stN", [P, MC, DC])
    c.stA = sb("stA", [P, M])
    c.stB = sb("stB", [P, M])
    c.hl = [Parts(sb, f"ctx{n}", True) for n in range(2)]
    c.ctx_in, c.begun, c.split = (sem("a0_" + n) for n in ("ctx_in", "begun", "split"))
    return c


def load_context0(sp, d, c, b):
    sp.dma_start(c.stA[:, :], d["ctxT"][bass.ds(b, 1), 0:P].rearrange("o p c -> (o p) c")).then_inc(c.ctx_in, 16)
    for s in (0, 64):
        sp.dma_start(c.stB[s:s + 64, :], d["ctxT"][bass.ds(b, 1), P:DC].rearrange("o p c -> (o p) c")).then_inc(c.ctx_in, 16)
    sp.dma_start(c.stN[:, :, :], d["ctxn"][bass.ds(b, 1)].rearrange("o p c f -> (o p) c f")).then_inc(c.ctx_in, 16)


def split_context0(pool, c, b, o):
    pool.wait_ge(c.ctx_in, (b + 1) * 64)
    pool.sem_inc(c.begun, 1)
    parts = ((o.ah[:, 0:M], o.al[:, 0:M], c.stA[:, :]), (o.bh[:, 0:M], o.bl[:, 0:M], c.stB[:, :]),
             (o.nh[:, :, :], o.nl[:, :, :], c.stN[:, :, :]))
    for first, group in ((0, parts[0:2]), (4, parts[2:3])):
        for hi, _, src in group:
            pool.tensor_copy(hi, src).then_inc(c.split, 1)
        for n, (hi, lo, src) in enumerate(group):
            pool.wait_ge(c.split, 1 + b * NSPLIT0 + first + n + 1)
            pool.tensor_tensor(lo, src, hi, ALU.subtract).then_inc(c.split, 1)


def l0x_queries(nc, m, d, c0):
    with ExitStack() as ctx:
        sb, ps, sem = names(nc, ctx)
        wq = sb("wq0", [P, KC, 1024])
        wk = sb("wk0", [P, PAIRS, D])
        wkh = sb("wk0h", [P, PAIRS, D], BF16)
        wkl = sb("wk0l", [P, PAIRS, D], BF16)
        qzh = sb("qzh", [P, 2, 2, TOK], BF16)
        qzl = sb("qzl", [P, 2, 2, TOK], BF16)
        pQ = ps("pQ", [P, 2, BANK])
        pK = ps("pK", [P, 4, BANK])
        w_in, wkh_done, wkl_done, zeroed, q_mm, q_hi, q_lo, qk_mm, qk_hi, qk_lo = (
            sem(n) for n in ("q0_w_in", "q0_wkh", "q0_wkl", "q0_zeroed", "q0_q_mm", "q0_q_hi", "q0_q_lo",
                             "q0_qk_mm", "q0_qk_hi", "q0_qk_lo"))
        with nc.Block() as block:
            @block.sync
            def _(sp):
                sp.dma_start(wq[:, :, :], d["wq0"]).then_inc(w_in, 16)
                sp.dma_start(wk[:, :, :], d["wk0"]).then_inc(w_in, 16)
                load_context0(sp, d, c0, 0)

            @block.gpsimd
            def _(pool):
                pool.memset(qzh[:, :, :, :], 0.0).then_inc(zeroed, 1)
                pool.memset(qzl[:, :, :, :], 0.0).then_inc(zeroed, 1)
                pool.wait_ge(w_in, 32)
                pool.tensor_copy(wkh[:, :, :], wk[:, :, :]).then_inc(wkh_done, 1)
                pool.wait_ge(wkh_done, 1)
                pool.tensor_tensor(wkl[:, :, :], wk[:, :, :], wkh[:, :, :], ALU.subtract).then_inc(wkl_done, 1)
                pool.wait_ge(wkl_done, 1)
                pool.sem_inc(c0.split, 1)
                split_context0(pool, c0, 0, c0.hl[0])

            @block.tensor
            def _(pe):
                pe.wait_ge(w_in, 32)
                for p in range(PAIRS + 1):
                    if p < PAIRS:
                        if p >= 2:
                            pe.wait_ge(q_lo, 2 * (p - 1))
                        for c in range(KC):
                            mm = pe.matmul(pQ[:, p % 2, :], wq[:, c, P * p:P * p + P], m.xnT[:, c, :],
                                           start=(c == 0), stop=(c == KC - 1))
                        mm.then_inc(q_mm, 1)
                    if p >= 1:
                        r = (p - 1) % 2
                        pe.wait_ge(q_lo, 2 * p)
                        pe.wait_ge(wkl_done, 1)
                        for n in range(4 * (p - 1), 4 * p):
                            h, part = (n % 4) // 2, n % 2
                            if n >= 4:
                                pe.wait_ge(qk_lo, n - 3)
                            w = slice(P * part, P * part + P)
                            for a, (wt, q) in enumerate(((wkh, qzh), (wkh, qzl), (wkl, qzh))):
                                mm = pe.matmul(pK[:, n % 4, :], wt[:, p - 1, w], q[:, r, h, :],
                                               start=(a == 0), stop=(a == 2))
                            mm.then_inc(qk_mm, 1)

            def qu_out(n):
                p, h, part = n // 4, (n % 4) // 2, n % 2
                s = slice(NQ * h, NQ * h + NQ)
                return part, (m.quA[:, 0, :, p, s], m.quA[:, 1, :, p, s], m.quB[:, :, p, s])

            @block.scalar
            def _(act):
                act.wait_ge(zeroed, 2)
                for p in range(PAIRS + 1):
                    if p < PAIRS:
                        act.wait_ge(q_mm, p + 1)
                        if p >= 2:
                            act.wait_ge(qk_mm, 4 * (p - 1))
                        for h in range(2):
                            s = slice(64 * h, 64 * h + 64)
                            act.activation(qzh[s, p % 2, h, :], pQ[s, p % 2, :], ACT.Copy).then_inc(q_hi, 1)
                    if p >= 1:
                        for n in range(4 * (p - 1), 4 * p):
                            part, (ah, al, b) = qu_out(n)
                            act.wait_ge(qk_mm, n + 1)
                            src = pK[:, n % 4, :].rearrange("p (b i) -> p b i", b=B)
                            act.activation(b if part else ah, src, ACT.Copy).then_inc(qk_hi, 1)

            @block.vector
            def _(dve):
                for p in range(PAIRS + 1):
                    if p < PAIRS:
                        for h in range(2):
                            s = slice(64 * h, 64 * h + 64)
                            dve.wait_ge(q_hi, 2 * p + h + 1)
                            dve.tensor_tensor(qzl[s, p % 2, h, :], pQ[s, p % 2, :], qzh[s, p % 2, h, :],
                                              ALU.subtract).then_inc(q_lo, 1)
                    if p >= 1:
                        for n in range(4 * (p - 1), 4 * p):
                            part, (ah, al, b) = qu_out(n)
                            dve.wait_ge(qk_hi, n + 1)
                            src = pK[:, n % 4, :].rearrange("p (b i) -> p b i", b=B)
                            if part:
                                dve.tensor_tensor(b[64:128], src[64:128], b[64:128], ALU.subtract).then_inc(qk_lo, 1)
                            else:
                                dve.tensor_tensor(al, src, ah, ALU.subtract).then_inc(qk_lo, 1)


def l0x_attention(nc, m, d, c0):
    SCALE = 64 ** -0.5
    T2 = 2 * PAIRS
    with ExitStack() as ctx:
        sb, ps, sem = names(nc, ctx)
        hl = c0.hl
        prob = sb("prob", [P, 2, M])
        pth = sb("pth", [P, MC, P], BF16)
        ptl = sb("ptl", [P, MC, P], BF16)
        mx = sb("mx", [P, 2])
        nmax = sb("nmax", [P, 2])
        rsum = sb("rsum", [P, 2])
        rinv = sb("rinv", [P, 2])
        u = sb("u", [P, D])
        pS = ps("pS", [P, 4 * BANK])
        pT = ps("pT", [P, 2, BANK])
        pU = ps("pU", [P, D])
        pV = ps("pV", [P, 2, P])
        (s_done, exp_done, t_done, hi_done, lo_done, av_done, mx_done, nmax_done, rinv_done,
         u_done, ut_done, uhi_done, ulo_done) = (sem("a0_" + n) for n in (
             "s_done", "exp_done", "t_done", "hi_done", "lo_done", "av_done", "mx_done",
             "nmax_done", "rinv_done", "u_done", "ut_done", "uhi_done", "ulo_done"))
        split = c0.split

        def bodies(eng, body):
            body(0, True, range(T2))
            with eng.Fori(1, B // 2) as i:
                body(i * 2, False, range(T2))
            body(B - 2, False, range(T2, T2 + 2))

        with nc.Block() as block:
            @block.sync
            def _(sp):
                with sp.Fori(1, B) as b:
                    sp.wait_ge(split, 1 + b * NSPLIT0)
                    load_context0(sp, d, c0, b)

            @block.gpsimd
            def _(pool):
                split_context0(pool, c0, 1, hl[1])
                with pool.Fori(1, B // 2) as i:
                    b = i * 2
                    for par in range(2):
                        pool.wait_ge(av_done, 1 + b * PAIRS + (par - 1) * PAIRS)
                        split_context0(pool, c0, b + par, hl[par])

            @block.tensor
            def _(pe):
                for s in (s_done, t_done, av_done, ut_done):
                    pe.sem_inc(s, 1)

                def body(b, first, steps):
                    k0 = b * PAIRS
                    least = 0 if first else -9

                    def scores(t, j):
                        par, p = t // PAIRS, t % PAIRS
                        c = hl[par % 2]
                        s, w = SEG[j]
                        qa = [m.quA[:, n, bass.ds(b + par, 1), p, :].rearrange("p o r -> p (o r)") for n in (0, 1)]
                        qb = m.quB[:, bass.ds(b + par, 1), p, :].rearrange("p o r -> p (o r)")
                        if j == 0:
                            pe.wait_ge(exp_done, 1 + k0 + t)
                            if p == 0:
                                pe.wait_ge(split, 1 + (b + par) * NSPLIT0 + 4)
                        for a, (q, k) in enumerate(((qa[0], c.ah), (qa[0], c.al), (qa[1], c.ah), (qb, c.bh), (qb, c.bl))):
                            mm = pe.matmul(pS[:, s:s + w], q, k[:, s:s + w], start=(a == 0), stop=(a == 4))
                        if j in (1, 3):
                            mm.then_inc(s_done, 1)

                    def turn_probs(t, g):
                        n = 4 * t + g
                        if g == 0:
                            pe.wait_ge(exp_done, 1 + k0 + t + 1)
                        pe.wait_ge(lo_done, 1 + k0 * NG + max(n - 1, least))
                        for c in TGRP[g][1]:
                            w = min(P, M - P * c)
                            mm = pe.transpose(pT[0:w, n % 2, P * (c % 4):P * (c % 4) + P],
                                              prob[:, t % 2, P * c:P * c + w], m.ident[:, :])
                        mm.then_inc(t_done, 1)

                    def values(t, chunks):
                        c = hl[t // PAIRS % 2]
                        if chunks[0] == 0:
                            pe.wait_ge(u_done, 1 + (k0 + t) * 2)
                            if t % PAIRS == 0:
                                pe.wait_ge(split, 1 + (b + t // PAIRS + 1) * NSPLIT0)
                        for n in chunks:
                            w = min(P, M - P * n)
                            if n % 4 == 0:
                                pe.wait_ge(lo_done, 1 + (k0 + t) * NG + n // 4 + 1)
                            for a, (pr, cx) in enumerate(((pth, c.nh), (pth, c.nl), (ptl, c.nh))):
                                mm = pe.matmul(pU[:, 0:DC], pr[0:w, n, :], cx[0:w, n, :],
                                               start=(n == 0 and a == 0), stop=(n == MC - 1 and a == 2))
                        if n == MC - 1:
                            mm.then_inc(av_done, 1)

                    def turn_result(t):
                        pe.wait_ge(u_done, 1 + (k0 + t + 1) * 2)
                        pe.wait_ge(ulo_done, 1 + (k0 + t) * 2)
                        for n in range(2):
                            pe.transpose(pV[:, n, :], u[:, P * n:P * n + P], m.ident[:, :]).then_inc(ut_done, 1)

                    for t in steps:
                        for j in range(4):
                            if t < T2:
                                scores(t, j)
                            if least + 1 <= t <= T2 and j < 2:
                                turn_probs(t - 1, j)
                        if least + 1 <= t <= T2:
                            turn_probs(t - 1, 2)
                            values(t - 1, range(0, 8))
                            turn_probs(t - 1, 3)
                            values(t - 1, range(8, MC))
                        if t >= least + 2:
                            turn_result(t - 2)

                bodies(pe, body)

            @block.scalar
            def _(act):
                for s in (exp_done, hi_done, uhi_done):
                    act.sem_inc(s, 1)

                def body(b, first, steps):
                    k0 = b * PAIRS
                    least = 0 if first else -9
                    def high_probs(t, g):
                        cs = TGRP[g][1]
                        n = 4 * t + g
                        w = min(P, M - P * cs[0])
                        if g == 0:
                            act.wait_ge(av_done, 1 + k0 + t)
                        act.wait_ge(t_done, 1 + (k0 + t) * NG + g + 1)
                        act.activation(pth[0:w, cs[0]:cs[-1] + 1, :], pT[0:w, n % 2, 0:P * len(cs)].rearrange(
                            "p (c r) -> p c r", r=P), ACT.Copy).then_inc(hi_done, 1)

                    for t in steps:
                        for g, cs in TGRP[:3] if least + 1 <= t <= T2 else ():
                            high_probs(t - 1, g)
                        if t < T2:
                            act.wait_ge(nmax_done, 1 + k0 + t + 1)
                            act.wait_ge(t_done, 1 + (k0 + max(t - 1, least)) * NG)
                            act.activation(prob[:, t % 2, :], pS[:, 0:M], ACT.Exp, bias=nmax[:, t % 2:t % 2 + 1], scale=SCALE,
                                           accum_out=rsum[:, t % 2:t % 2 + 1]).then_inc(exp_done, 1)
                        if least + 1 <= t <= T2:
                            high_probs(t - 1, 3)
                        if t >= least + 2:
                            par, p = (t - 2) // PAIRS, (t - 2) % PAIRS
                            for n in range(2):
                                act.wait_ge(ut_done, 1 + (k0 + t - 1) * 2)
                                o = m.quB[:, bass.ds(b + par, 1), p, :] if n else m.quA[:, 0, bass.ds(b + par, 1), p, :]
                                act.activation(o.rearrange("p o r -> p (o r)"), pV[:, n, :], ACT.Copy).then_inc(uhi_done, 1)

                bodies(act, body)

            @block.vector
            def _(dve):
                for s in (lo_done, mx_done, nmax_done, rinv_done, u_done, ulo_done):
                    dve.sem_inc(s, 1)

                def body(b, first, steps):
                    k0 = b * PAIRS
                    least = 0 if first else -9

                    def low_probs(t, g):
                        cs = TGRP[g][1]
                        n = 4 * t + g
                        w = min(P, M - P * cs[0])
                        dve.wait_ge(hi_done, 1 + (k0 + t) * NG + g + 1)
                        dve.tensor_tensor(ptl[0:w, cs[0]:cs[-1] + 1, :], pT[0:w, n % 2, 0:P * len(cs)].rearrange(
                            "p (c r) -> p c r", r=P), pth[0:w, cs[0]:cs[-1] + 1, :], ALU.subtract).then_inc(lo_done, 1)

                    def maxima(t, half):
                        a, z = (0, 2 * BANK) if half == 0 else (2 * BANK, M)
                        dve.wait_ge(s_done, 1 + (k0 + t) * 2 + half + 1)
                        dve.tensor_reduce(mx[:, half:half + 1], pS[:, a:z], AX_X, ALU.max, negate=True).then_inc(mx_done, 1)

                    for t in steps:
                        for half in range(2):
                            if least + 1 <= t <= T2:
                                low_probs(t - 1, half)
                            if t < T2:
                                maxima(t, half)
                        if t < T2:
                            dve.wait_ge(mx_done, 1 + (k0 + t + 1) * 2)
                            dve.tensor_scalar(nmax[:, t % 2:t % 2 + 1], mx[:, 0:1], mx[:, 1:2], SCALE, ALU.min,
                                              ALU.mult).then_inc(nmax_done, 1)
                        if least + 1 <= t <= T2:
                            low_probs(t - 1, 2)
                            low_probs(t - 1, 3)
                        if t >= least + 2:
                            par, p = (t - 2) // PAIRS, (t - 2) % PAIRS
                            ah, al = (m.quA[:, n, bass.ds(b + par, 1), p, :].rearrange("p o r -> p (o r)") for n in (0, 1))
                            bb = m.quB[64:128, bass.ds(b + par, 1), p, :].rearrange("p o r -> p (o r)")
                            dve.wait_ge(uhi_done, 1 + (k0 + t - 1) * 2)
                            dve.tensor_tensor(al, pV[:, 0, :], ah, ALU.subtract).then_inc(ulo_done, 1)
                            dve.tensor_tensor(bb, pV[64:128, 1, :], bb, ALU.subtract).then_inc(ulo_done, 1)
                        if least + 1 <= t <= T2:
                            s = (t - 1) % 2
                            dve.wait_ge(exp_done, 1 + k0 + t)
                            dve.reciprocal(rinv[:, s:s + 1], rsum[:, s:s + 1]).then_inc(rinv_done, 1)
                            dve.wait_ge(rinv_done, 1 + k0 + t)
                            dve.wait_ge(av_done, 1 + k0 + t)
                            dve.wait_ge(ut_done, 1 + (k0 + t - 1) * 2)
                            dve.tensor_scalar(u[:, 0:DC], pU[:, 0:DC], rinv[:, s:s + 1], None, ALU.mult).then_inc(u_done, 1)
                            dve.tensor_scalar(u[:, DC:D], pU[:, P:DC], rinv[:, s:s + 1], None, ALU.mult).then_inc(u_done, 1)

                bodies(dve, body)


def l0x_output(nc, m, d):
    with ExitStack() as ctx:
        sb, ps, sem = names(nc, ctx)
        wvh, wvl = (sb(n, [P, 2, 1024], BF16) for n in ("wv0h", "wv0l"))
        woh, wol = (sb(n, [P, PAIRS, D], BF16) for n in ("wo0h", "wo0l"))
        oh, ol = (sb(n, [P, PAIRS, TOK], BF16) for n in ("o0h", "o0l"))
        pO = ps("pO", [P, 2, BANK])
        pX = ps("pX", [P, TT, BANK])
        whi, wlo, o_mm, o_hi, o_lo, x_mm, x_done = (
            sem("o0_" + n) for n in ("whi", "wlo", "o_mm", "o_hi", "o_lo", "x_mm", "x_done"))
        with nc.Block() as block:
            @block.gpsimd
            def _(pool):
                one = m.small[0:96, SMALL["onehot"]:SMALL["onehot"] + H]
                pool.tensor_copy(m.onehot[:, :, :], one.unsqueeze(2).broadcast_to([96, H, P])).then_inc(m.onehot_made, 1)

            @block.tensor
            def _(pe):
                for p in range(PAIRS + 1):
                    if p < PAIRS:
                        if p == 0:
                            pe.wait_ge(wlo, 1)
                        if p >= 2:
                            pe.wait_ge(o_lo, p - 1)
                        ops = ((wvh, 0, 0), (wvh, 0, 1), (wvl, 0, 0), (wvh, 1, 2), (wvl, 1, 2))
                        for a, (w, part, q) in enumerate(ops):
                            for h in range(2):
                                s = slice(NQ * h, NQ * h + NQ)
                                mov = m.quB[:, :, p, s] if q == 2 else m.quA[:, q, :, p, s]
                                mm = pe.matmul(pO[64 * h:64 * h + 64, p % 2, :].rearrange("p (b i) -> p b i", b=B),
                                               w[:, part, P * p + 64 * h:P * p + 64 * h + 64], mov,
                                               start=(a == 0), stop=(a == 4))
                        mm.then_inc(o_mm, 1)
                    if p >= 1:
                        pe.wait_ge(o_lo, p)
                        if p == 1:
                            pe.wait_ge(wlo, 2)
                        for t in range(TT):
                            s = slice(P * t, P * t + P)
                            for a, (o, w) in enumerate(((oh, woh), (oh, wol), (ol, woh))):
                                pe.matmul(pX[:, t, 0:D], o[:, p - 1, s], w[:, p - 1, :],
                                          start=(p == 1 and a == 0), stop=False)
                for t in range(TT):
                    pe.matmul(pX[:, t, 0:D], m.ones_row, m.bo0[:, :], start=False, stop=True).then_inc(x_mm, 1)

            @block.scalar
            def _(act):
                act.wait_ge(m.w0_loaded, 48)
                act.activation(wvh[:, :, :], m.wv0[:, :, :], ACT.Copy).then_inc(whi, 1)
                act.activation(woh[:, :, :], m.wo0[:, :, :], ACT.Copy).then_inc(whi, 1)
                for p in range(PAIRS):
                    act.wait_ge(o_mm, p + 1)
                    act.activation(oh[:, p, :], pO[:, p % 2, :], ACT.Copy).then_inc(o_hi, 1)

            @block.vector
            def _(dve):
                dve.wait_ge(whi, 1)
                dve.tensor_tensor(wvl[:, :, :], m.wv0[:, :, :], wvh[:, :, :], ALU.subtract).then_inc(wlo, 1)
                dve.wait_ge(whi, 2)
                dve.tensor_tensor(wol[:, :, :], m.wo0[:, :, :], woh[:, :, :], ALU.subtract).then_inc(wlo, 1)
                for p in range(PAIRS):
                    dve.wait_ge(o_hi, p + 1)
                    dve.tensor_tensor(ol[:, p, :], pO[:, p % 2, :], oh[:, p, :], ALU.subtract).then_inc(o_lo, 1)
                for t in range(TT):
                    dve.wait_ge(x_mm, t + 1)
                    dve.tensor_tensor(m.x[:, t, :], m.x[:, t, :], pX[:, t, 0:D], ALU.add).then_inc(x_done, 1)


def project(nc, m, tag, srcT, w, bias_row, src=None):
    with ExitStack() as ctx:
        sb, ps, sem = names(nc, ctx)
        pX = ps(f"{tag}_pX", [P, TT, BANK])
        pT = ps(f"{tag}_pT", [P, KC, BANK])
        turned, copied, x_mm, x_done = (sem(f"{tag}_{n}") for n in ("turned", "copied", "x_mm", "x_done"))
        with nc.Block() as block:
            @block.tensor
            def _(pe):
                if src is not None:
                    for c in range(KC):
                        for t in range(TT):
                            pe.transpose(pT[:, c, P * t:P * t + P], src[:, t, P * c:P * c + P],
                                         m.ident[:, :]).then_inc(turned, 1)
                for c in range(KC):
                    if src is not None:
                        pe.wait_ge(copied, c + 1)
                    for t in range(TT):
                        mm = pe.matmul(pX[:, t, 0:D], srcT[:, c, P * t:P * t + P], w[:, c, :], start=(c == 0),
                                       stop=(c == KC - 1 and bias_row is None))
                        if c == KC - 1 and bias_row is not None:
                            mm = pe.matmul(pX[:, t, 0:D], m.ones_row, bias_row, start=False, stop=True)
                        if c == KC - 1:
                            mm.then_inc(x_mm, 1)

            if src is not None:
                @block.scalar
                def _(act):
                    for c in range(KC):
                        act.wait_ge(turned, TT * (c + 1))
                        act.activation(srcT[:, c, :], pT[:, c, :], ACT.Copy).then_inc(copied, 1)

            @block.vector
            def _(dve):
                for t in range(TT):
                    dve.wait_ge(x_mm, t + 1)
                    dve.tensor_tensor(m.x[:, t, :], m.x[:, t, :], pX[:, t, 0:D], ALU.add).then_inc(x_done, 1)


def heads16(nc, m, tag, qT, kT, vhl, o, gate, decay):
    with ExitStack() as ctx:
        sb, ps, sem = names(nc, ctx)
        R = 3
        qm = sb(f"{tag}_qm", [P, KC, 8, TOK])
        arg = sb(f"{tag}_arg", [P, 2, BANK])
        ex = sb(f"{tag}_ex", [P, 2, BANK])
        wt = sb(f"{tag}_wt", [P, R, BANK])
        wh = sb(f"{tag}_wh", [P, R, BANK], BF16)
        wl = sb(f"{tag}_wl", [P, R, BANK], BF16)
        o2 = sb(f"{tag}_o2", [P, TT, H, 16])
        pA = ps(f"{tag}_pA", [P, 2, BANK])
        pD = ps(f"{tag}_pD", [P, 2, BANK])
        pO = ps(f"{tag}_pO", [P, TT, H, 32])
        qm_dve, qm_act, a_mm, d_mm, arg_done, ex_done, wt_done, wh_done, wl_done, av_mm, o2_done, o_done, gated = (
            sem(f"{tag}_{n}") for n in ("qm_dve", "qm_act", "a_mm", "d_mm", "arg_done", "ex_done", "wt_done",
                                        "wh_done", "wl_done", "av_mm", "o2_done", "o_done", "gated"))
        LAG = 2
        LATER = LAG + 1
        G = 4 * TT
        hmask = m.small[:, SMALL["hmask"]:SMALL["hmask"] + 8]
        with nc.Block() as block:
            @block.tensor
            def _(pe):
                for g in range(G + LAG):
                    if g < G:
                        t, q = g // 4, g % 4
                        s = slice(P * t, P * t + P)
                        if g < 4:
                            pe.wait_ge(qm_dve if g < 2 else qm_act, 4 * (g % 2) + 4)
                        if decay is not None:
                            if g >= 2:
                                pe.wait_ge(arg_done, g - 1)
                            F, nF = decay
                            pe.matmul(pD[:, g % 2, :], nF[:, s], m.late["onehot"][:, 4 * q:4 * q + 4, :].rearrange(
                                "p h r -> p (h r)"), start=True, stop=False)
                            for h in range(4):
                                mm = pe.matmul(pD[:, g % 2, P * h:P * h + P], m.late["onehot"][:, 4 * q + h, :], F[:, s],
                                               start=False, stop=(h == 3))
                            mm.then_inc(d_mm, 1)
                        if g >= 2:
                            pe.wait_ge(wt_done if decay is not None else ex_done, g - 1)
                        c = q // 2
                        pe.matmul(pA[:, g % 2, :].rearrange("p (h r) -> p h r", h=4), kT[:, c, s],
                                  qm[:, c, 4 * (q % 2):4 * (q % 2) + 4, s], start=True, stop=True).then_inc(a_mm, 1)
                    if g >= LAG:
                        v = g - LAG
                        t, q = v // 4, v % 4
                        pe.wait_ge(wh_done, v + 1)
                        pe.wait_ge(wl_done, v + 1)
                        for h in range(4):
                            n, s = 4 * q + h, slice(P * h, P * h + P)
                            pe.matmul(pO[:, t, n, :], wh[:, v % R, s], vhl[:, t, n, :], start=True, stop=False)
                            mm = pe.matmul(pO[:, t, n, 0:16], wl[:, v % R, s], vhl[:, t, n, 0:16],
                                           start=False, stop=True)
                        mm.then_inc(av_mm, 1)

            @block.scalar
            def _(act):
                def cast(g):
                    act.wait_ge(wt_done, g + 1)
                    if g >= R:
                        act.wait_ge(av_mm, g - R + 1)
                    act.activation(wh[:, g % R, :], wt[:, g % R, :], ACT.Copy).then_inc(wh_done, 1)

                def finish(t):
                    act.wait_ge(av_mm, 4 * (t + 1))
                    act.activation(o2[:, t, :, :], pO[:, t, :, 16:32], ACT.Copy).then_inc(o2_done, 1)

                for n in range(8):
                    act.activation(qm[:, 1, n, :], qT[:, 1, :], ACT.Copy, scale=hmask[:, n:n + 1]).then_inc(qm_act, 1)
                for g in range(G):
                    if decay is not None:
                        act.wait_ge(arg_done, g + 1)
                        if g >= 2:
                            act.wait_ge(wt_done, g - 1)
                        act.activation(ex[:, g % 2, :], arg[:, g % 2, :], ACT.Exp).then_inc(ex_done, 1)
                    else:
                        act.wait_ge(a_mm, g + 1)
                        if g >= 2:
                            act.wait_ge(wt_done, g - 1)
                        act.activation(ex[:, g % 2, :], pA[:, g % 2, :], ACT.Tanh, bias=m.tanh_bias,
                                       scale=15.0).then_inc(ex_done, 1)
                    if g >= 1:
                        cast(g - 1)
                    if g > LATER and (g - LATER) % 4 == 0:
                        finish((g - LATER) // 4 - 1)
                cast(G - 1)
                for t in range((G - 1 - LATER) // 4, TT):
                    finish(t)

            @block.vector
            def _(dve):
                def finish(t):
                    o4 = o[:, t, :].rearrange("p (h e) -> p h e", h=H)
                    dve.wait_ge(o2_done, t + 1)
                    dve.tensor_tensor(o4, pO[:, t, :, 0:16], o2[:, t, :, :], ALU.add).then_inc(o_done, 1)
                    dve.wait_ge(o_done, t + 1)
                    dve.tensor_tensor(o4, o4, gate(t), ALU.mult).then_inc(gated, 1)

                for n in range(8):
                    dve.tensor_scalar(qm[:, 0, n, :], qT[:, 0, :], hmask[:, n:n + 1], None, ALU.mult).then_inc(qm_dve, 1)
                for g in range(G + 1):
                    if decay is not None and g < G:
                        dve.wait_ge(d_mm, g + 1)
                        if g >= 2:
                            dve.wait_ge(ex_done, g - 1)
                        dve.tensor_tensor(arg[:, g % 2, :], pD[:, g % 2, :], m.maskneg[:, :], ALU.min).then_inc(arg_done, 1)
                    if g >= 1:
                        r, k = (g - 1) % 2, (g - 1) % R
                        dve.wait_ge(ex_done, g)
                        if g > R:
                            dve.wait_ge(wl_done, g - R)
                            dve.wait_ge(wh_done, g - R)
                        if decay is not None:
                            dve.wait_ge(a_mm, g)
                            dve.tensor_tensor(wt[:, k, :], pA[:, r, :], ex[:, r, :], ALU.mult).then_inc(wt_done, 1)
                        else:
                            dve.scalar_tensor_tensor(wt[:, k, :], ex[:, r, :], 1.0, m.mask05[:, :], ALU.add,
                                                     ALU.mult).then_inc(wt_done, 1)
                    if g > LATER and (g - LATER) % 4 == 0:
                        finish((g - LATER) // 4 - 1)
                for t in range((G - LATER) // 4, TT):
                    finish(t)

            @block.gpsimd
            def _(pool):
                for g in range(G):
                    pool.wait_ge(wh_done, g + 1)
                    if g >= R:
                        pool.wait_ge(av_mm, g - R + 1)
                    pool.tensor_tensor(wl[:, g % R, :], wt[:, g % R, :], wh[:, g % R, :], ALU.subtract).then_inc(wl_done, 1)


def l0_gla(nc, m, d):
    with ExitStack() as ctx:
        sb, ps, sem = names(nc, ctx)
        qT = sb("gl_qT", [P, KC, TOK])
        kv = sb("gl_kv", [P, TT, 2 * D])
        sq = sb("gl_sq", [P, TT, D])
        ssq = sb("gl_ssq", [P, TT, H])
        nrm = sb("gl_nrm", [P, TT, H])
        inv = sb("gl_inv", [P, TT, H])
        kn = sb("gl_kn", [P, TT, D])
        kT = sb("gl_kT", [P, KC, TOK])
        vhl = sb("gl_vhl", [P, TT, H, 32], BF16)
        g1 = sb("gl_g1", [16, TOK])
        gate = sb("gl_gate", [P, TT, D])
        o = sb("gl_o", [P, TT, D])
        F = sb("gl_F", [96, TOK], BF16)
        nF = sb("gl_nF", [96, TOK], BF16)
        with ExitStack() as c2:
            sb2, ps2, sem2 = names(nc, c2)
            fa = sb2("gl_fa", [96, TOK])
            fe = sb2("gl_fe", [96, TOK])
            fl = sb2("gl_fl", [96, TOK])
            fs = sb2("gl_fs", [96, TOK])
            fc = sb2("gl_fc", [96, TOK])
            fr = sb2("gl_fr", [96, TOK])
            f1 = sb2("gl_f1", [96, TOK], BF16)
            pq = ps2("gl_pq", [P, KC, BANK])
            pkv = ps2("gl_pkv", [P, TT, BANK])
            pf = ps2("gl_pf", [P, BANK])
            pg = ps2("gl_pg", [P, BANK])
            (q_mm, kv_mm, f_mm, g1_mm, q_done, kv_done, fabs, fexp, fln, g1_done, gt_mm, gate_done, sq_done, ssq_done,
             nrm_done, inv_done, kn_done, kt_mm, kt_done, fchain, v_hi, v_lo) = (sem2("gl_" + n) for n in (
                 "q_mm", "kv_mm", "f_mm", "g1_mm", "q_done", "kv_done", "fabs", "fexp", "fln", "g1_done", "gt_mm",
                 "gate_done", "sq_done", "ssq_done", "nrm_done", "inv_done", "kn_done", "kt_mm", "kt_done", "fchain",
                 "v_hi", "v_lo"))
            with nc.Block() as block:
                @block.tensor
                def _(pe):
                    pe.wait_ge(m.late_loaded, m.late_n)
                    for c in range(KC):
                        mm = pe.matmul(pf[0:96, :], m.late["gl_wf"][:, c, :], m.xnT[:, c, :], start=(c == 0), stop=(c == KC - 1))
                    mm.then_inc(f_mm, 1)
                    for c in range(KC):
                        mm = pe.matmul(pg[0:16, :], m.late["gl_g1"][:, c, :], m.xnT[:, c, :], start=(c == 0), stop=(c == KC - 1))
                    mm.then_inc(g1_mm, 1)
                    for t in range(TT):
                        for c in range(KC):
                            mm = pe.matmul(pkv[:, t, :], m.xnT[:, c, P * t:P * t + P], m.late["gl_wkv"][:, c, :],
                                           start=(c == 0), stop=(c == KC - 1))
                        mm.then_inc(kv_mm, 1)
                    for n in range(KC):
                        for c in range(KC):
                            mm = pe.matmul(pq[:, n, :], m.late["gl_wq"][:, c, P * n:P * n + P], m.xnT[:, c, :],
                                           start=(c == 0), stop=(c == KC - 1))
                        mm.then_inc(q_mm, 1)
                    pe.wait_ge(g1_done, 1)
                    pe.wait_ge(q_done, 2)
                    for t in range(TT):
                        pe.matmul(pq[:, t // 2, D * (t % 2):D * (t % 2) + D], g1[:, P * t:P * t + P], m.late["gl_g2"][:, :],
                                  start=True, stop=True).then_inc(gt_mm, 1)
                    pe.wait_ge(kn_done, 1)
                    for c in range(KC):
                        for t in range(TT):
                            mm = pe.transpose(pkv[:, c, P * t:P * t + P], kn[:, t, P * c:P * c + P], m.ident[:, :])
                        mm.then_inc(kt_mm, 1)

                @block.scalar
                def _(act):
                    act.wait_ge(f_mm, 1)
                    act.activation(fa[:, :], pf[0:96, :], ACT.Abs).then_inc(fabs, 1)
                    act.wait_ge(fabs, 1)
                    act.activation(fe[:, :], fa[:, :], ACT.Exp, scale=-1.0).then_inc(fexp, 1)
                    act.wait_ge(fexp, 1)
                    act.activation(fl[:, :], fe[:, :], ACT.Ln, bias=m.one[0:96, :]).then_inc(fln, 1)
                    act.wait_ge(g1_mm, 1)
                    act.activation(g1[:, :], pg[0:16, :], ACT.Copy).then_inc(g1_done, 1)
                    for t in range(TT):
                        act.wait_ge(kv_mm, t + 1)
                        act.activation(kv[:, t, :], pkv[:, t, :], ACT.Silu).then_inc(kv_done, 1)
                    for n in range(KC):
                        act.wait_ge(q_mm, n + 1)
                        act.activation(qT[:, n, :], pq[:, n, :], ACT.Silu).then_inc(q_done, 1)
                    act.wait_ge(ssq_done, 1)
                    act.activation(nrm[:, :, :], ssq[:, :, :], ACT.Sqrt).then_inc(nrm_done, 1)
                    act.wait_ge(gt_mm, TT)
                    for n in range(2):
                        act.activation(gate[:, 2 * n:2 * n + 2, :], pq[:, n, :].rearrange("p (t f) -> p t f", t=2),
                                       ACT.Sigmoid).then_inc(gate_done, 1)
                    act.wait_ge(kt_mm, 1)
                    act.activation(kT[:, 0, :], pkv[:, 0, :], ACT.Copy).then_inc(kt_done, 1)

                @block.vector
                def _(dve):
                    k4 = kv[:, :, 0:D]
                    dve.wait_ge(fln, 1)
                    link = chained(dve, fchain)
                    link(dve.scalar_tensor_tensor(fs[:, :], pf[0:96, :], 0.0, fl[:, :], ALU.min, ALU.subtract))
                    link(dve.tensor_tensor_scan(fc[:, :], m.late["scanmask"][0:96, :], fs[:, :], 0.0, ALU.mult, ALU.add))
                    link(dve.tensor_copy(f1[:, :], fc[:, :]))
                    link(dve.tensor_tensor(fr[:, :], fc[:, :], f1[:, :], ALU.subtract))
                    link(dve.tensor_copy(F[:, :], fr[:, :]))
                    link(dve.tensor_tensor(fa[:, :], fr[:, :], F[:, :], ALU.subtract))
                    link(dve.tensor_copy(F[0:32, :], f1[0:32, :]))
                    link(dve.tensor_copy(F[64:96, :], fa[64:96, :]))
                    link(dve.tensor_scalar(nF[:, :], F[:, :], -1.0, None, ALU.mult))
                    dve.wait_ge(kv_done, TT)
                    dve.tensor_tensor(sq[:, :, :], k4, k4, ALU.mult).then_inc(sq_done, 1)
                    dve.wait_ge(sq_done, 1)
                    dve.tensor_reduce(ssq[:, :, :], sq[:, :, :].rearrange("p t (h e) -> p t h e", h=H), AX_X,
                                      ALU.add).then_inc(ssq_done, 1)
                    dve.wait_ge(nrm_done, 1)
                    dve.tensor_scalar(nrm[:, :, :], nrm[:, :, :], 1e-12, None, ALU.max).then_inc(inv_done, 1)
                    dve.wait_ge(inv_done, 1)
                    dve.reciprocal(inv[:, :, :], nrm[:, :, :]).then_inc(inv_done, 1)
                    dve.wait_ge(inv_done, 2)
                    dve.tensor_tensor(kn[:, :, :].rearrange("p t (h e) -> p t h e", h=H),
                                      k4.rearrange("p t (h e) -> p t h e", h=H),
                                      inv[:, :, :].unsqueeze(3).broadcast_to([P, TT, H, 16]), ALU.mult).then_inc(kn_done, 1)
                    dve.wait_ge(kt_mm, 2)
                    dve.tensor_copy(kT[:, 1, :], pkv[:, 1, :]).then_inc(kt_done, 1)

                @block.gpsimd
                def _(pool):
                    v4 = kv[:, :, D:2 * D].rearrange("p t (h e) -> p t h e", h=H)
                    pool.wait_ge(kv_done, TT)
                    for t in range(TT):
                        pool.tensor_copy(vhl[:, t, :, 0:16], v4[:, t]).then_inc(v_hi, 1)
                    for t in range(TT):
                        pool.wait_ge(v_hi, t + 1)
                        pool.tensor_tensor(vhl[:, t, :, 16:32], v4[:, t], vhl[:, t, :, 0:16], ALU.subtract).then_inc(v_lo, 1)
        heads16(nc, m, "gh", qT, kT, vhl, o, lambda t: gate[:, t, :].rearrange("p (h e) -> p h e", h=H), (F, nF))
        layer_norm(nc, m, "lng", o, kn, kT, (m.late["gl_lnw"][:, :], None))
        project(nc, m, "gp", kT, m.late["gl_wo"], None)


def l0_moe(nc, m, d):
    with ExitStack() as ctx:
        sb, ps, sem = names(nc, ctx)
        mask = sb("mo_mask", [P, TT, E])
        xs = sb("mo_xs", [P, TT, D])
        xsT = sb("mo_xsT", [P, KC, TOK])
        with ExitStack() as c2:
            sb2, ps2, sem2 = names(nc, c2)
            lg = sb2("mo_lg", [P, TT, E])
            top = sb2("mo_top", [P, TT])
            rw = sb2("mo_rw", [P, TT])
            eq = sb2("mo_eq", [P, TT, E])
            cand = sb2("mo_cand", [P, TT, E])
            best = sb2("mo_best", [P, TT])
            pL = ps2("mo_pL", [P, TT * E])
            pT = ps2("mo_pT", [P, KC, BANK])
            l_mm, chain, rw_done, xs_done, turned, copied = (
                sem2("mo_" + n) for n in ("l_mm", "chain", "rw_done", "xs_done", "turned", "copied"))
            with nc.Block() as block:
                @block.tensor
                def _(pe):
                    pe.wait_ge(m.late_loaded, m.late_n)
                    for t in range(TT):
                        for c in range(KC):
                            mm = pe.matmul(pL[:, E * t:E * t + E], m.xnT[:, c, P * t:P * t + P], m.late["mo_gate"][:, c, :],
                                           start=(c == 0), stop=(c == KC - 1))
                    mm.then_inc(l_mm, 1)
                    pe.wait_ge(xs_done, TT)
                    for c in range(KC):
                        for t in range(TT):
                            mm = pe.transpose(pT[:, c, P * t:P * t + P], xs[:, t, P * c:P * c + P], m.ident[:, :])
                        mm.then_inc(turned, 1)

                @block.scalar
                def _(act):
                    act.wait_ge(chain, 2)
                    act.activation(rw[:, :], top[:, :], ACT.Sigmoid).then_inc(rw_done, 1)
                    act.wait_ge(turned, 1)
                    act.activation(xsT[:, 0, :], pT[:, 0, :], ACT.Copy).then_inc(copied, 1)

                @block.vector
                def _(dve):
                    dve.wait_ge(l_mm, 1)
                    def wide(a):
                        return a[:, :].unsqueeze(2).broadcast_to([P, TT, E])
                    desc = m.small[:, SMALL["desc"]:SMALL["desc"] + E].unsqueeze(1).broadcast_to([P, TT, E])
                    link = chained(dve, chain)
                    link(dve.tensor_copy(lg[:, :, :], pL[:, :].rearrange("p (t e) -> p t e", e=E)))
                    link(dve.tensor_reduce(top[:, :], lg[:, :, :], AX_X, ALU.max))
                    link(dve.tensor_tensor(eq[:, :, :], lg[:, :, :], wide(top), ALU.is_equal))
                    link(dve.tensor_tensor(cand[:, :, :], eq[:, :, :], desc, ALU.mult))
                    link(dve.tensor_reduce(best[:, :], cand[:, :, :], AX_X, ALU.max))
                    link(dve.tensor_tensor(mask[:, :, :], cand[:, :, :], wide(best), ALU.is_equal))
                    dve.wait_ge(rw_done, 1)
                    for t in range(TT):
                        dve.tensor_scalar(xs[:, t, :], m.xn[:, t, :], rw[:, t:t + 1], None, ALU.mult).then_inc(xs_done, 1)
                    dve.wait_ge(turned, 2)
                    dve.tensor_copy(xsT[:, 1, :], pT[:, 1, :]).then_inc(copied, 1)
        sg = sb("mo_sg", [P, 2, TOK])
        hT = sb("mo_hT", [P, 2, TOK])
        pG = ps("mo_pG", [P, 2, BANK])
        pU = ps("mo_pU", [P, 2, BANK])
        pD = ps("mo_pD", [P, TT, BANK])
        g_mm, u_mm, sg_done, h_done, d_mm, x_done = (
            sem("mo_" + n) for n in ("g_mm", "u_mm", "sg_done", "h_done", "d_mm", "x_done"))
        with nc.Block() as block:
            @block.tensor
            def _(pe):
                for e in range(E + 1):
                    if e < E:
                        if e >= 2:
                            pe.wait_ge(h_done, e - 1)
                        for w, o, s in ((m.late["mo_wg"], pG, g_mm), (m.late["mo_wu"], pU, u_mm)):
                            for c in range(KC):
                                mm = pe.matmul(o[:, e % 2, :], w[:, e, c, :], xsT[:, c, :], start=(c == 0),
                                               stop=(c == KC - 1))
                            mm.then_inc(s, 1)
                    if e >= 1:
                        pe.wait_ge(h_done, e)
                        for t in range(TT):
                            if e >= 2:
                                pe.wait_ge(x_done, TT * (e - 2) + t + 1)
                            pe.matmul(pD[:, t, 0:D], hT[:, (e - 1) % 2, P * t:P * t + P], m.late["mo_wd"][:, e - 1, :],
                                      start=True, stop=True).then_inc(d_mm, 1)

            @block.scalar
            def _(act):
                for e in range(E):
                    act.wait_ge(g_mm, e + 1)
                    if e >= 2:
                        act.wait_ge(h_done, e - 1)
                    act.activation(sg[:, e % 2, :], pG[:, e % 2, :], ACT.Silu).then_inc(sg_done, 1)

            @block.vector
            def _(dve):
                for e in range(E + 1):
                    if e < E:
                        dve.wait_ge(u_mm, e + 1)
                        dve.wait_ge(sg_done, e + 1)
                        if e >= 2:
                            dve.wait_ge(d_mm, TT * (e - 1))
                        dve.tensor_tensor(hT[:, e % 2, :], pU[:, e % 2, :], sg[:, e % 2, :], ALU.mult).then_inc(h_done, 1)
                    if e >= 1:
                        for t in range(TT):
                            n = TT * (e - 1) + t
                            dve.wait_ge(d_mm, n + 1)
                            if e >= 2:
                                dve.wait_ge(x_done, n - TT + 1)
                            dve.scalar_tensor_tensor(m.x[:, t, :], pD[:, t, 0:D], mask[:, t, e - 1:e], m.x[:, t, :],
                                                     ALU.mult, ALU.add).then_inc(x_done, 1)


NSPLIT = 4


def load_context(sp, d, stA, stB, b, ctx_in):
    sp.dma_start(stA[:, :], d["ctxT"][bass.ds(b, 1), 0:P].rearrange("o p c -> (o p) c")).then_inc(ctx_in, 16)
    for s in (0, 64):
        sp.dma_start(stB[s:s + 64, :], d["ctxT"][bass.ds(b, 1), P:DC].rearrange("o p c -> (o p) c")).then_inc(ctx_in, 16)


def split_context(pool, b, o, stA, stB, ctx_in, begun, split):
    pool.wait_ge(ctx_in, (b + 1) * 48)
    pool.sem_inc(begun, 1)
    parts = ((o.ah[:, 0:M], o.al[:, 0:M], stA[:, :]), (o.bh[:, 0:M], o.bl[:, 0:M], stB[:, :]))
    for hi, _, src in parts:
        pool.tensor_copy(hi, src).then_inc(split, 1)
    for n, (hi, lo, src) in enumerate(parts):
        pool.wait_ge(split, 1 + b * NSPLIT + n + 1)
        pool.tensor_tensor(lo, src, hi, ALU.subtract).then_inc(split, 1)


def l1x_tiles(nc, m, d, c0, qbh, qbl, wh, wl, wB, oT):
    SCALE = 16 ** -0.5
    T2 = 2 * PAIRS
    with ExitStack() as ctx:
        sb, ps, sem = names(nc, ctx)
        stA, stB, hl, ctx_in, begun, split = c0
        kh, kl = ([sb(f"x1_{n}{par}", [P, KC, M + 1], BF16) for par in range(2)] for n in ("kh", "kl"))
        vhl = [sb(f"x1_vhl{par}", [P, MC, PAIRS, 64], BF16) for par in range(2)]
        prob = sb("x1_prob", [P, 2, M])
        pth = sb("x1_pth", [P, 2, MC, P], BF16)
        ptl = sb("x1_ptl", [P, 2, MC, P], BF16)
        mx = sb("x1_mx", [P, 2])
        nmax = sb("x1_nmax", [P, 2])
        rsum = sb("x1_rsum", [P, 2])
        rinv = sb("x1_rinv", [P, 2])
        u = sb("x1_u", [P, 2, 2, PAIRS, 32])
        pS = ps("x1_pS", [P, 4 * BANK])
        pT = ps("x1_pT", [P, 2, BANK])
        pK = ps("x1_pK", [P, BANK])
        pUF = ps("x1_pUF", [P, BANK])
        pU = pUF[:, 0:64]
        pF = pUF[:, 64:64 + KC * NQ].rearrange("p (n i) -> p n i", n=KC)
        (kv_mm, kv_hi, kv_lo, s_done, exp_done, t_done, hi_done, lo_done, av_done,
         mx_done, nmax_done, rinv_done, u_done, f_mm, f_done) = (sem("x1_" + n) for n in (
             "kv_mm", "kv_hi", "kv_lo", "s_done", "exp_done", "t_done",
             "hi_done", "lo_done", "av_done", "mx_done", "nmax_done", "rinv_done", "u_done", "f_mm", "f_done"))
        VG = [range(2 * n, min(2 * n + 2, MC)) for n in range(-(-MC // 2))]
        PIECES = [("k", n, j) for n in range(KC) for j in range(len(SEG))] + [("v", n, cs) for n, cs in enumerate(VG)]
        NP = len(PIECES)
        NKP = KC * len(SEG)
        rowmask = m.small[:, SMALL["rowmask"]:SMALL["rowmask"] + 64].rearrange("p (a c) -> p a c", a=2)
        fold = m.small[:, SMALL["fold"]:SMALL["fold"] + NQ]

        def beside(t, half):
            i = 2 * (t % PAIRS) + half
            return i if 0 <= t < T2 and i < NP else None

        def bodies(eng, body):
            body(0, True, False)
            with eng.Fori(1, B // 2 - 1) as i:
                body(i * 2, False, False)
            body(B - 2, False, True)

        with nc.Block() as block:
            @block.sync
            def _(sp):
                with sp.Fori(1, B) as b:
                    sp.wait_ge(split, 1 + b * NSPLIT)
                    load_context(sp, d, stA, stB, b, ctx_in)

            @block.gpsimd
            def _(pool):
                split_context(pool, 1, hl[1], stA, stB, ctx_in, begun, split)
                with pool.Fori(1, B // 2) as i:
                    b = i * 2
                    for par in range(2):
                        pool.wait_ge(kv_mm, 1 + (b + par - 1) * NP)
                        split_context(pool, b + par, hl[par], stA, stB, ctx_in, begun, split)

            @block.tensor
            def _(pe):
                for s in (s_done, t_done, av_done, kv_mm, f_mm):
                    pe.sem_inc(s, 1)

                def piece(b, par, i, dst, ahead):
                    c = hl[par]
                    if i == 0:
                        pe.wait_ge(split, 1 + (b + 1) * NSPLIT)
                    pe.wait_ge(kv_lo, 1 + b * NP + max(i - ahead, 0))
                    kind, n, x = PIECES[i]
                    if kind == "k":
                        w = slice(P * n, P * n + P)
                        s, z = SEG[x]
                        for a, (st, mv) in enumerate(((wh[:, 0, w], c.ah), (wh[:, 0, w], c.al), (wl[:, 0, w], c.ah),
                                                      (wB[:, w], c.bh), (wB[:, w], c.bl))):
                            mm = pe.matmul(dst[:, 0:z], st, mv[:, s:s + z], start=(a == 0), stop=(a == 4))
                    else:
                        w = slice(D, 2 * D)
                        for ch in x:
                            r = min(P, M - P * ch)
                            s = slice(P * ch, P * ch + r)
                            o = dst[0:r, D * (ch % 2):D * (ch % 2) + D]
                            for a, (st, mv) in enumerate(((c.ah, wh[:, 0, w]), (c.ah, wl[:, 0, w]), (c.al, wh[:, 0, w]),
                                                          (c.bh, wB[:, w]), (c.bl, wB[:, w]))):
                                mm = pe.matmul(o, st[:, s], mv, start=(a == 0), stop=(a == 4))
                    mm.then_inc(kv_mm, 1)

                def body(b, first, last):
                    k0 = b * PAIRS
                    least = 0 if first else -9

                    def scores(t, j):
                        par, p = t // PAIRS, t % PAIRS
                        s, w = SEG[j]
                        q = [a[:, bass.ds(b + par, 1), p, :].rearrange("p o r -> p (o r)") for a in (qbh, qbl)]
                        if j == 0:
                            pe.wait_ge(exp_done, 1 + k0 + t)
                            if p == 0:
                                pe.wait_ge(kv_lo, 1 + (b + par) * NP + NKP)
                        for a, (st, mv) in enumerate(((q[0], kh), (q[0], kl), (q[1], kh))):
                            mm = pe.matmul(pS[:, s:s + w], st, mv[par % 2][:, p // 4, s:s + w], start=(a == 0), stop=(a == 2))
                        if j in (1, 3):
                            mm.then_inc(s_done, 1)

                    def turn_probs(t, g):
                        n = 4 * t + g
                        if g == 0:
                            pe.wait_ge(exp_done, 1 + k0 + t + 1)
                        pe.wait_ge(lo_done, 1 + k0 * NG + max(n - 1, least))
                        for ch in TGRP[g][1]:
                            w = min(P, M - P * ch)
                            mm = pe.transpose(pT[0:w, n % 2, P * (ch % 4):P * (ch % 4) + P], prob[:, t % 2, P * ch:P * ch + w],
                                              m.ident[:, :])
                        mm.then_inc(t_done, 1)

                    def values(t):
                        par, p = t // PAIRS, t % PAIRS
                        pe.wait_ge(u_done, 1 + k0 + t)
                        pe.wait_ge(lo_done, 1 + (k0 + t + 1) * NG)
                        if p == 0:
                            pe.wait_ge(kv_lo, 1 + (b + par + 1) * NP)
                            pe.wait_ge(f_done, 1 + (b + par) * KC)
                        for n in range(MC):
                            w = min(P, M - P * n)
                            pe.matmul(pU, pth[0:w, t % 2, n, :], vhl[par % 2][0:w, n, p, :], start=(n == 0), stop=False)
                            mm = pe.matmul(pU[:, 0:32], ptl[0:w, t % 2, n, :], vhl[par % 2][0:w, n, p, 0:32], start=False,
                                           stop=(n == MC - 1))
                        mm.then_inc(av_done, 1)

                    def fold_rows(par):
                        pe.wait_ge(u_done, 1 + k0 + (par + 1) * PAIRS)
                        for n in range(KC):
                            for a in range(2):
                                mm = pe.matmul(pF[:, n, :], u[:, par % 2, a, 4 * n:4 * n + 4, :].rearrange("p a c -> p (a c)"), fold,
                                               start=(a == 0), stop=(a == 1))
                        mm.then_inc(f_mm, 1)

                    def beside_piece(t, half):
                        i = beside(t, half)
                        par = t // PAIRS
                        if i is not None and not (last and par):
                            piece(b + par + 1, 1 - par, i, pK, 0)

                    for t in range(T2 + 3 if last else T2):
                        for j in range(4):
                            if t < T2:
                                scores(t, j)
                            if j == 1:
                                beside_piece(t - 1, 1)
                        if t - 3 >= least and (t - 3) % PAIRS == PAIRS - 1:
                            fold_rows((t - 3) // PAIRS)
                        if least + 1 <= t <= T2:
                            turn_probs(t - 1, 0)
                            turn_probs(t - 1, 1)
                        beside_piece(t, 0)
                        if least + 1 <= t <= T2:
                            turn_probs(t - 1, 2)
                        if least + 2 <= t <= T2 + 1:
                            values(t - 2)
                        if least + 1 <= t <= T2:
                            turn_probs(t - 1, 3)

                for i in range(NP):
                    piece(0, 0, i, pS[:, BANK * (i % 4):BANK * (i % 4) + BANK], 3)
                pe.wait_ge(kv_lo, 1 + NP)
                bodies(pe, body)

            @block.scalar
            def _(act):
                for s in (exp_done, hi_done, kv_hi, f_done):
                    act.sem_inc(s, 1)

                def piece(b, par, i, src):
                    act.wait_ge(kv_mm, 1 + b * NP + i + 1)
                    kind, n, x = PIECES[i]
                    if kind == "k":
                        s, z = SEG[x]
                        act.activation(kh[par][:, n, s:s + z], src[:, 0:z], ACT.Identity,
                                       bias=m.late["x1_bk"][:, n:n + 1]).then_inc(kv_hi, 1)
                    else:
                        r = min(P, M - P * x[0])
                        act.activation(vhl[par][0:r, x[0]:x[-1] + 1, :, 0:32], src[0:r, 0:D * len(x)].rearrange(
                            "p (c a e) -> p c a e", a=PAIRS, e=32), ACT.Copy).then_inc(kv_hi, 1)

                def body(b, first, last):
                    k0 = b * PAIRS
                    least = 0 if first else -9

                    def high_probs(t, g):
                        cs = TGRP[g][1]
                        n = 4 * t + g
                        w = min(P, M - P * cs[0])
                        if g == 0:
                            act.wait_ge(av_done, 1 + k0 + max(t - 1, least))
                        act.wait_ge(t_done, 1 + (k0 + t) * NG + g + 1)
                        act.activation(pth[0:w, t % 2, cs[0]:cs[-1] + 1, :], pT[0:w, n % 2, 0:P * len(cs)].rearrange(
                            "p (c r) -> p c r", r=P), ACT.Copy).then_inc(hi_done, 1)

                    def beside_piece(t, half):
                        i = beside(t, half)
                        par = t // PAIRS
                        if i is not None and not (last and par):
                            if i == NKP:
                                act.wait_ge(av_done, 1 + k0 + par * PAIRS)
                            piece(b + par + 1, 1 - par, i, pK)

                    for t in range(T2 + 3 if last else T2):
                        beside_piece(t - 1, 1)
                        if least + 1 <= t <= T2:
                            high_probs(t - 1, 0)
                            high_probs(t - 1, 1)
                        if t < T2:
                            act.wait_ge(nmax_done, 1 + k0 + t + 1)
                            act.wait_ge(t_done, 1 + (k0 + max(t - 1, least)) * NG)
                            act.wait_ge(rinv_done, 1 + k0 + max(t - 1, least))
                            act.activation(prob[:, t % 2, :], pS[:, 0:M], ACT.Exp, bias=nmax[:, t % 2:t % 2 + 1], scale=SCALE,
                                           accum_out=rsum[:, t % 2:t % 2 + 1]).then_inc(exp_done, 1)
                        if t - 3 >= least and (t - 3) % PAIRS == PAIRS - 1:
                            par = (t - 3) // PAIRS
                            act.wait_ge(f_mm, 1 + b + par + 1)
                            for n in range(KC):
                                act.activation(oT[:, n, bass.ds((b + par) * NQ, NQ)], pF[:, n, :], ACT.Identity,
                                               bias=m.late["x1_bv"][:, n:n + 1]).then_inc(f_done, 1)
                        beside_piece(t, 0)
                        if least + 1 <= t <= T2:
                            high_probs(t - 1, 2)
                            high_probs(t - 1, 3)

                for i in range(NP):
                    piece(0, 0, i, pS[:, BANK * (i % 4):BANK * (i % 4) + BANK])
                bodies(act, body)

            @block.vector
            def _(dve):
                for s in (lo_done, mx_done, nmax_done, rinv_done, u_done, kv_lo):
                    dve.sem_inc(s, 1)

                def piece(b, par, i, src):
                    dve.wait_ge(kv_hi, 1 + b * NP + i + 1)
                    kind, n, x = PIECES[i]
                    if kind == "k":
                        s, z = SEG[x]
                        dve.scalar_tensor_tensor(kl[par][:, n, s:s + z], src[:, 0:z], m.late["x1_bk"][:, n:n + 1],
                                                 kh[par][:, n, s:s + z], ALU.add, ALU.subtract).then_inc(kv_lo, 1)
                    else:
                        r = min(P, M - P * x[0])
                        v = vhl[par][0:r, x[0]:x[-1] + 1, :, :]
                        dve.tensor_tensor(v[:, :, :, 32:64], src[0:r, 0:D * len(x)].rearrange(
                            "p (c a e) -> p c a e", a=PAIRS, e=32), v[:, :, :, 0:32], ALU.subtract).then_inc(kv_lo, 1)

                def body(b, first, last):
                    k0 = b * PAIRS
                    least = 0 if first else -9

                    def low_probs(t, g):
                        cs = TGRP[g][1]
                        n = 4 * t + g
                        w = min(P, M - P * cs[0])
                        dve.wait_ge(hi_done, 1 + (k0 + t) * NG + g + 1)
                        dve.tensor_tensor(ptl[0:w, t % 2, cs[0]:cs[-1] + 1, :], pT[0:w, n % 2, 0:P * len(cs)].rearrange(
                            "p (c r) -> p c r", r=P), pth[0:w, t % 2, cs[0]:cs[-1] + 1, :], ALU.subtract).then_inc(lo_done, 1)

                    def maxima(t, half):
                        a, z = (0, 2 * BANK) if half == 0 else (2 * BANK, M)
                        dve.wait_ge(s_done, 1 + (k0 + t) * 2 + half + 1)
                        dve.tensor_reduce(mx[:, half:half + 1], pS[:, a:z], AX_X, ALU.max, negate=True).then_inc(mx_done, 1)

                    def beside_piece(t, half):
                        i = beside(t, half)
                        par = t // PAIRS
                        if i is not None and not (last and par):
                            piece(b + par + 1, 1 - par, i, pK)

                    for t in range(T2 + 3 if last else T2):
                        if t < T2:
                            maxima(t, 0)
                        beside_piece(t - 1, 1)
                        if t < T2:
                            maxima(t, 1)
                            dve.wait_ge(mx_done, 1 + (k0 + t + 1) * 2)
                            dve.tensor_scalar(nmax[:, t % 2:t % 2 + 1], mx[:, 0:1], mx[:, 1:2], SCALE, ALU.min,
                                              ALU.mult).then_inc(nmax_done, 1)
                        if least + 1 <= t <= T2:
                            s = (t - 1) % 2
                            low_probs(t - 1, 0)
                            dve.wait_ge(exp_done, 1 + k0 + t)
                            dve.wait_ge(u_done, 1 + k0 + max(t - 2, least))
                            dve.reciprocal(rinv[:, s:s + 1], rsum[:, s:s + 1]).then_inc(rinv_done, 1)
                            low_probs(t - 1, 1)
                        beside_piece(t, 0)
                        if least + 1 <= t <= T2:
                            low_probs(t - 1, 2)
                        if least + 2 <= t <= T2 + 1:
                            par, p, s = (t - 2) // PAIRS, (t - 2) % PAIRS, t % 2
                            dve.wait_ge(rinv_done, 1 + k0 + t - 1)
                            dve.wait_ge(av_done, 1 + k0 + t - 1)
                            if p == 0:
                                dve.wait_ge(f_mm, 1 + (b if first else b + par - 1))
                            dve.scalar_tensor_tensor(u[:, par % 2, :, p, :], pU.rearrange("p (a c) -> p a c", a=2),
                                                     rinv[:, s:s + 1], rowmask, ALU.mult, ALU.mult).then_inc(u_done, 1)
                        if least + 1 <= t <= T2:
                            low_probs(t - 1, 3)

                for i in range(NP):
                    piece(0, 0, i, pS[:, BANK * (i % 4):BANK * (i % 4) + BANK])
                bodies(dve, body)


def l1x(nc, m, d):
    with ExitStack() as ctx:
        sb, ps, sem = names(nc, ctx)
        qbh = sb("x1_qbh", [P, B, PAIRS, P], BF16)
        qbl = sb("x1_qbl", [P, B, PAIRS, P], BF16)
        wh = sb("x1_wh", [P, 2, 2 * D], BF16)
        wl = sb("x1_wl", [P, 2, 2 * D], BF16)
        wB = sb("x1_wB", [P, 2 * D], BF16)
        oT = sb("x1_oT", [P, KC, TOK])
        stA = sb("x1_stA", [P, M])
        stB = sb("x1_stB", [P, M])
        hl = [Parts(sb, f"x1_ctx{n}", False) for n in range(2)]
        ctx_in, begun, split = (sem("x1_" + n) for n in ("ctx_in", "begun", "split"))
        with ExitStack() as c2:
            sb2, ps2, sem2 = names(nc, c2)
            qT = sb2("x1_qT", [P, KC, TOK])
            qm = sb2("x1_qm", [P, 2, 8, TOK])
            pq = ps2("x1_pq", [P, KC, BANK])
            q_mm, q_done, qm_done, qbh_done, qbl_done, whi, wlo = (
                sem2("x1_" + n) for n in ("q_mm", "q_done", "qm_done", "qbh_done", "qbl_done", "whi", "wlo"))
            with nc.Block() as block:
                @block.sync
                def _(sp):
                    load_context(sp, d, stA, stB, 0, ctx_in)

                @block.tensor
                def _(pe):
                    pe.wait_ge(m.late_loaded, m.late_n)
                    for n in range(KC):
                        for c in range(KC):
                            mm = pe.matmul(pq[:, n, :], m.late["x1_wq"][:, c, P * n:P * n + P], m.xnT[:, c, :], start=(c == 0),
                                           stop=(c == KC - 1))
                        mm.then_inc(q_mm, 1)

                def q_out(q, n, h):
                    return q[:, :, 4 * n + h // 2, NQ * (h % 2):NQ * (h % 2) + NQ]

                def by_batch(a):
                    return a.rearrange("p (b i) -> p b i", b=B)

                @block.scalar
                def _(act):
                    for n in range(KC):
                        act.wait_ge(q_mm, n + 1)
                        act.activation(qT[:, n, :], pq[:, n, :], ACT.Identity, bias=m.late["x1_bq"][:, n:n + 1]).then_inc(q_done, 1)
                    act.activation(wh[:, :, :], m.late["x1_wkv"][:, :, :], ACT.Copy).then_inc(whi, 1)
                    for k in range(16):
                        n, h = k // 8, k % 8
                        act.wait_ge(qm_done, k + 1)
                        act.activation(q_out(qbh, n, h), by_batch(qm[:, n, h, :]), ACT.Copy).then_inc(qbh_done, 1)

                @block.vector
                def _(dve):
                    hmask = m.small[:, SMALL["hmask"]:SMALL["hmask"] + 8]
                    for k in range(16):
                        n, h = k // 8, k % 8
                        dve.wait_ge(q_done, n + 1)
                        dve.tensor_scalar(qm[:, n, h, :], qT[:, n, :], hmask[:, h:h + 1], None, ALU.mult).then_inc(qm_done, 1)
                    for k in range(16):
                        n, h = k // 8, k % 8
                        dve.wait_ge(qbh_done, k + 1)
                        dve.tensor_tensor(q_out(qbl, n, h), by_batch(qm[:, n, h, :]), q_out(qbh, n, h),
                                          ALU.subtract).then_inc(qbl_done, 1)

                @block.gpsimd
                def _(pool):
                    pool.wait_ge(m.late_loaded, m.late_n)
                    pool.wait_ge(whi, 1)
                    pool.tensor_tensor(wl[:, :, :], m.late["x1_wkv"][:, :, :], wh[:, :, :], ALU.subtract).then_inc(wlo, 1)
                    pool.tensor_copy(wB[0:64, :], wh[0:64, 1, :]).then_inc(wlo, 1)
                    pool.wait_ge(wlo, 1)
                    pool.tensor_copy(wB[64:128, :], wl[64:128, 1, :]).then_inc(wlo, 1)
                    pool.wait_ge(wlo, 3)
                    pool.sem_inc(split, 1)
                    split_context(pool, 0, hl[0], stA, stB, ctx_in, begun, split)

        l1x_tiles(nc, m, d, (stA, stB, hl, ctx_in, begun, split), qbh, qbl, wh, wl, wB, oT)
        project(nc, m, "xp", oT, m.late["x1_wo"], m.late["x1_bo"][:, :])


def l1_attn(nc, m, d):
    with ExitStack() as ctx:
        sb, ps, sem = names(nc, ctx)
        x2 = sb("a1_x2", [P, TT, D])
        x2T = sb("a1_x2T", [P, KC, TOK])
        layer_norm(nc, m, "ln4b", m.xn, x2, x2T, (m.late["a1_gamma"][:, :], m.late["a1_beta"][:, :]))
        qk = sb("a1_qk", [P, TT, 2 * D])
        kT = sb("a1_kT", [P, KC, TOK])
        qT = sb("a1_qT", [P, KC, TOK])
        vhl = sb("a1_vhl", [P, TT, H, 32], BF16)
        gates = sb("a1_gates", [P, TT, 2 * H])
        o = sb("a1_o", [P, TT, D])
        with ExitStack() as c2:
            sb2, ps2, sem2 = names(nc, c2)
            sq = sb2("a1_sq", [P, TT, 2 * D])
            ss = sb2("a1_ss", [P, TT, 2 * H])
            nrm = sb2("a1_nrm", [P, TT, 2 * H])
            vg = sb2("a1_vg", [P, TT, D])
            pqk = ps2("a1_pqk", [P, TT, BANK])
            pv = ps2("a1_pv", [P, TT, BANK])
            qk_mm, v_mm, qk_done, chain, nrm_done, sig_done, turned, copied, v_hi, v_lo, freed = (
                sem2("a1_" + n) for n in ("qk_mm", "v_mm", "qk_done", "chain", "nrm_done", "sig_done", "turned",
                                          "copied", "v_hi", "v_lo", "freed"))

            def by_head(a, n):
                return a.rearrange("p t (h e) -> p t h e", h=n)

            with nc.Block() as block:
                @block.tensor
                def _(pe):
                    for t in range(TT):
                        s = slice(P * t, P * t + P)
                        for c in range(KC):
                            mm = pe.matmul(pqk[:, t, :], x2T[:, c, s], m.late["a1_wqk"][:, c, :], start=(c == 0), stop=(c == KC - 1))
                        mm.then_inc(qk_mm, 1)
                    for t in range(TT):
                        s = slice(P * t, P * t + P)
                        for c in range(KC):
                            mm = pe.matmul(pv[:, t, 0:D], m.xnT[:, c, s], m.late["a1_wv"][:, c, :], start=(c == 0), stop=(c == KC - 1))
                        mm.then_inc(v_mm, 1)
                    pe.wait_ge(chain, 5)
                    for n in range(4):
                        for t in range(TT):
                            mm = pe.transpose(pqk[:, n, P * t:P * t + P], qk[:, t, P * n:P * n + P], m.ident[:, :])
                        mm.then_inc(turned, 1)

                @block.scalar
                def _(act):
                    for t in range(TT):
                        act.wait_ge(qk_mm, t + 1)
                        act.activation(qk[:, t, :], pqk[:, t, :], ACT.Copy).then_inc(qk_done, 1)
                    act.wait_ge(chain, 2)
                    act.activation(nrm[:, :, :], ss[:, :, :], ACT.Sqrt).then_inc(nrm_done, 1)
                    act.wait_ge(chain, 7)
                    act.activation(gates[:, :, :], ss[:, :, :], ACT.Sigmoid).then_inc(sig_done, 1)
                    for n in range(4):
                        act.wait_ge(turned, n + 1)
                        o_ = (qT if n < 2 else kT)[:, n % 2, :]
                        act.activation(o_, pqk[:, n, :], ACT.Copy).then_inc(copied, 1)

                @block.vector
                def _(dve):
                    dve.wait_ge(qk_done, TT)
                    inv = nrm
                    q4 = by_head(qk[:, :, :], 2 * H)
                    link = chained(dve, chain)
                    link(dve.tensor_tensor(sq[:, :, :], qk[:, :, :], qk[:, :, :], ALU.mult))
                    link(dve.tensor_reduce(ss[:, :, :], by_head(sq[:, :, :], 2 * H), AX_X, ALU.add))
                    dve.wait_ge(nrm_done, 1)
                    link(dve.tensor_scalar(nrm[:, :, :], nrm[:, :, :], 1e-12, None, ALU.max))
                    link(dve.reciprocal(inv[:, :, :], nrm[:, :, :]))
                    link(dve.tensor_tensor(q4, q4, inv[:, :, :].unsqueeze(3).broadcast_to([P, TT, 2 * H, 16]), ALU.mult))
                    link(dve.tensor_tensor(sq[:, :, :], qk[:, :, :],
                         m.late["a1_g"][:, :].unsqueeze(1).broadcast_to([P, TT, 2 * D]), ALU.mult))
                    link(dve.tensor_reduce(ss[:, :, :], by_head(sq[:, :, :], 2 * H), AX_X, ALU.add))
                    dve.wait_ge(sig_done, 1)
                    dve.wait_ge(v_mm, TT)
                    link(dve.tensor_scalar(gates[:, :, :], gates[:, :, :], 0.75, 0.25, ALU.mult, ALU.add))
                    link(dve.tensor_tensor(
                         by_head(vg[:, :, :], H), pv[:, :, 0:D].rearrange("p t (h e) -> p t h e", h=H),
                         gates[:, :, H:2 * H].unsqueeze(3).broadcast_to([P, TT, H, 16]), ALU.mult))

                @block.gpsimd
                def _(pool):
                    pool.wait_ge(chain, 9)
                    v4 = by_head(vg[:, :, :], H)
                    for t in range(TT):
                        pool.tensor_copy(vhl[:, t, :, 0:16], v4[:, t]).then_inc(v_hi, 1)
                    for t in range(TT):
                        pool.wait_ge(v_hi, t + 1)
                        pool.tensor_tensor(vhl[:, t, :, 16:32], v4[:, t], vhl[:, t, :, 0:16], ALU.subtract).then_inc(v_lo, 1)
        heads16(nc, m, "ah", qT, kT, vhl, o, lambda t: gates[:, t, 0:H].unsqueeze(2).broadcast_to([P, H, 16]), None)
        project(nc, m, "ap", kT, m.late["a1_wo"], m.late["a1_bo"][:, :], src=o)


MAGIC = 1.5 * 2 ** 23


def l1_ffn(nc, m, d):
    with ExitStack() as ctx:
        sb, ps, sem = names(nc, ctx)
        wq = sb("ff_wq", [P, KC, FF], BF16)
        wo = sb("ff_wo_sim", [P, FC, D])
        am = sb("ff_am", [P, 2, FC])
        rs = sb("ff_rs", [P, 2, FC])
        dq = sb("ff_dq", [P, 2, FC])
        wo_done = sem("ff_wo_done")
        with ExitStack() as c2:
            sb2, ps2, sem2 = names(nc, c2)
            w1 = sb2("ff_w1", [P, FC, D])
            w2 = sb2("ff_w2", [P, FC, D])
            w1q = sb2("ff_w1q", [P, FC, D], BF16)
            idb = sb2("ff_idb", [P, P], BF16)
            pW = ps2("ff_pW", [P, 4, 2 * BANK], BF16)
            chain, id_done, w_t, w_c, scaled, w2_done = (sem2("ff_" + n) for n in (
                "chain", "id_done", "w_t", "w_c", "scaled", "w2_done"))
            with nc.Block() as block:
                @block.vector
                def _(dve):
                    dve.wait_ge(m.late_loaded, m.late_n)
                    link = chained(dve, chain)
                    for n, w in ((0, m.late["ff_w_in"]), (1, m.late["ff_w_out"])):
                        link(dve.tensor_reduce(am[:, n, :], w[:, :, :], AX_X, ALU.max, apply_absolute_value=True))
                        link(dve.tensor_scalar(am[:, n, :], am[:, n, :], 1e-8, None, ALU.max))
                        link(dve.reciprocal(rs[:, n, :], am[:, n, :]))
                        link(dve.tensor_scalar(rs[:, n, :], rs[:, n, :], 127.0, None, ALU.mult))
                        link(dve.tensor_scalar(dq[:, n, :], am[:, n, :], 1 / 127.0, None, ALU.mult))
                    half = FC // 2
                    for n in range(2):
                        c = slice(half * n, half * n + half)
                        dve.wait_ge(scaled, half * (n + 1))
                        link(dve.tensor_scalar(w1[:, c, :], w1[:, c, :], 127.0, -128.0, ALU.min, ALU.max))
                        link(dve.tensor_scalar(w1q[:, c, :], w1[:, c, :], MAGIC, MAGIC, ALU.add, ALU.subtract))
                    for n in range(2):
                        c = slice(half * n, half * n + half)
                        dve.wait_ge(scaled, FC + half * (n + 1))
                        link(dve.tensor_scalar(w2[:, c, :], w2[:, c, :], 127.0, -128.0, ALU.min, ALU.max))
                        dve.tensor_scalar(w2[:, c, :], w2[:, c, :], MAGIC, MAGIC, ALU.add, ALU.subtract).then_inc(w2_done, 1)
                    for n in range(4):
                        dve.wait_ge(w_t, n + 1)
                        dve.tensor_copy(wq[:, n % 2, BANK * (n // 2):BANK * (n // 2) + BANK], pW[:, n, 0:BANK]).then_inc(w_c, 1)

                @block.scalar
                def _(act):
                    for n, (w, o) in enumerate(((m.late["ff_w_in"], w1), (m.late["ff_w_out"], w2))):
                        act.wait_ge(chain, 5 * n + 4)
                        for c in range(FC):
                            act.activation(o[:, c, :], w[:, c, :], ACT.Copy, scale=rs[:, n, c:c + 1]).then_inc(scaled, 1)
                    for n in range(2):
                        act.wait_ge(w2_done, n + 1)
                        act.wait_ge(chain, 10)
                        for c in range(FC // 2 * n, FC // 2 * (n + 1)):
                            act.activation(wo[:, c, :], w2[:, c, :], ACT.Copy, scale=dq[:, 1, c:c + 1]).then_inc(wo_done, 1)

                @block.gpsimd
                def _(pool):
                    pool.tensor_copy(idb[:, :], m.ident[:, :]).then_inc(id_done, 1)

                @block.tensor
                def _(pe):
                    pe.wait_ge(id_done, 1)
                    for h in range(2):
                        pe.wait_ge(chain, 10 + 2 * (h + 1))
                        for c in range(KC):
                            for a in range(4):
                                mm = pe.transpose(pW[:, 2 * h + c, P * a:P * a + P],
                                                  w1q[:, 4 * h + a, P * c:P * c + P], idb[:, :])
                            mm.then_inc(w_t, 1)
        xq = sb("ff_xq", [P, TT, D])
        xh = sb("ff_xh", [P, KC, TOK], BF16)
        xl = sb("ff_xl", [P, KC, TOK], BF16)
        hid = sb("ff_hid", [P, FC, TOK])
        cols = sb("ff_cols", [P, 8])
        hmax = sb("ff_hmax", [P, FC])
        top = sb("ff_top", [1, 2])
        sc = sb("ff_sc", [P, 2, 2])
        dqx = sb("ff_dqx", [P, FC])
        pM = ps("ff_pM", [P, BANK])
        pXT = ps("ff_pXT", [P, KC, BANK])
        pH = ps("ff_pH", [P, 2, BANK])
        chain, m_mm, turned, xhi, h_mm, h_done, hm_done, x_mm = (
            sem("fg_" + n) for n in ("chain", "m_mm", "turned", "xhi", "h_mm", "h_done", "hm_done", "x_mm"))
        steps = [0]

        def largest(dve, link, column, k):
            dve.wait_ge(m_mm, 2 * k + 1)
            link(dve.tensor_reduce(top[0:1, k:k + 1], pM[0:1, 0:P], AX_X, ALU.max))
            link(dve.tensor_scalar(top[0:1, k:k + 1], top[0:1, k:k + 1], 1e-8, None, ALU.max))
            dve.wait_ge(m_mm, 2 * k + 2)
            link(dve.tensor_copy(cols[:, 2 + k:3 + k], pM[:, P:P + 1]))
            link(dve.reciprocal(sc[:, k, 0:1], cols[:, 2 + k:3 + k]))
            link(dve.tensor_scalar(sc[:, k, 0:1], sc[:, k, 0:1], 32767.0, None, ALU.mult))
            link(dve.tensor_scalar(sc[:, k, 1:2], cols[:, 2 + k:3 + k], 1 / 32767.0, None, ALU.mult))

        C_AMAX, C_TOP, C_XQ = 1, 3, 10
        with nc.Block() as block:
            @block.vector
            def _(dve):
                def link(ins):
                    steps[0] += 1
                    ins.then_inc(chain, 1)
                    dve.wait_ge(chain, steps[0])

                link(dve.tensor_reduce(cols[:, 0:1], m.xn[:, :, :].rearrange("p t f -> p (t f)"), AX_X, ALU.max,
                                       apply_absolute_value=True))
                largest(dve, link, 0, 0)
                link(dve.tensor_scalar(xq[:, :, :], m.xn[:, :, :], sc[:, 0, 0:1], 32767.0, ALU.mult, ALU.min))
                link(dve.tensor_scalar(xq[:, :, :], xq[:, :, :], -32768.0, MAGIC, ALU.max, ALU.add))
                link(dve.tensor_scalar(xq[:, :, :], xq[:, :, :], MAGIC, None, ALU.subtract))
                assert steps[0] == C_XQ
                link(dve.tensor_scalar(dqx[:, :], dq[:, 0, :], sc[:, 0, 1:2], None, ALU.mult))
                for c in range(KC):
                    dve.wait_ge(xhi, c + 1)
                    link(dve.tensor_tensor(xl[:, c, :], pXT[:, c, :], xh[:, c, :], ALU.subtract))
                link(dve.tensor_tensor(m.x[:, :, :], m.x[:, :, :], m.late["ff_b_out"][:, :].unsqueeze(1).broadcast_to([P, TT, D]),
                                       ALU.add))
                for n in range(FC):
                    dve.wait_ge(h_done, n + 1)
                    dve.tensor_reduce(hmax[:, n:n + 1], hid[:, n, :], AX_X, ALU.max, apply_absolute_value=True).then_inc(
                        hm_done, 1)
                dve.wait_ge(hm_done, FC)
                link(dve.tensor_reduce(cols[:, 1:2], hmax[:, :], AX_X, ALU.max))

            @block.scalar
            def _(act):
                for c in range(KC):
                    act.wait_ge(turned, c + 1)
                    act.activation(xh[:, c, :], pXT[:, c, :], ACT.Copy).then_inc(xhi, 1)
                act.wait_ge(chain, C_XQ + 1)
                for n in range(FC):
                    act.wait_ge(h_mm, n + 1)
                    act.activation(hid[:, n, :], pH[:, n % 2, :], ACT.Gelu, bias=m.late["ff_b_in"][:, n:n + 1],
                                   scale=dqx[:, n:n + 1]).then_inc(h_done, 1)

            @block.tensor
            def _(pe):
                pe.wait_ge(chain, C_AMAX)
                pe.transpose(pM[0:1, 0:P], cols[:, 0:1], m.ident[:, :]).then_inc(m_mm, 1)
                pe.wait_ge(chain, C_TOP)
                pe.matmul(pM[:, P:P + 1], m.ones_row, top[0:1, 0:1], start=True, stop=True).then_inc(m_mm, 1)
                pe.wait_ge(chain, C_XQ)
                for c in range(KC):
                    for t in range(TT):
                        mm = pe.transpose(pXT[:, c, P * t:P * t + P], xq[:, t, P * c:P * c + P], m.ident[:, :])
                    mm.then_inc(turned, 1)
                pe.wait_ge(chain, C_XQ + 1 + KC)
                for n in range(FC):
                    if n >= 2:
                        pe.wait_ge(h_done, n - 1)
                    for a in range(4):
                        c, xx = a // 2, (xh, xl)[a % 2]
                        mm = pe.matmul(pH[:, n % 2, :], wq[:, c, P * n:P * n + P], xx[:, c, :], start=(a == 0), stop=(a == 3))
                    mm.then_inc(h_mm, 1)
        pX = ps("ff_pX", [P, 2, BANK])
        chain2, x_done, fq = (sem("fh_" + n) for n in ("chain", "x_done", "fq"))
        with nc.Block() as block:
            @block.vector
            def _(dve):
                done = [0]

                def link(ins):
                    done[0] += 1
                    ins.then_inc(chain2, 1)
                    dve.wait_ge(chain2, done[0])

                largest(dve, link, 1, 1)
                for n in range(FC):
                    link(dve.tensor_scalar(hid[:, n, :], hid[:, n, :], sc[:, 1, 0:1], 32767.0, ALU.mult, ALU.min))
                    link(dve.tensor_scalar(hid[:, n, :], hid[:, n, :], -32768.0, MAGIC, ALU.max, ALU.add))
                    link(dve.tensor_scalar(hid[:, n, :], hid[:, n, :], MAGIC, None, ALU.subtract))
                for t in range(TT):
                    dve.wait_ge(x_mm, t + 1)
                    dve.scalar_tensor_tensor(m.x[:, t, :], (pX if t < 2 else pXT)[:, t % 2, 0:D], sc[:, 1, 1:2], m.x[:, t, :],
                                             ALU.mult, ALU.add).then_inc(x_done, 1)

            @block.tensor
            def _(pe):
                pe.transpose(pM[0:1, 0:P], cols[:, 1:2], m.ident[:, :]).then_inc(m_mm, 1)
                pe.wait_ge(chain2, 2)
                pe.matmul(pM[:, P:P + 1], m.ones_row, top[0:1, 1:2], start=True, stop=True).then_inc(m_mm, 1)
                for n in range(FC):
                    pe.wait_ge(chain2, 6 + 3 * (n + 1))
                    for t in range(TT):
                        mm = pe.matmul((pX if t < 2 else pXT)[:, t % 2, 0:D], hid[:, n, P * t:P * t + P], wo[:, n, :],
                                       start=(n == 0), stop=(n == FC - 1))
                        if n == FC - 1:
                            mm.then_inc(x_mm, 1)


LATE = {
    "gl_wq": [P, KC, D], "gl_wkv": [P, KC, 2 * D], "gl_wf": [P, KC, 96], "gl_g1": [P, KC, 16], "gl_g2": [16, D],
    "gl_lnw": [P, D], "gl_wo": [P, KC, D], "scanmask": [P, TOK],
    "x1_wq": [P, KC, D], "x1_bq": [P, KC], "x1_wkv": [P, 2, 2 * D], "x1_bk": [P, KC], "x1_bv": [P, KC],
    "x1_wo": [P, KC, D], "x1_bo": [1, D],
    "a1_wqk": [P, KC, 2 * D], "a1_wv": [P, KC, D], "a1_wo": [P, KC, D], "a1_bo": [1, D], "a1_gamma": [P, D],
    "a1_beta": [P, D], "a1_g": [P, 2 * D],
    "ff_w_in": [P, FC, D], "ff_w_out": [P, FC, D], "ff_b_in": [P, FC], "ff_b_out": [P, D],
    "mo_gate": [P, KC, E], "mo_wg": [P, E, KC, I], "mo_wu": [P, E, KC, I], "mo_wd": [P, E, D],
}


def late_weights(nc, m, d, sb, prefixes):
    tiles = {name: sb("w_" + name, shape) for name, shape in LATE.items() if name[:2] in prefixes}
    m.late.update(tiles)
    m.late_n += 16 * len(tiles)
    with nc.Block() as block:
        @block.sync
        def _(sp):
            sp.wait_ge(m.w0_loaded, 48)
            for name, t in tiles.items():
                rank = len(LATE[name])
                sp.dma_start(t[:, :] if rank == 2 else t[:, :, :] if rank == 3 else t[:, :, :, :],
                             d[name]).then_inc(m.late_loaded, 16)


def clear_semaphores(nc):
    done = sorted(nc.released_uncleared_semaphores)
    runs, start = [], None
    for n, s in enumerate(done):
        start = s if start is None else start
        if n + 1 == len(done) or done[n + 1] != s + 1:
            runs.append(range(start, s + 1))
            start = None
    with nc.Block() as block:
        @block.gpsimd
        def _(pool):
            for r in runs:
                pool.sem_clear(r)


def build(nc, d, out):
    with ExitStack() as ctx:
        sb, ps, sem = names(nc, ctx)
        m = Shared()
        m.x_loaded, m.const_loaded, m.w0_loaded, m.late_loaded, m.onehot_made, m.stored = (
            sem(n) for n in ("x_loaded", "const_loaded", "w0_loaded", "late_loaded", "onehot_made", "stored"))
        m.x = sb("x", [P, TT, D])
        m.xn = sb("xn", [P, TT, D])
        m.xnT = sb("xnT", [P, KC, TOK])
        m.ident = sb("ident", [P, P])
        m.onehot = sb("onehot", [96, H, P], BF16)
        m.maskneg = sb("maskneg", [P, BANK])
        m.mask05 = sb("mask05", [P, BANK])
        m.small = sb("small", [P, SMALL["n"]])
        m.eps = m.small[:, SMALL["eps"]:SMALL["eps"] + 1]
        m.one = m.small[:, SMALL["ones"]:SMALL["ones"] + 1]
        m.tanh_bias = m.small[:, SMALL["tanh"]:SMALL["tanh"] + 1]
        m.ones_row = m.small[0:1, SMALL["ones"]:SMALL["ones"] + P]
        m.const_n = 64
        with ExitStack() as c2:
            sb2, _, _ = names(nc, c2)
            m.wv0 = sb2("wv0", [P, 2, 1024])
            m.wo0 = sb2("wo0", [P, PAIRS, D])
            m.bo0 = sb2("bo0", [1, D])
            load_inputs(nc, m, d)
            m.quA = sb2("quA", [P, 2, B, PAIRS, P], BF16)
            m.quB = sb2("quB", [P, B, PAIRS, P], BF16)
            with ExitStack() as c3:
                c0 = context0(nc, c3)
                layer_norm(nc, m, "ln0", m.x, m.xn, m.xnT)
                l0x_queries(nc, m, d, c0)
                l0x_attention(nc, m, d, c0)
            l0x_output(nc, m, d)
        with ExitStack() as c2:
            sb2, _, _ = names(nc, c2)
            m.late, m.late_n = {"onehot": m.onehot}, 0
            with ExitStack() as c3:
                late_weights(nc, m, d, names(nc, c3)[0], ("gl", "sc", "mo"))
                layer_norm(nc, m, "ln1", m.x, m.xn, m.xnT)
                l0_gla(nc, m, d)
                layer_norm(nc, m, "ln2", m.x, m.xn, m.xnT)
                l0_moe(nc, m, d)
            clear_semaphores(nc)
            c3 = c2.enter_context(ExitStack())
            late_weights(nc, m, d, names(nc, c3)[0], ("x1",))
            layer_norm(nc, m, "ln3", m.x, m.xn, m.xnT)
            l1x(nc, m, d)
            c3.close()
            late_weights(nc, m, d, sb2, ("a1", "ff"))
            layer_norm(nc, m, "ln4", m.x, m.xn, m.xnT)
            l1_attn(nc, m, d)
            layer_norm(nc, m, "ln5", m.x, m.xn, None)
            l1_ffn(nc, m, d)
        with nc.Block() as block:
            @block.sync
            def _(sp):
                sp.wait_ge(m.w0_loaded, 48)
                sp.wait_ge(m.late_loaded, m.late_n)
                sp.dma_start(out, m.x[:, :, :]).then_inc(m.stored, 16)
                sp.wait_ge(m.stored, 16)


SMALL = {"eps": 0, "ones": 1, "hmask": 129, "desc": 137, "tanh": 145, "rowmask": 146, "fold": 210, "onehot": 274, "n": 290}


def layouts(v):
    f = np.float32
    c = np.ascontiguousarray

    def rows(w, n=P):
        w = np.asarray(w)
        return c(w.reshape(-1, n, w.shape[1]).transpose(1, 0, 2))

    a = {}
    a["x"] = rows(v["x"].reshape(TOK, D))
    ctx = v["ctx_768"]
    pad = np.zeros((B, MC * P, DC), f)
    pad[:, :M] = ctx
    a["ctxn"] = c(pad.reshape(B, MC, P, DC).transpose(0, 2, 1, 3))
    a["ctxT"] = c(ctx.transpose(0, 2, 1))
    a["wq0"] = rows(v["L0_xattn_Wq"])
    wkT = v["L0_xattn_Wk"].T
    a["wk0"] = rows(np.concatenate([wkT, wkT[:, P:]], axis=1))
    wv = v["L0_xattn_Wv"]
    a["wv0"] = c(np.stack([wv[:P], np.concatenate([wv[P:], wv[P:]])], axis=1))
    a["wo0"] = rows(v["L0_xattn_Wo"])
    a["bo0"] = c(v["L0_xattn_bo"][None])
    a["ident"] = np.eye(P, dtype=f)
    s, t = np.arange(P)[:, None], np.arange(P)[None]
    same = s // NQ == t // NQ
    a["maskneg"] = np.tile(np.where(same & (s <= t), 0, -1e30).astype(f), (1, 4))
    a["mask05"] = np.tile(np.where(same, 0.5, 0).astype(f), (1, 4))
    small = np.zeros((P, SMALL["n"]), f)
    small[:, SMALL["eps"]] = 1e-5
    small[:, SMALL["ones"]:SMALL["ones"] + P] = 1
    small[:, SMALL["hmask"]:SMALL["hmask"] + 8] = np.arange(P)[:, None] // 16 == np.arange(8)
    small[:, SMALL["desc"]:SMALL["desc"] + E] = E - np.arange(E)
    small[:, SMALL["tanh"]] = -15.0 * 0.27
    r = np.arange(P)[:, None]
    small[:, SMALL["rowmask"]:SMALL["rowmask"] + 64] = r // NQ == np.arange(64) % 32 // 16
    small[:, SMALL["fold"]:SMALL["fold"] + NQ] = r % NQ == np.arange(NQ)
    small[:, SMALL["onehot"]:SMALL["onehot"] + H] = r % 32 == np.arange(H)
    a["small"] = small

    gl = {n: v["L0_attn_" + n] for n in ("Wq", "Wk", "Wv", "Wf", "Wg1", "Wg2", "ln_w", "Wo")}
    a["gl_wq"] = rows(gl["Wq"].T)
    a["gl_wkv"] = rows(np.concatenate([gl["Wk"].T, gl["Wv"].T], axis=1))
    wf = np.zeros((D, 96), f)
    for n in range(3):
        wf[:, 32 * n:32 * n + 16] = gl["Wf"].T
    a["gl_wf"] = rows(wf)
    a["gl_g1"] = rows(gl["Wg1"].T)
    a["gl_g2"] = c(gl["Wg2"].T)
    a["gl_lnw"] = c(np.broadcast_to(gl["ln_w"], (P, D)))
    a["gl_wo"] = rows(gl["Wo"].T)
    a["scanmask"] = np.tile((np.arange(TOK) % NQ != 0).astype(f), (P, 1))
    a["mo_gate"] = rows(v["L0_ffn_gate_w"].T)
    for n, w in (("mo_wg", "w_gate"), ("mo_wu", "w_up")):
        a[n] = c(v["L0_ffn_" + w].reshape(E, I, KC, P).transpose(3, 0, 2, 1))
    a["mo_wd"] = c(v["L0_ffn_w_down"].transpose(2, 0, 1))

    def cols(b, n=P):
        return c(np.asarray(b).reshape(-1, n).T)

    x1 = {n: v["L1_xattn_" + n] for n in ("Wq", "bq", "Wkv", "bkv", "Wo", "bo")}
    ik = (np.arange(H)[:, None] * 32 + np.arange(16)).ravel()
    a["x1_wq"] = rows(x1["Wq"].T)
    a["x1_bq"] = cols(x1["bq"])
    wkv = x1["Wkv"][np.concatenate([ik, ik + 16])].T
    a["x1_wkv"] = c(np.stack([wkv[:P], np.concatenate([wkv[P:], wkv[P:]])], axis=1))
    a["x1_bk"] = cols(x1["bkv"][ik])
    a["x1_bv"] = cols(x1["bkv"][ik + 16])
    a["x1_wo"] = rows(x1["Wo"].T)
    a["x1_bo"] = c(x1["bo"][None])
    a1 = {n: v["L1_attn_" + n] for n in ("w_q", "w_k", "w_v", "g_q", "g_k", "w_o", "b_o", "gamma", "beta")}
    a["a1_wqk"] = rows(np.concatenate([a1["w_q"], a1["w_k"]], axis=1))
    a["a1_wv"] = rows(a1["w_v"])
    a["a1_wo"] = rows(a1["w_o"])
    a["a1_bo"] = c(a1["b_o"][None])
    for n in ("gamma", "beta"):
        a["a1_" + n] = c(np.broadcast_to(a1[n], (P, D)))
    a["a1_g"] = c(np.broadcast_to(np.concatenate([np.tile(a1["g_q"], H), np.tile(a1["g_k"], H)]), (P, 2 * D)))
    a["ff_w_in"] = rows(v["L1_ffn_W_in"].T)
    a["ff_w_out"] = rows(v["L1_ffn_W_out"])
    a["ff_b_in"] = cols(v["L1_ffn_b_in"])
    a["ff_b_out"] = c(np.broadcast_to(v["L1_ffn_b_out"], (P, D)))
    return a


def kernel(**inputs):
    import concourse.bacc as _bacc
    from concourse.bass_utils import run_bass_kernel_spmd as _run

    arrays = layouts({k: np.asarray(v) for k, v in inputs.items()})
    nc = _bacc.Bacc("TRN2", target_bir_lowering=False, num_devices=1)
    d = {n: nc.dram_tensor(f"in_{n}", a.shape, mybir.dt.from_np(a.dtype), kind="ExternalInput").ap()
         for n, a in arrays.items()}
    out = nc.dram_tensor("out_x", (P, TT, D), F32, kind="ExternalOutput").ap()
    build(nc, d, out)
    r = _run(nc, [{f"in_{n}": a for n, a in arrays.items()}], core_ids=[0])
    y = np.asarray(r.results[0]["out_x"])
    return y.transpose(1, 0, 2).reshape(B, NQ, D)
```

```python
from contextlib import ExitStack

import numpy as np
import concourse.bass as bass
from concourse import mybir
from concourse.alu_op_type import AluOpType as ALU

F32 = mybir.dt.float32
BF16 = mybir.dt.bfloat16
ACT = mybir.ActivationFunctionType
AX_X = mybir.AxisListType.X

P = 128
B, NQ, D = 8, 64, 256
TOK = B * NQ
TT = TOK // P
KC = D // P
M, DC = 1601, 192
DB = DC - P
MC = -(-M // P)
ML = M - (MC - 1) * P
H = 16
PAIRS = H // 2
BANK = 512
SEG = [(j * BANK, min(BANK, M - j * BANK)) for j in range(-(-M // BANK))]
TGRP = [(g, range(4 * g, min(4 * g + 4, MC))) for g in range(-(-MC // 4))]
NG = len(TGRP)
E, I = 8, 128
FF = 1024
FC = FF // P


class Shared:
    pass


class Parts:
    def __init__(self, sb, tag, natural):
        if natural:
            self.nh, self.nl = (sb(f"{tag}_{n}", [P, MC, DC], BF16) for n in ("nh", "nl"))
        self.ah, self.al, self.bh, self.bl = (sb(f"{tag}_{n}", [P, M + 1], BF16) for n in ("ah", "al", "bh", "bl"))


def names(nc, ctx):
    def sb(name, shape, dt=F32):
        return ctx.enter_context(nc.sbuf_tensor(name, shape, dt))

    def ps(name, shape, dt=F32):
        return ctx.enter_context(nc.psum_tensor(name, shape, dt))

    def sem(name):
        return ctx.enter_context(nc.semaphore(name))

    return sb, ps, sem


def chained(eng, sem):
    done = [0]

    def link(ins):
        done[0] += 1
        ins.then_inc(sem, 1)
        eng.wait_ge(sem, done[0])

    return link


def load_inputs(sp, m, d, c0):
    sp.dma_start(m.x[:, :, :], d["x"]).then_inc(m.x_loaded, 16)
    sp.dma_start(m.small[:, :], d["small"]).then_inc(m.const_loaded, 16)
    sp.dma_start(m.ident[:, :], d["ident"]).then_inc(m.const_loaded, 16)
    sp.dma_start(c0.wq[:, :, :], d["wq0"]).then_inc(c0.wq_in, 16)
    sp.dma_start(c0.wk[:, :, :], d["wk0"]).then_inc(c0.wk_in, 16)
    load_context0(sp, d, c0, 0)
    sp.dma_start(m.wv0[:, :, :], d["wv0"]).then_inc(m.w0_loaded, 16)
    sp.dma_start(m.wo0[:, :, :], d["wo0"]).then_inc(m.w0_loaded, 16)
    sp.dma_start(m.bo0[:, :], d["bo0"]).then_inc(m.w0_loaded, 16)
    sp.dma_start(m.maskneg[:, :], d["maskneg"]).then_inc(m.w0_loaded, 16)
    sp.dma_start(m.mask05[:, :], d["mask05"]).then_inc(m.w0_loaded, 16)


def loaded(m, eng, layer):
    eng.wait_ge(m.weights_in[layer], m.weights_n[layer])


def layer_norm(nc, m, tag, src, dst, dstT, affine=None, start=None):
    with ExitStack() as ctx:
        sb, ps, sem = names(nc, ctx)
        stats = sb(f"{tag}_stats", [P, TT, 6])
        mv = sb(f"{tag}_meanvar", [P, TT, 2])
        std = sb(f"{tag}_std", [P, TT])
        rstd = sb(f"{tag}_rstd", [P, TT])
        pT = ps(f"{tag}_pT", [P, KC, BANK])
        stats_done, mv_done, std_done, rstd_done, normed, scaled, done, turned, copied = (
            sem(f"{tag}_{n}") for n in
            ("stats_done", "mv_done", "std_done", "rstd_done", "normed", "scaled", "done", "turned", "copied"))
        with nc.Block() as block:
            if start is not None:
                @block.sync
                def _(sp):
                    start(sp)

            @block.vector
            def _(dve):
                dve.wait_ge(m.x_loaded, 16)
                for t in range(TT):
                    dve.bn_stats(stats[:, t, :], src[:, t, :]).then_inc(stats_done, 1)
                for t in range(TT):
                    dve.wait_ge(stats_done, t + 1)
                    dve.bn_aggr(mv[:, t, :], stats[:, t, :]).then_inc(mv_done, 1)
                dve.wait_ge(std_done, 1)
                dve.reciprocal(rstd[:, :], std[:, :]).then_inc(rstd_done, 1)
                dve.wait_ge(rstd_done, 1)
                for t in range(TT):
                    o = dve.tensor_scalar(dst[:, t, :], src[:, t, :], mv[:, t, 0:1], rstd[:, t:t + 1],
                                          ALU.subtract, ALU.mult)
                    o.then_inc(normed if affine else done, 1)
                if affine:
                    loaded(m, dve, affine[2])
                    for t in range(TT):
                        dve.wait_ge(normed, t + 1)
                        dve.tensor_tensor(dst[:, t, :], dst[:, t, :], affine[0], ALU.mult).then_inc(
                            scaled if affine[1] is not None else done, 1)
                    if affine[1] is not None:
                        for t in range(TT):
                            dve.wait_ge(scaled, t + 1)
                            dve.tensor_tensor(dst[:, t, :], dst[:, t, :], affine[1], ALU.add).then_inc(done, 1)
                if dstT is not None:
                    dve.wait_ge(turned, KC * TT)
                    dve.tensor_copy(dstT[:, 1, :], pT[:, 1, :]).then_inc(copied, 1)

            @block.scalar
            def _(act):
                act.wait_ge(mv_done, TT)
                act.wait_ge(m.const_loaded, m.const_n)
                act.activation(std[:, :], mv[:, :, 1], ACT.Sqrt, bias=m.eps).then_inc(std_done, 1)
                if dstT is not None:
                    act.wait_ge(turned, KC * TT)
                    act.activation(dstT[:, 0, :], pT[:, 0, :], ACT.Copy).then_inc(copied, 1)

            if dstT is not None:
                @block.tensor
                def _(pe):
                    pe.wait_ge(m.const_loaded, m.const_n)
                    for t in range(TT):
                        pe.wait_ge(done, t + 1)
                        for c in range(KC):
                            pe.transpose(pT[:, c, P * t:P * t + P], dst[:, t, P * c:P * c + P],
                                         m.ident[:, :]).then_inc(turned, 1)


NSPLIT0 = 6


def context0(nc, ctx):
    sb, _, sem = names(nc, ctx)
    c = Shared()
    c.stN = sb("stN", [P, MC, DC])
    c.stA = sb("stA", [P, M])
    c.stB = sb("stB", [P, M])
    c.hl = [Parts(sb, f"ctx{n}", True) for n in range(2)]
    c.ctx_in, c.begun, c.split, c.wq_in, c.wk_in = (sem("a0_" + n) for n in ("ctx_in", "begun", "split", "wq_in", "wk_in"))
    return c


def load_context0(sp, d, c, b):
    sp.dma_start(c.stA[:, :], d["ctxT"][bass.ds(b, 1), 0:P].rearrange("o p c -> (o p) c")).then_inc(c.ctx_in, 16)
    for s in (0, 64):
        sp.dma_start(c.stB[s:s + 64, :], d["ctxT"][bass.ds(b, 1), P:DC].rearrange("o p c -> (o p) c")).then_inc(c.ctx_in, 16)
    sp.dma_start(c.stN[:, :, :], d["ctxn"][bass.ds(b, 1)].rearrange("o p c f -> (o p) c f")).then_inc(c.ctx_in, 16)


def split_context0(pool, c, b, o):
    pool.wait_ge(c.ctx_in, (b + 1) * 64)
    pool.sem_inc(c.begun, 1)
    parts = ((o.ah[:, 0:M], o.al[:, 0:M], c.stA[:, :]), (o.bh[:, 0:M], o.bl[:, 0:M], c.stB[:, :]),
             (o.nh[:, :, :], o.nl[:, :, :], c.stN[:, :, :]))
    for first, group in ((0, parts[0:2]), (4, parts[2:3])):
        for hi, _, src in group:
            pool.tensor_copy(hi, src).then_inc(c.split, 1)
        for n, (hi, lo, src) in enumerate(group):
            pool.wait_ge(c.split, 1 + b * NSPLIT0 + first + n + 1)
            pool.tensor_tensor(lo, src, hi, ALU.subtract).then_inc(c.split, 1)


def l0x_queries(nc, m, d, c0):
    with ExitStack() as ctx:
        sb, ps, sem = names(nc, ctx)
        wq, wk = c0.wq, c0.wk
        wkh = sb("wk0h", [P, PAIRS, D], BF16)
        wkl = sb("wk0l", [P, PAIRS, D], BF16)
        qzh = sb("qzh", [P, 2, 2, TOK], BF16)
        qzl = sb("qzl", [P, 2, 2, TOK], BF16)
        pQ = ps("pQ", [P, 2, BANK])
        pK = ps("pK", [P, 4, BANK])
        wkh_done, wkl_done, zeroed, q_mm, q_hi, q_lo, qk_mm, qk_hi, qk_lo = (
            sem(n) for n in ("q0_wkh", "q0_wkl", "q0_zeroed", "q0_q_mm", "q0_q_hi", "q0_q_lo",
                             "q0_qk_mm", "q0_qk_hi", "q0_qk_lo"))
        with nc.Block() as block:
            @block.sync
            def _(sp):
                load_weights(m, d, sp, "gl")
                load_weights(m, d, sp, "x1")

            @block.gpsimd
            def _(pool):
                pool.memset(qzh[:, :, :, :], 0.0).then_inc(zeroed, 1)
                pool.memset(qzl[:, :, :, :], 0.0).then_inc(zeroed, 1)
                pool.wait_ge(wkh_done, 1)
                pool.tensor_tensor(wkl[:, :, :], wk[:, :, :], wkh[:, :, :], ALU.subtract).then_inc(wkl_done, 1)
                pool.wait_ge(wkl_done, 1)
                pool.sem_inc(c0.split, 1)
                split_context0(pool, c0, 0, c0.hl[0])

            @block.tensor
            def _(pe):
                pe.wait_ge(c0.wq_in, 16)
                for p in range(PAIRS + 1):
                    if p < PAIRS:
                        if p >= 2:
                            pe.wait_ge(q_lo, 2 * (p - 1))
                        for c in range(KC):
                            mm = pe.matmul(pQ[:, p % 2, :], wq[:, c, P * p:P * p + P], m.xnT[:, c, :],
                                           start=(c == 0), stop=(c == KC - 1))
                        mm.then_inc(q_mm, 1)
                    if p >= 1:
                        r = (p - 1) % 2
                        pe.wait_ge(q_lo, 2 * p)
                        pe.wait_ge(wkl_done, 1)
                        for n in range(4 * (p - 1), 4 * p):
                            h, part = (n % 4) // 2, n % 2
                            if n >= 4:
                                pe.wait_ge(qk_lo, n - 3)
                            w = slice(P * part, P * part + P)
                            for a, (wt, q) in enumerate(((wkh, qzh), (wkh, qzl), (wkl, qzh))):
                                mm = pe.matmul(pK[:, n % 4, :], wt[:, p - 1, w], q[:, r, h, :],
                                               start=(a == 0), stop=(a == 2))
                            mm.then_inc(qk_mm, 1)

            def qu_out(n):
                p, h, part = n // 4, (n % 4) // 2, n % 2
                s = slice(NQ * h, NQ * h + NQ)
                return part, (m.quA[:, 0, :, p, s], m.quA[:, 1, :, p, s], m.quB[:, :, p, s])

            @block.scalar
            def _(act):
                act.wait_ge(c0.wk_in, 16)
                act.activation(wkh[:, :, :], wk[:, :, :], ACT.Copy).then_inc(wkh_done, 1)
                act.wait_ge(zeroed, 2)
                for p in range(PAIRS + 1):
                    if p < PAIRS:
                        act.wait_ge(q_mm, p + 1)
                        if p >= 2:
                            act.wait_ge(qk_mm, 4 * (p - 1))
                        for h in range(2):
                            s = slice(64 * h, 64 * h + 64)
                            act.activation(qzh[s, p % 2, h, :], pQ[s, p % 2, :], ACT.Copy).then_inc(q_hi, 1)
                    if p >= 1:
                        for n in range(4 * (p - 1), 4 * p):
                            part, (ah, al, b) = qu_out(n)
                            act.wait_ge(qk_mm, n + 1)
                            src = pK[:, n % 4, :].rearrange("p (b i) -> p b i", b=B)
                            act.activation(b if part else ah, src, ACT.Copy).then_inc(qk_hi, 1)

            @block.vector
            def _(dve):
                for p in range(PAIRS + 1):
                    if p < PAIRS:
                        for h in range(2):
                            s = slice(64 * h, 64 * h + 64)
                            dve.wait_ge(q_hi, 2 * p + h + 1)
                            dve.tensor_tensor(qzl[s, p % 2, h, :], pQ[s, p % 2, :], qzh[s, p % 2, h, :],
                                              ALU.subtract).then_inc(q_lo, 1)
                    if p >= 1:
                        for n in range(4 * (p - 1), 4 * p):
                            part, (ah, al, b) = qu_out(n)
                            dve.wait_ge(qk_hi, n + 1)
                            src = pK[:, n % 4, :].rearrange("p (b i) -> p b i", b=B)
                            if part:
                                dve.tensor_tensor(b[64:128], src[64:128], b[64:128], ALU.subtract).then_inc(qk_lo, 1)
                            else:
                                dve.tensor_tensor(al, src, ah, ALU.subtract).then_inc(qk_lo, 1)


def l0x_attention(nc, m, d, c0):
    SCALE = 64 ** -0.5
    T2 = 2 * PAIRS
    with ExitStack() as ctx:
        sb, ps, sem = names(nc, ctx)
        hl = c0.hl
        prob = sb("prob", [P, 2, M])
        pth = sb("pth", [P, MC, P], BF16)
        ptl = sb("ptl", [P, MC, P], BF16)
        mx = sb("mx", [P, 2])
        nmax = sb("nmax", [P, 2])
        rsum = sb("rsum", [P, 2])
        rinv = sb("rinv", [P, 2])
        u = sb("u", [P, D])
        pS = ps("pS", [P, 4 * BANK])
        pT = ps("pT", [P, 2, BANK])
        pU = ps("pU", [P, D])
        pV = ps("pV", [P, 2, P])
        (s_done, exp_done, t_done, hi_done, lo_done, av_done, mx_done, nmax_done, rinv_done,
         u_done, ut_done, uhi_done, ulo_done) = (sem("a0_" + n) for n in (
             "s_done", "exp_done", "t_done", "hi_done", "lo_done", "av_done", "mx_done",
             "nmax_done", "rinv_done", "u_done", "ut_done", "uhi_done", "ulo_done"))
        split = c0.split
        wv_split = sem("a0_wv_split")

        def bodies(eng, body):
            body(0, True, range(T2))
            with eng.Fori(1, B // 2) as i:
                body(i * 2, False, range(T2))
            body(B - 2, False, range(T2, T2 + 2))

        with nc.Block() as block:
            @block.sync
            def _(sp):
                with sp.Fori(1, B) as b:
                    sp.wait_ge(split, 1 + b * NSPLIT0)
                    load_context0(sp, d, c0, b)

            @block.gpsimd
            def _(pool):
                split_context0(pool, c0, 1, hl[1])
                with pool.Fori(1, B // 2) as i:
                    b = i * 2
                    for par in range(2):
                        pool.wait_ge(av_done, 1 + b * PAIRS + (par - 1) * PAIRS)
                        split_context0(pool, c0, b + par, hl[par])
                pool.wait_ge(m.w0_loaded, m.w0_n)
                pool.wait_ge(split, 1 + B * NSPLIT0)
                pool.tensor_copy(m.wvh[:, :, :], m.wv0[:, :, :]).then_inc(wv_split, 1)
                pool.wait_ge(wv_split, 1)
                pool.tensor_tensor(m.wvl[:, :, :], m.wv0[:, :, :], m.wvh[:, :, :], ALU.subtract).then_inc(wv_split, 1)

            @block.tensor
            def _(pe):
                for s in (s_done, t_done, av_done, ut_done):
                    pe.sem_inc(s, 1)

                def body(b, first, steps):
                    k0 = b * PAIRS
                    least = 0 if first else -9

                    def scores(t, j):
                        par, p = t // PAIRS, t % PAIRS
                        c = hl[par % 2]
                        s, w = SEG[j]
                        qa = [m.quA[:, n, bass.ds(b + par, 1), p, :].rearrange("p o r -> p (o r)") for n in (0, 1)]
                        qb = m.quB[:, bass.ds(b + par, 1), p, :].rearrange("p o r -> p (o r)")
                        if j == 0:
                            pe.wait_ge(exp_done, 1 + k0 + t)
                            if p == 0:
                                pe.wait_ge(split, 1 + (b + par) * NSPLIT0 + 4)
                        for a, (q, k) in enumerate(((qa[0], c.ah), (qa[0], c.al), (qa[1], c.ah), (qb, c.bh), (qb, c.bl))):
                            mm = pe.matmul(pS[:, s:s + w], q, k[:, s:s + w], start=(a == 0), stop=(a == 4))
                        if j in (1, 3):
                            mm.then_inc(s_done, 1)

                    def turn_probs(t, g):
                        n = 4 * t + g
                        if g == 0:
                            pe.wait_ge(exp_done, 1 + k0 + t + 1)
                        pe.wait_ge(lo_done, 1 + k0 * NG + max(n - 1, least))
                        for c in TGRP[g][1]:
                            w = min(P, M - P * c)
                            mm = pe.transpose(pT[0:w, n % 2, P * (c % 4):P * (c % 4) + P],
                                              prob[:, t % 2, P * c:P * c + w], m.ident[:, :])
                        mm.then_inc(t_done, 1)

                    def values(t, chunks):
                        c = hl[t // PAIRS % 2]
                        if chunks[0] == 0:
                            pe.wait_ge(u_done, 1 + (k0 + t) * 2)
                            if t % PAIRS == 0:
                                pe.wait_ge(split, 1 + (b + t // PAIRS + 1) * NSPLIT0)
                        for n in chunks:
                            w = min(P, M - P * n)
                            if n % 4 == 0:
                                pe.wait_ge(lo_done, 1 + (k0 + t) * NG + n // 4 + 1)
                            for a, (pr, cx) in enumerate(((pth, c.nh), (pth, c.nl), (ptl, c.nh))):
                                mm = pe.matmul(pU[:, 0:DC], pr[0:w, n, :], cx[0:w, n, :],
                                               start=(n == 0 and a == 0), stop=(n == MC - 1 and a == 2))
                        if n == MC - 1:
                            mm.then_inc(av_done, 1)

                    def turn_result(t):
                        pe.wait_ge(u_done, 1 + (k0 + t + 1) * 2)
                        pe.wait_ge(ulo_done, 1 + (k0 + t) * 2)
                        for n in range(2):
                            pe.transpose(pV[:, n, :], u[:, P * n:P * n + P], m.ident[:, :]).then_inc(ut_done, 1)

                    for t in steps:
                        for j in range(4):
                            if t < T2:
                                scores(t, j)
                            if least + 1 <= t <= T2 and j < 2:
                                turn_probs(t - 1, j)
                        if least + 1 <= t <= T2:
                            turn_probs(t - 1, 2)
                            values(t - 1, range(0, 8))
                            turn_probs(t - 1, 3)
                            values(t - 1, range(8, MC))
                        if t >= least + 2:
                            turn_result(t - 2)

                bodies(pe, body)

            @block.scalar
            def _(act):
                for s in (exp_done, hi_done, uhi_done):
                    act.sem_inc(s, 1)

                def body(b, first, steps):
                    k0 = b * PAIRS
                    least = 0 if first else -9
                    def high_probs(t, g):
                        cs = TGRP[g][1]
                        n = 4 * t + g
                        w = min(P, M - P * cs[0])
                        if g == 0:
                            act.wait_ge(av_done, 1 + k0 + t)
                        act.wait_ge(t_done, 1 + (k0 + t) * NG + g + 1)
                        act.activation(pth[0:w, cs[0]:cs[-1] + 1, :], pT[0:w, n % 2, 0:P * len(cs)].rearrange(
                            "p (c r) -> p c r", r=P), ACT.Copy).then_inc(hi_done, 1)

                    for t in steps:
                        for g, cs in TGRP[:3] if least + 1 <= t <= T2 else ():
                            high_probs(t - 1, g)
                        if t < T2:
                            act.wait_ge(nmax_done, 1 + k0 + t + 1)
                            act.wait_ge(t_done, 1 + (k0 + max(t - 1, least)) * NG)
                            act.activation(prob[:, t % 2, :], pS[:, 0:M], ACT.Exp, bias=nmax[:, t % 2:t % 2 + 1], scale=SCALE,
                                           accum_out=rsum[:, t % 2:t % 2 + 1]).then_inc(exp_done, 1)
                        if least + 1 <= t <= T2:
                            high_probs(t - 1, 3)
                        if t >= least + 2:
                            par, p = (t - 2) // PAIRS, (t - 2) % PAIRS
                            for n in range(2):
                                act.wait_ge(ut_done, 1 + (k0 + t - 1) * 2)
                                o = m.quB[:, bass.ds(b + par, 1), p, :] if n else m.quA[:, 0, bass.ds(b + par, 1), p, :]
                                act.activation(o.rearrange("p o r -> p (o r)"), pV[:, n, :], ACT.Copy).then_inc(uhi_done, 1)

                bodies(act, body)

            @block.vector
            def _(dve):
                for s in (lo_done, mx_done, nmax_done, rinv_done, u_done, ulo_done):
                    dve.sem_inc(s, 1)

                def body(b, first, steps):
                    k0 = b * PAIRS
                    least = 0 if first else -9

                    def low_probs(t, g):
                        cs = TGRP[g][1]
                        n = 4 * t + g
                        w = min(P, M - P * cs[0])
                        dve.wait_ge(hi_done, 1 + (k0 + t) * NG + g + 1)
                        dve.tensor_tensor(ptl[0:w, cs[0]:cs[-1] + 1, :], pT[0:w, n % 2, 0:P * len(cs)].rearrange(
                            "p (c r) -> p c r", r=P), pth[0:w, cs[0]:cs[-1] + 1, :], ALU.subtract).then_inc(lo_done, 1)

                    def maxima(t, half):
                        a, z = (0, 2 * BANK) if half == 0 else (2 * BANK, M)
                        dve.wait_ge(s_done, 1 + (k0 + t) * 2 + half + 1)
                        dve.tensor_reduce(mx[:, half:half + 1], pS[:, a:z], AX_X, ALU.max, negate=True).then_inc(mx_done, 1)

                    for t in steps:
                        for half in range(2):
                            if least + 1 <= t <= T2:
                                low_probs(t - 1, half)
                            if t < T2:
                                maxima(t, half)
                        if t < T2:
                            dve.wait_ge(mx_done, 1 + (k0 + t + 1) * 2)
                            dve.tensor_scalar(nmax[:, t % 2:t % 2 + 1], mx[:, 0:1], mx[:, 1:2], SCALE, ALU.min,
                                              ALU.mult).then_inc(nmax_done, 1)
                        if least + 1 <= t <= T2:
                            low_probs(t - 1, 2)
                            low_probs(t - 1, 3)
                        if t >= least + 2:
                            par, p = (t - 2) // PAIRS, (t - 2) % PAIRS
                            ah, al = (m.quA[:, n, bass.ds(b + par, 1), p, :].rearrange("p o r -> p (o r)") for n in (0, 1))
                            bb = m.quB[64:128, bass.ds(b + par, 1), p, :].rearrange("p o r -> p (o r)")
                            dve.wait_ge(uhi_done, 1 + (k0 + t - 1) * 2)
                            dve.tensor_tensor(al, pV[:, 0, :], ah, ALU.subtract).then_inc(ulo_done, 1)
                            dve.tensor_tensor(bb, pV[64:128, 1, :], bb, ALU.subtract).then_inc(ulo_done, 1)
                        if least + 1 <= t <= T2:
                            s = (t - 1) % 2
                            dve.wait_ge(exp_done, 1 + k0 + t)
                            dve.reciprocal(rinv[:, s:s + 1], rsum[:, s:s + 1]).then_inc(rinv_done, 1)
                            dve.wait_ge(rinv_done, 1 + k0 + t)
                            dve.wait_ge(av_done, 1 + k0 + t)
                            dve.wait_ge(ut_done, 1 + (k0 + t - 1) * 2)
                            dve.tensor_scalar(u[:, 0:DC], pU[:, 0:DC], rinv[:, s:s + 1], None, ALU.mult).then_inc(u_done, 1)
                            dve.tensor_scalar(u[:, DC:D], pU[:, P:DC], rinv[:, s:s + 1], None, ALU.mult).then_inc(u_done, 1)

                bodies(dve, body)


def l0x_output(nc, m, d):
    with ExitStack() as ctx:
        sb, ps, sem = names(nc, ctx)
        wvh, wvl = m.wvh, m.wvl
        woh, wol = (sb(n, [P, PAIRS, D], BF16) for n in ("wo0h", "wo0l"))
        oh, ol = (sb(n, [P, PAIRS, TOK], BF16) for n in ("o0h", "o0l"))
        pO = ps("pO", [P, 2, BANK])
        pX = ps("pX", [P, TT, BANK])
        whi, wlo, o_mm, o_hi, o_lo, x_mm, x_done = (
            sem("o0_" + n) for n in ("whi", "wlo", "o_mm", "o_hi", "o_lo", "x_mm", "x_done"))
        with nc.Block() as block:
            @block.gpsimd
            def _(pool):
                one = m.small[0:96, SMALL["onehot"]:SMALL["onehot"] + H]
                pool.tensor_copy(m.onehot[:, :, :], one.unsqueeze(2).broadcast_to([96, H, P])).then_inc(m.onehot_made, 1)

            @block.tensor
            def _(pe):
                for p in range(PAIRS + 1):
                    if p < PAIRS:
                        if p >= 2:
                            pe.wait_ge(o_lo, p - 1)
                        ops = ((wvh, 0, 0), (wvh, 0, 1), (wvl, 0, 0), (wvh, 1, 2), (wvl, 1, 2))
                        for a, (w, part, q) in enumerate(ops):
                            for h in range(2):
                                s = slice(NQ * h, NQ * h + NQ)
                                mov = m.quB[:, :, p, s] if q == 2 else m.quA[:, q, :, p, s]
                                mm = pe.matmul(pO[64 * h:64 * h + 64, p % 2, :].rearrange("p (b i) -> p b i", b=B),
                                               w[:, part, P * p + 64 * h:P * p + 64 * h + 64], mov,
                                               start=(a == 0), stop=(a == 4))
                        mm.then_inc(o_mm, 1)
                    if p >= 1:
                        pe.wait_ge(o_lo, p)
                        if p == 1:
                            pe.wait_ge(wlo, 1)
                        for t in range(TT):
                            s = slice(P * t, P * t + P)
                            for a, (o, w) in enumerate(((oh, woh), (oh, wol), (ol, woh))):
                                pe.matmul(pX[:, t, 0:D], o[:, p - 1, s], w[:, p - 1, :],
                                          start=(p == 1 and a == 0), stop=False)
                for t in range(TT):
                    pe.matmul(pX[:, t, 0:D], m.ones_row, m.bo0[:, :], start=False, stop=True).then_inc(x_mm, 1)

            @block.scalar
            def _(act):
                act.wait_ge(m.w0_loaded, m.w0_n)
                act.activation(woh[:, :, :], m.wo0[:, :, :], ACT.Copy).then_inc(whi, 1)
                for p in range(PAIRS):
                    act.wait_ge(o_mm, p + 1)
                    act.activation(oh[:, p, :], pO[:, p % 2, :], ACT.Copy).then_inc(o_hi, 1)

            @block.vector
            def _(dve):
                dve.wait_ge(whi, 1)
                dve.tensor_tensor(wol[:, :, :], m.wo0[:, :, :], woh[:, :, :], ALU.subtract).then_inc(wlo, 1)
                for p in range(PAIRS):
                    dve.wait_ge(o_hi, p + 1)
                    dve.tensor_tensor(ol[:, p, :], pO[:, p % 2, :], oh[:, p, :], ALU.subtract).then_inc(o_lo, 1)
                for t in range(TT):
                    dve.wait_ge(x_mm, t + 1)
                    dve.tensor_tensor(m.x[:, t, :], m.x[:, t, :], pX[:, t, 0:D], ALU.add).then_inc(x_done, 1)


def project(nc, m, tag, srcT, wm, bias_row, src=None, w=None):
    with ExitStack() as ctx:
        sb, ps, sem = names(nc, ctx)
        pX = ps(f"{tag}_pX", [P, TT, BANK])
        pT = ps(f"{tag}_pT", [P, KC, BANK])
        pW = ps(f"{tag}_pW", [P, 2, KC, BANK], BF16) if w is not None else None
        turned, copied, x_mm, x_done = (sem(f"{tag}_{n}") for n in ("turned", "copied", "x_mm", "x_done"))
        with nc.Block() as block:
            @block.tensor
            def _(pe):
                if src is not None:
                    for c in range(KC):
                        for t in range(TT):
                            pe.transpose(pT[:, c, P * t:P * t + P], src[:, t, P * c:P * c + P],
                                         m.ident[:, :]).then_inc(turned, 1)
                for c in range(KC):
                    if src is not None:
                        pe.wait_ge(copied, c + 1)
                    for t in range(TT):
                        mm = pe.matmul(pX[:, t, 0:D], srcT[:, c, P * t:P * t + P], wm[:, c, :], start=(c == 0),
                                       stop=(c == KC - 1 and bias_row is None))
                        if c == KC - 1 and bias_row is not None:
                            mm = pe.matmul(pX[:, t, 0:D], m.ones_row, bias_row, start=False, stop=True)
                        if c == KC - 1:
                            mm.then_inc(x_mm, 1)
                if w is not None:
                    w.turn(pe, pW)

            if src is not None:
                @block.scalar
                def _(act):
                    for c in range(KC):
                        act.wait_ge(turned, TT * (c + 1))
                        act.activation(srcT[:, c, :], pT[:, c, :], ACT.Copy).then_inc(copied, 1)

            @block.vector
            def _(dve):
                if w is not None:
                    w.round(dve, pW)
                for t in range(TT):
                    dve.wait_ge(x_mm, t + 1)
                    dve.tensor_tensor(m.x[:, t, :], m.x[:, t, :], pX[:, t, 0:D], ALU.add).then_inc(x_done, 1)


def heads16(nc, m, tag, qT, kT, vhl, o, gate, decay):
    with ExitStack() as ctx:
        sb, ps, sem = names(nc, ctx)
        R = 4
        qm = sb(f"{tag}_qm", [P, KC, 8, TOK])
        arg = sb(f"{tag}_arg", [P, 2, BANK])
        ex = sb(f"{tag}_ex", [P, 2, BANK])
        wt = sb(f"{tag}_wt", [P, R, BANK])
        wh = sb(f"{tag}_wh", [P, R, BANK], BF16)
        wl = sb(f"{tag}_wl", [P, R, BANK], BF16)
        o2 = sb(f"{tag}_o2", [P, TT, H, 16])
        pA = ps(f"{tag}_pA", [P, 2, BANK])
        pD = ps(f"{tag}_pD", [P, 2, BANK])
        pO = ps(f"{tag}_pO", [P, TT, H, 32])
        qm_dve, qm_act, qm_pool, a_mm, d_mm, arg_done, ex_done, wt_done, wh_done, wl_done, av_mm, o2_done, o_done, gated = (
            sem(f"{tag}_{n}") for n in ("qm_dve", "qm_act", "qm_pool", "a_mm", "d_mm", "arg_done", "ex_done", "wt_done",
                                        "wh_done", "wl_done", "av_mm", "o2_done", "o_done", "gated"))
        LAG = 3
        LATER = LAG + 1
        G = 4 * TT
        hmask = m.small[:, SMALL["hmask"]:SMALL["hmask"] + 8]
        with nc.Block() as block:
            @block.tensor
            def _(pe):
                for g in range(G + LAG):
                    if g < G:
                        t, q = g // 4, g % 4
                        s = slice(P * t, P * t + P)
                        if g < 4:
                            pe.wait_ge((qm_dve, qm_dve, qm_act, qm_pool)[g], 8 if g == 1 else 4)
                        if decay is not None:
                            if g >= 2:
                                pe.wait_ge(arg_done, g - 1)
                            F, nF = decay
                            pe.matmul(pD[:, g % 2, :], nF[:, s], m.late["onehot"][:, 4 * q:4 * q + 4, :].rearrange(
                                "p h r -> p (h r)"), start=True, stop=False)
                            for h in range(4):
                                mm = pe.matmul(pD[:, g % 2, P * h:P * h + P], m.late["onehot"][:, 4 * q + h, :], F[:, s],
                                               start=False, stop=(h == 3))
                            mm.then_inc(d_mm, 1)
                        if g >= 2:
                            pe.wait_ge(wt_done if decay is not None else ex_done, g - 1)
                        c = q // 2
                        pe.matmul(pA[:, g % 2, :].rearrange("p (h r) -> p h r", h=4), kT[:, c, s],
                                  qm[:, c, 4 * (q % 2):4 * (q % 2) + 4, s], start=True, stop=True).then_inc(a_mm, 1)
                    if g >= LAG:
                        v = g - LAG
                        t, q = v // 4, v % 4
                        pe.wait_ge(wh_done, v + 1)
                        pe.wait_ge(wl_done, v + 1)
                        for h in range(4):
                            n, s = 4 * q + h, slice(P * h, P * h + P)
                            pe.matmul(pO[:, t, n, :], wh[:, v % R, s], vhl[:, t, n, :], start=True, stop=False)
                            mm = pe.matmul(pO[:, t, n, 0:16], wl[:, v % R, s], vhl[:, t, n, 0:16],
                                           start=False, stop=True)
                        mm.then_inc(av_mm, 1)

            @block.scalar
            def _(act):
                def cast(g):
                    act.wait_ge(wt_done, g + 1)
                    if g >= R:
                        act.wait_ge(av_mm, g - R + 1)
                    act.activation(wh[:, g % R, :], wt[:, g % R, :], ACT.Copy).then_inc(wh_done, 1)

                def finish(t):
                    act.wait_ge(av_mm, 4 * (t + 1))
                    act.activation(o2[:, t, :, :], pO[:, t, :, 16:32], ACT.Copy).then_inc(o2_done, 1)

                for g in range(G):
                    if decay is not None:
                        act.wait_ge(arg_done, g + 1)
                        if g >= 2:
                            act.wait_ge(wt_done, g - 1)
                        act.activation(ex[:, g % 2, :], arg[:, g % 2, :], ACT.Exp).then_inc(ex_done, 1)
                    else:
                        act.wait_ge(a_mm, g + 1)
                        if g >= 2:
                            act.wait_ge(wt_done, g - 1)
                        act.activation(ex[:, g % 2, :], pA[:, g % 2, :], ACT.Tanh, bias=m.tanh_bias,
                                       scale=15.0).then_inc(ex_done, 1)
                    if g == 0:
                        for n in range(4):
                            act.activation(qm[:, 1, n, :], qT[:, 1, :], ACT.Copy, scale=hmask[:, n:n + 1]).then_inc(qm_act, 1)
                    if g >= 1:
                        cast(g - 1)
                    if g > LATER and (g - LATER) % 4 == 0:
                        finish((g - LATER) // 4 - 1)
                cast(G - 1)
                for t in range((G - 1 - LATER) // 4, TT):
                    finish(t)

            @block.vector
            def _(dve):
                def finish(t):
                    o4 = o[:, t, :].rearrange("p (h e) -> p h e", h=H)
                    dve.wait_ge(o2_done, t + 1)
                    dve.tensor_tensor(o4, pO[:, t, :, 0:16], o2[:, t, :, :], ALU.add).then_inc(o_done, 1)
                    dve.wait_ge(o_done, t + 1)
                    dve.tensor_tensor(o4, o4, gate(t), ALU.mult).then_inc(gated, 1)

                for n in range(8):
                    dve.tensor_scalar(qm[:, 0, n, :], qT[:, 0, :], hmask[:, n:n + 1], None, ALU.mult).then_inc(qm_dve, 1)
                for g in range(G + 1):
                    if decay is not None and g < G:
                        dve.wait_ge(d_mm, g + 1)
                        if g >= 2:
                            dve.wait_ge(ex_done, g - 1)
                        dve.tensor_tensor(arg[:, g % 2, :], pD[:, g % 2, :], m.maskneg[:, :], ALU.min).then_inc(arg_done, 1)
                    if g >= 1:
                        r, k = (g - 1) % 2, (g - 1) % R
                        dve.wait_ge(ex_done, g)
                        if g > R:
                            dve.wait_ge(wl_done, g - R)
                            dve.wait_ge(wh_done, g - R)
                        if decay is not None:
                            dve.wait_ge(a_mm, g)
                            dve.tensor_tensor(wt[:, k, :], pA[:, r, :], ex[:, r, :], ALU.mult).then_inc(wt_done, 1)
                        else:
                            dve.scalar_tensor_tensor(wt[:, k, :], ex[:, r, :], 1.0, m.mask05[:, :], ALU.add,
                                                     ALU.mult).then_inc(wt_done, 1)
                    if g > LATER and (g - LATER) % 4 == 0:
                        finish((g - LATER) // 4 - 1)
                for t in range((G - LATER) // 4, TT):
                    finish(t)

            @block.gpsimd
            def _(pool):
                for n in range(4, 8):
                    pool.tensor_scalar(qm[:, 1, n, :], qT[:, 1, :], hmask[:, n:n + 1], None, ALU.mult).then_inc(qm_pool, 1)
                for g in range(G):
                    pool.wait_ge(wh_done, g + 1)
                    if g >= R:
                        pool.wait_ge(av_mm, g - R + 1)
                    pool.tensor_tensor(wl[:, g % R, :], wt[:, g % R, :], wh[:, g % R, :], ALU.subtract).then_inc(wl_done, 1)


def l0_gla(nc, m, d):
    with ExitStack() as ctx:
        sb, ps, sem = names(nc, ctx)
        qT = sb("gl_qT", [P, KC, TOK])
        kv = sb("gl_kv", [P, TT, 2 * D])
        sq = sb("gl_sq", [P, TT, D])
        ssq = sb("gl_ssq", [P, TT, H])
        nrm = sb("gl_nrm", [P, TT, H])
        inv = sb("gl_inv", [P, TT, H])
        kn = sb("gl_kn", [P, TT, D])
        kT = sb("gl_kT", [P, KC, TOK])
        vhl = sb("gl_vhl", [P, TT, H, 32], BF16)
        g1 = sb("gl_g1", [16, TOK])
        gate = sb("gl_gate", [P, TT, D])
        o = sb("gl_o", [P, TT, D])
        F = sb("gl_F", [96, TOK], BF16)
        nF = sb("gl_nF", [96, TOK], BF16)
        with ExitStack() as c2:
            sb2, ps2, sem2 = names(nc, c2)
            fa = sb2("gl_fa", [96, TOK])
            fe = sb2("gl_fe", [96, TOK])
            fl = sb2("gl_fl", [96, TOK])
            fs = sb2("gl_fs", [96, TOK])
            fc = sb2("gl_fc", [96, TOK])
            fr = sb2("gl_fr", [96, TOK])
            f1 = sb2("gl_f1", [96, TOK], BF16)
            pq = ps2("gl_pq", [P, KC, BANK])
            pkv = ps2("gl_pkv", [P, TT, BANK])
            pf = ps2("gl_pf", [P, BANK])
            pg = ps2("gl_pg", [P, BANK])
            (q_mm, kv_mm, f_mm, g1_mm, q_done, kv_done, fabs, fexp, fln, g1_done, gt_mm, gate_done, sq_done, ssq_done,
             nrm_done, inv_done, kn_done, kt_mm, kt_done, fchain, v_hi, v_lo) = (sem2("gl_" + n) for n in (
                 "q_mm", "kv_mm", "f_mm", "g1_mm", "q_done", "kv_done", "fabs", "fexp", "fln", "g1_done", "gt_mm",
                 "gate_done", "sq_done", "ssq_done", "nrm_done", "inv_done", "kn_done", "kt_mm", "kt_done", "fchain",
                 "v_hi", "v_lo"))
            with nc.Block() as block:
                @block.tensor
                def _(pe):
                    loaded(m, pe, "gl")
                    for c in range(KC):
                        mm = pe.matmul(pf[0:96, :], m.late["gl_wf"][:, c, :], m.xnT[:, c, :], start=(c == 0), stop=(c == KC - 1))
                    mm.then_inc(f_mm, 1)
                    for c in range(KC):
                        mm = pe.matmul(pg[0:16, :], m.late["gl_g1"][:, c, :], m.xnT[:, c, :], start=(c == 0), stop=(c == KC - 1))
                    mm.then_inc(g1_mm, 1)
                    for t in range(TT):
                        for c in range(KC):
                            mm = pe.matmul(pkv[:, t, :], m.xnT[:, c, P * t:P * t + P], m.late["gl_wkv"][:, c, :],
                                           start=(c == 0), stop=(c == KC - 1))
                        mm.then_inc(kv_mm, 1)
                    for n in range(KC):
                        for c in range(KC):
                            mm = pe.matmul(pq[:, n, :], m.late["gl_wq"][:, c, P * n:P * n + P], m.xnT[:, c, :],
                                           start=(c == 0), stop=(c == KC - 1))
                        mm.then_inc(q_mm, 1)
                    pe.wait_ge(g1_done, 1)
                    pe.wait_ge(q_done, 2)
                    for t in range(TT):
                        pe.matmul(pq[:, t // 2, D * (t % 2):D * (t % 2) + D], g1[:, P * t:P * t + P], m.late["gl_g2"][:, :],
                                  start=True, stop=True).then_inc(gt_mm, 1)
                    pe.wait_ge(kn_done, 1)
                    for c in range(KC):
                        for t in range(TT):
                            mm = pe.transpose(pkv[:, c, P * t:P * t + P], kn[:, t, P * c:P * c + P], m.ident[:, :])
                        mm.then_inc(kt_mm, 1)

                @block.scalar
                def _(act):
                    act.wait_ge(f_mm, 1)
                    act.activation(fa[:, :], pf[0:96, :], ACT.Abs).then_inc(fabs, 1)
                    act.wait_ge(fabs, 1)
                    act.activation(fe[:, :], fa[:, :], ACT.Exp, scale=-1.0).then_inc(fexp, 1)
                    act.wait_ge(fexp, 1)
                    act.activation(fl[:, :], fe[:, :], ACT.Ln, bias=m.one[0:96, :]).then_inc(fln, 1)
                    act.wait_ge(g1_mm, 1)
                    act.activation(g1[:, :], pg[0:16, :], ACT.Copy).then_inc(g1_done, 1)
                    for t in range(TT):
                        act.wait_ge(kv_mm, t + 1)
                        act.activation(kv[:, t, :], pkv[:, t, :], ACT.Silu).then_inc(kv_done, 1)
                    for n in range(KC):
                        act.wait_ge(q_mm, n + 1)
                        act.activation(qT[:, n, :], pq[:, n, :], ACT.Silu).then_inc(q_done, 1)
                    act.wait_ge(ssq_done, 1)
                    act.activation(nrm[:, :, :], ssq[:, :, :], ACT.Sqrt).then_inc(nrm_done, 1)
                    act.wait_ge(gt_mm, TT)
                    for n in range(2):
                        act.activation(gate[:, 2 * n:2 * n + 2, :], pq[:, n, :].rearrange("p (t f) -> p t f", t=2),
                                       ACT.Sigmoid).then_inc(gate_done, 1)
                    act.wait_ge(kt_mm, 1)
                    act.activation(kT[:, 0, :], pkv[:, 0, :], ACT.Copy).then_inc(kt_done, 1)

                @block.vector
                def _(dve):
                    k4 = kv[:, :, 0:D]
                    dve.wait_ge(fln, 1)
                    link = chained(dve, fchain)
                    link(dve.scalar_tensor_tensor(fs[:, :], pf[0:96, :], 0.0, fl[:, :], ALU.min, ALU.subtract))
                    link(dve.tensor_tensor_scan(fc[:, :], m.late["gl_scanmask"][0:96, :], fs[:, :], 0.0, ALU.mult, ALU.add))
                    link(dve.tensor_copy(f1[:, :], fc[:, :]))
                    link(dve.tensor_tensor(fr[:, :], fc[:, :], f1[:, :], ALU.subtract))
                    link(dve.tensor_copy(F[:, :], fr[:, :]))
                    link(dve.tensor_tensor(fa[:, :], fr[:, :], F[:, :], ALU.subtract))
                    link(dve.tensor_copy(F[0:32, :], f1[0:32, :]))
                    link(dve.tensor_copy(F[64:96, :], fa[64:96, :]))
                    link(dve.tensor_scalar(nF[:, :], F[:, :], -1.0, None, ALU.mult))
                    dve.wait_ge(kv_done, TT)
                    dve.tensor_tensor(sq[:, :, :], k4, k4, ALU.mult).then_inc(sq_done, 1)
                    dve.wait_ge(sq_done, 1)
                    dve.tensor_reduce(ssq[:, :, :], sq[:, :, :].rearrange("p t (h e) -> p t h e", h=H), AX_X,
                                      ALU.add).then_inc(ssq_done, 1)
                    dve.wait_ge(nrm_done, 1)
                    dve.tensor_scalar(nrm[:, :, :], nrm[:, :, :], 1e-12, None, ALU.max).then_inc(inv_done, 1)
                    dve.wait_ge(inv_done, 1)
                    dve.reciprocal(inv[:, :, :], nrm[:, :, :]).then_inc(inv_done, 1)
                    dve.wait_ge(inv_done, 2)
                    dve.tensor_tensor(kn[:, :, :].rearrange("p t (h e) -> p t h e", h=H),
                                      k4.rearrange("p t (h e) -> p t h e", h=H),
                                      inv[:, :, :].unsqueeze(3).broadcast_to([P, TT, H, 16]), ALU.mult).then_inc(kn_done, 1)
                    dve.wait_ge(kt_mm, 2)
                    dve.tensor_copy(kT[:, 1, :], pkv[:, 1, :]).then_inc(kt_done, 1)

                @block.gpsimd
                def _(pool):
                    v4 = kv[:, :, D:2 * D].rearrange("p t (h e) -> p t h e", h=H)
                    pool.wait_ge(kv_done, TT)
                    for t in range(TT):
                        pool.tensor_copy(vhl[:, t, :, 0:16], v4[:, t]).then_inc(v_hi, 1)
                    for t in range(TT):
                        pool.wait_ge(v_hi, t + 1)
                        pool.tensor_tensor(vhl[:, t, :, 16:32], v4[:, t], vhl[:, t, :, 0:16], ALU.subtract).then_inc(v_lo, 1)
        heads16(nc, m, "gh", qT, kT, vhl, o, lambda t: gate[:, t, :].rearrange("p (h e) -> p h e", h=H), (F, nF))
        layer_norm(nc, m, "lng", o, kn, kT, (m.late["gl_lnw"][:, :], None, "gl"))
        project(nc, m, "gp", kT, m.late["gl_wo"], None)


def l0_moe(nc, m, d, early):
    with ExitStack() as ctx:
        sb, ps, sem = names(nc, ctx)
        mask = sb("mo_mask", [P, TT, E])
        xs = sb("mo_xs", [P, TT, D])
        xh, xl = (sb("mo_" + n, [P, KC, TOK], BF16) for n in ("xh", "xl"))
        parts = {}
        for n, shape in (("wg", [P, E, KC, I]), ("wu", [P, E, KC, I]), ("wd", [P, E, D])):
            parts[n] = [sb(f"mo_{n}{part}", shape, BF16) for part in ("h", "l")]
        w_hi, w_lo = sem("mo_w_hi"), sem("mo_w_lo")

        def weights(e):
            for n, (h, l) in parts.items():
                yield m.late["mo_" + n][:, e], h[:, e], l[:, e]

        def low_weights(pool, e):
            for n, (src, h, l) in enumerate(weights(e)):
                pool.wait_ge(w_hi, 3 * e + n + 1)
                pool.tensor_tensor(l, src, h, ALU.subtract).then_inc(w_lo, 1)

        with ExitStack() as c2:
            sb2, ps2, sem2 = names(nc, c2)
            lg = sb2("mo_lg", [P, TT, E])
            top = sb2("mo_top", [P, TT])
            rw = sb2("mo_rw", [P, TT])
            eq = sb2("mo_eq", [P, TT, E])
            cand = sb2("mo_cand", [P, TT, E])
            best = sb2("mo_best", [P, TT])
            pL = ps2("mo_pL", [P, TT * E])
            pT = ps2("mo_pT", [P, KC, BANK])
            l_mm, chain, rw_done, xs_done, turned, copied, xl_done = (
                sem2("mo_" + n) for n in ("l_mm", "chain", "rw_done", "xs_done", "turned", "copied", "xl_done"))
            with nc.Block() as block:
                @block.tensor
                def _(pe):
                    loaded(m, pe, "mo")
                    for t in range(TT):
                        for c in range(KC):
                            mm = pe.matmul(pL[:, E * t:E * t + E], m.xnT[:, c, P * t:P * t + P], m.late["mo_gate"][:, c, :],
                                           start=(c == 0), stop=(c == KC - 1))
                    mm.then_inc(l_mm, 1)
                    pe.wait_ge(xs_done, TT)
                    for c in range(KC):
                        for t in range(TT):
                            mm = pe.transpose(pT[:, c, P * t:P * t + P], xs[:, t, P * c:P * c + P], m.ident[:, :])
                        mm.then_inc(turned, 1)

                @block.gpsimd
                def _(pool):
                    for e in range(E // 2):
                        low_weights(pool, e)

                @block.scalar
                def _(act):
                    loaded(m, act, "mo")
                    for e in range(E // 2):
                        for src, h, _ in weights(e):
                            act.activation(h, src, ACT.Copy).then_inc(w_hi, 1)
                    act.wait_ge(chain, 2)
                    act.activation(rw[:, :], top[:, :], ACT.Sigmoid).then_inc(rw_done, 1)
                    for e in range(E // 2, E):
                        for src, h, _ in weights(e):
                            act.activation(h, src, ACT.Copy).then_inc(w_hi, 1)
                    for c in range(KC):
                        act.wait_ge(turned, c + 1)
                        act.activation(xh[:, c, :], pT[:, c, :], ACT.Copy).then_inc(copied, 1)

                @block.vector
                def _(dve):
                    dve.wait_ge(l_mm, 1)
                    def wide(a):
                        return a[:, :].unsqueeze(2).broadcast_to([P, TT, E])
                    desc = m.small[:, SMALL["desc"]:SMALL["desc"] + E].unsqueeze(1).broadcast_to([P, TT, E])
                    link = chained(dve, chain)
                    link(dve.tensor_copy(lg[:, :, :], pL[:, :].rearrange("p (t e) -> p t e", e=E)))
                    link(dve.tensor_reduce(top[:, :], lg[:, :, :], AX_X, ALU.max))
                    link(dve.tensor_tensor(eq[:, :, :], lg[:, :, :], wide(top), ALU.is_equal))
                    link(dve.tensor_tensor(cand[:, :, :], eq[:, :, :], desc, ALU.mult))
                    link(dve.tensor_reduce(best[:, :], cand[:, :, :], AX_X, ALU.max))
                    link(dve.tensor_tensor(mask[:, :, :], cand[:, :, :], wide(best), ALU.is_equal))
                    dve.wait_ge(rw_done, 1)
                    for t in range(TT):
                        dve.tensor_scalar(xs[:, t, :], m.xn[:, t, :], rw[:, t:t + 1], None, ALU.mult).then_inc(xs_done, 1)
                    for c in range(KC):
                        dve.wait_ge(copied, c + 1)
                        dve.tensor_tensor(xl[:, c, :], pT[:, c, :], xh[:, c, :], ALU.subtract).then_inc(xl_done, 1)
        sg = sb("mo_sg", [P, 2, TOK])
        hT = sb("mo_hT", [P, 2, TOK])
        hh, hl = (sb("mo_" + n, [P, 2, TOK], BF16) for n in ("hh", "hl"))
        pG = ps("mo_pG", [P, 2, BANK])
        pU = ps("mo_pU", [P, 2, BANK])
        pD = ps("mo_pD", [P, TT, BANK])
        g_mm, u_mm, sg_done, h_done, hh_done, hl_done, d_mm, x_done = (
            sem("mo_" + n) for n in ("g_mm", "u_mm", "sg_done", "h_done", "hh_done", "hl_done", "d_mm", "x_done"))
        with nc.Block() as block:
            @block.sync
            def _(sp):
                load_context(sp, d, early, 0)

            @block.gpsimd
            def _(pool):
                for e in range(E // 2, E):
                    low_weights(pool, e)
                pool.wait_ge(w_lo, 3 * E)
                early.prepare(pool, m)

            @block.tensor
            def _(pe):
                for e in range(E + 1):
                    if e < E:
                        if e >= 2:
                            pe.wait_ge(h_done, e - 1)
                        pe.wait_ge(w_lo, 3 * (e + 1))
                        for (wh, wl), o, s in ((parts["wg"], pG, g_mm), (parts["wu"], pU, u_mm)):
                            for c in range(KC):
                                for a, (w, x) in enumerate(((wh, xh), (wh, xl), (wl, xh))):
                                    mm = pe.matmul(o[:, e % 2, :], w[:, e, c, :], x[:, c, :], start=(c == 0 and a == 0),
                                                   stop=(c == KC - 1 and a == 2))
                            mm.then_inc(s, 1)
                    if e >= 1:
                        pe.wait_ge(hl_done, e)
                        wh, wl = parts["wd"]
                        for t in range(TT):
                            if e >= 2:
                                pe.wait_ge(x_done, TT * (e - 2) + t + 1)
                            for a, (h, w) in enumerate(((hh, wh), (hh, wl), (hl, wh))):
                                mm = pe.matmul(pD[:, t, 0:D], h[:, (e - 1) % 2, P * t:P * t + P], w[:, e - 1, :],
                                               start=(a == 0), stop=(a == 2))
                            mm.then_inc(d_mm, 1)

            @block.scalar
            def _(act):
                for e in range(E):
                    act.wait_ge(g_mm, e + 1)
                    if e >= 2:
                        act.wait_ge(h_done, e - 1)
                    act.activation(sg[:, e % 2, :], pG[:, e % 2, :], ACT.Silu).then_inc(sg_done, 1)
                    act.wait_ge(h_done, e + 1)
                    if e >= 2:
                        act.wait_ge(d_mm, TT * (e - 1))
                    act.activation(hh[:, e % 2, :], hT[:, e % 2, :], ACT.Copy).then_inc(hh_done, 1)

            @block.vector
            def _(dve):
                for e in range(E + 1):
                    if e < E:
                        dve.wait_ge(u_mm, e + 1)
                        dve.wait_ge(sg_done, e + 1)
                        if e >= 2:
                            dve.wait_ge(hl_done, e - 1)
                        dve.tensor_tensor(hT[:, e % 2, :], pU[:, e % 2, :], sg[:, e % 2, :], ALU.mult).then_inc(h_done, 1)
                        dve.wait_ge(hh_done, e + 1)
                        dve.tensor_tensor(hl[:, e % 2, :], hT[:, e % 2, :], hh[:, e % 2, :], ALU.subtract).then_inc(hl_done, 1)
                    if e >= 1:
                        for t in range(TT):
                            n = TT * (e - 1) + t
                            dve.wait_ge(d_mm, n + 1)
                            if e >= 2:
                                dve.wait_ge(x_done, n - TT + 1)
                            dve.scalar_tensor_tensor(m.x[:, t, :], pD[:, t, 0:D], mask[:, t, e - 1:e], m.x[:, t, :],
                                                     ALU.mult, ALU.add).then_inc(x_done, 1)


NSPLIT = 4


class ContextL1:
    def __init__(self, sb, sem):
        self.wh = sb("x1_wh", [P, 2, 2 * D], BF16)
        self.wl = sb("x1_wl", [P, 2, 2 * D], BF16)
        self.wB = sb("x1_wB", [P, 2 * D], BF16)
        self.stA = sb("x1_stA", [P, M])
        self.stB = sb("x1_stB", [P, M])
        self.hl = [Parts(sb, "x1_ctx0", False)]
        self.ctx_in, self.begun, self.split, self.wparts = (
            sem("x1_" + n) for n in ("ctx_in", "begun", "split", "wparts"))

    def prepare(self, pool, m):
        loaded(m, pool, "x1")
        w = m.late["x1_wkv"]
        pool.tensor_copy(self.wh[:, :, :], w[:, :, :]).then_inc(self.wparts, 1)
        pool.wait_ge(self.wparts, 1)
        pool.tensor_tensor(self.wl[:, :, :], w[:, :, :], self.wh[:, :, :], ALU.subtract).then_inc(self.wparts, 1)
        pool.tensor_copy(self.wB[0:64, :], self.wh[0:64, 1, :]).then_inc(self.wparts, 1)
        pool.wait_ge(self.wparts, 2)
        pool.tensor_copy(self.wB[64:128, :], self.wl[64:128, 1, :]).then_inc(self.wparts, 1)
        pool.wait_ge(self.wparts, 4)
        pool.sem_inc(self.split, 1)
        split_context(pool, self, 0, self.hl[0])


def load_context(sp, d, c, b):
    sp.dma_start(c.stA[:, :], d["ctxT"][bass.ds(b, 1), 0:P].rearrange("o p c -> (o p) c")).then_inc(c.ctx_in, 16)
    for s in (0, 64):
        sp.dma_start(c.stB[s:s + 64, :], d["ctxT"][bass.ds(b, 1), P:DC].rearrange("o p c -> (o p) c")).then_inc(c.ctx_in, 16)


def split_context(pool, c, b, o):
    pool.wait_ge(c.ctx_in, (b + 1) * 48)
    pool.sem_inc(c.begun, 1)
    parts = ((o.ah[:, 0:M], o.al[:, 0:M], c.stA[:, :]), (o.bh[:, 0:M], o.bl[:, 0:M], c.stB[:, :]))
    for hi, _, src in parts:
        pool.tensor_copy(hi, src).then_inc(c.split, 1)
    for n, (hi, lo, src) in enumerate(parts):
        pool.wait_ge(c.split, 1 + b * NSPLIT + n + 1)
        pool.tensor_tensor(lo, src, hi, ALU.subtract).then_inc(c.split, 1)


def l1x_tiles(nc, m, d, c0, oT):
    SCALE = 16 ** -0.5
    T2 = 2 * PAIRS
    with ExitStack() as ctx:
        sb, ps, sem = names(nc, ctx)
        hl, split, wh, wl, wB = c0.hl, c0.split, c0.wh, c0.wl, c0.wB
        qT = oT
        qch, qcl = (sb("x1_" + n, [P, KC, B, 2, NQ], BF16) for n in ("qch", "qcl"))
        qs = sb("x1_qs", [P, PAIRS, B, P], BF16)
        ks = sb("x1_ks", [P, PAIRS, M + 1], BF16)
        kh, kl = (sb("x1_" + n, [P, KC, M + 1], BF16) for n in ("kh", "kl"))
        vhl = [sb(f"x1_vhl{par}", [P, MC, PAIRS, 64], BF16) for par in range(2)]
        prob = sb("x1_prob", [P, 2, M])
        pth = sb("x1_pth", [P, 2, MC, P], BF16)
        ptl = sb("x1_ptl", [P, 2, MC, P], BF16)
        mx = sb("x1_mx", [P, 2])
        nmax = sb("x1_nmax", [P, 2])
        rsum = sb("x1_rsum", [P, 2])
        rinv = sb("x1_rinv", [P, 2])
        u = sb("x1_u", [P, 2, 2, PAIRS, 32])
        pS = ps("x1_pS", [P, 4 * BANK])
        pT = ps("x1_pT", [P, 2, BANK])
        pK = ps("x1_pK", [P, BANK])
        pUF = ps("x1_pUF", [P, BANK])
        pU = pUF[:, 0:64]
        pF = pUF[:, 64:64 + KC * NQ].rearrange("p (n i) -> p n i", n=KC)
        (kv_mm, kv_hi, kv_lo, s_done, exp_done, t_done, hi_done, lo_done, av_done,
         mx_done, nmax_done, rinv_done, u_done, f_mm, f_done) = (sem("x1_" + n) for n in (
             "kv_mm", "kv_hi", "kv_lo", "s_done", "exp_done", "t_done",
             "hi_done", "lo_done", "av_done", "mx_done", "nmax_done", "rinv_done", "u_done", "f_mm", "f_done"))
        q_mm, q_done, qch_done, qcl_done = (sem("x1_" + n) for n in ("q_mm", "q_done", "qch_done", "qcl_done"))
        ks_in = [sem(f"x1_ks_in{p}") for p in range(PAIRS)]
        qs_in = [sem(f"x1_qs_in{j}") for j in range(4)]
        parity = m.small[:, SMALL["parity"]:SMALL["parity"] + 2]

        def by_batch(a):
            return a.rearrange("p (b i) -> p b i", b=B)

        VG = [range(2 * n, min(2 * n + 2, MC)) for n in range(-(-MC // 2))]
        PIECES = [("k", n, j) for n in range(KC) for j in range(len(SEG))] + [("v", n, cs) for n, cs in enumerate(VG)]
        NP = len(PIECES)
        NKP = KC * len(SEG)
        rowmask = m.small[:, SMALL["rowmask"]:SMALL["rowmask"] + 64].rearrange("p (a c) -> p a c", a=2)
        fold = m.small[:, SMALL["fold"]:SMALL["fold"] + NQ]

        def beside(t, half):
            i = 2 * (t % PAIRS) + half
            return i if 0 <= t < T2 and i < NP else None

        def bodies(eng, body):
            body(0, True, False)
            with eng.Fori(1, B // 2 - 1) as i:
                body(i * 2, False, False)
            body(B - 2, False, True)

        with nc.Block() as block:
            @block.sync
            def _(sp):
                def stack_queries(j):
                    for r, src in enumerate((qch, qch, qcl, qcl)):
                        sp.dma_start(qs[32 * r:32 * r + 32, j:PAIRS:4, :, :], src[32 * j:32 * j + 32, :, :, :, :].rearrange(
                            "p n b e i -> p n b (e i)")).then_inc(qs_in[j], 16)

                def stack_keys(b, first, pairs=range(PAIRS)):
                    for p in pairs:
                        n, j = p // 4, p % 4
                        if j == 0:
                            sp.wait_ge(kv_lo, 1 + b * NP + len(SEG) * (n + 1))
                        if not first:
                            sp.wait_ge(s_done, 1 + (b * PAIRS - PAIRS + p + 1) * 2)
                        for r, src in enumerate((kh, kl, kh, kl)):
                            sp.dma_start(ks[32 * r:32 * r + 32, p, 0:M], src[32 * j:32 * j + 32, n, 0:M]).then_inc(ks_in[p], 16)

                def next_context(b):
                    sp.wait_ge(split, 1 + b * NSPLIT)
                    load_context(sp, d, c0, b)

                next_context(1)
                sp.wait_ge(qcl_done, 2 * KC)
                stack_queries(0)
                stack_queries(1)
                stack_keys(0, True, range(4))
                stack_queries(2)
                stack_queries(3)
                stack_keys(0, True, range(4, PAIRS))
                with sp.Fori(1, B - 1) as b:
                    next_context(b + 1)
                    stack_keys(b, False)
                stack_keys(B - 1, False)

            @block.gpsimd
            def _(pool):
                split_context(pool, c0, 1, hl[1])
                with pool.Fori(1, B // 2) as i:
                    b = i * 2
                    for par in range(2):
                        pool.wait_ge(kv_mm, 1 + (b + par - 1) * NP)
                        split_context(pool, c0, b + par, hl[par])

            @block.tensor
            def _(pe):
                for s in (s_done, t_done, av_done, kv_mm, f_mm):
                    pe.sem_inc(s, 1)

                def piece(b, par, i, dst, ahead):
                    c = hl[par]
                    if i == 0:
                        pe.wait_ge(split, 1 + (b + 1) * NSPLIT)
                    pe.wait_ge(kv_lo, 1 + b * NP + max(i - ahead, 0))
                    kind, n, x = PIECES[i]
                    if kind == "k":
                        w = slice(P * n, P * n + P)
                        s, z = SEG[x]
                        for a, (st, mv) in enumerate(((wh[:, 0, w], c.ah), (wh[:, 0, w], c.al), (wl[:, 0, w], c.ah),
                                                      (wB[:, w], c.bh), (wB[:, w], c.bl))):
                            mm = pe.matmul(dst[:, 0:z], st, mv[:, s:s + z], start=(a == 0), stop=(a == 4))
                    else:
                        w = slice(D, 2 * D)
                        for ch in x:
                            r = min(P, M - P * ch)
                            s = slice(P * ch, P * ch + r)
                            o = dst[0:r, D * (ch % 2):D * (ch % 2) + D]
                            for a, (st, mv) in enumerate(((c.ah, wh[:, 0, w]), (c.ah, wl[:, 0, w]), (c.al, wh[:, 0, w]),
                                                          (c.bh, wB[:, w]), (c.bl, wB[:, w]))):
                                mm = pe.matmul(o, st[:, s], mv, start=(a == 0), stop=(a == 4))
                    mm.then_inc(kv_mm, 1)

                def body(b, first, last):
                    k0 = b * PAIRS
                    least = 0 if first else -9

                    def scores(t, j):
                        par, p = t // PAIRS, t % PAIRS
                        s, w = SEG[j]
                        if j == 0:
                            pe.wait_ge(exp_done, 1 + k0 + t)
                            pe.wait_ge(ks_in[p], (b + par + 1) * 64)
                            if first and t < 4:
                                pe.wait_ge(qs_in[t], 64)
                        mm = pe.matmul(pS[:, s:s + w], qs[:, p, bass.ds(b + par, 1), :].rearrange("p o r -> p (o r)"),
                                       ks[:, p, s:s + w], start=True, stop=True)
                        if j in (1, 3):
                            mm.then_inc(s_done, 1)

                    def turn_probs(t, g):
                        n = 4 * t + g
                        if g == 0:
                            pe.wait_ge(exp_done, 1 + k0 + t + 1)
                        pe.wait_ge(lo_done, 1 + k0 * NG + max(n - 1, least))
                        for ch in TGRP[g][1]:
                            w = min(P, M - P * ch)
                            mm = pe.transpose(pT[0:w, n % 2, P * (ch % 4):P * (ch % 4) + P], prob[:, t % 2, P * ch:P * ch + w],
                                              m.ident[:, :])
                        mm.then_inc(t_done, 1)

                    def values(t):
                        par, p = t // PAIRS, t % PAIRS
                        pe.wait_ge(u_done, 1 + k0 + t)
                        pe.wait_ge(lo_done, 1 + (k0 + t + 1) * NG)
                        if p == 0:
                            pe.wait_ge(kv_lo, 1 + (b + par + 1) * NP)
                            pe.wait_ge(f_done, 1 + (b + par) * KC)
                        for n in range(MC):
                            w = min(P, M - P * n)
                            pe.matmul(pU, pth[0:w, t % 2, n, :], vhl[par % 2][0:w, n, p, :], start=(n == 0), stop=False)
                            mm = pe.matmul(pU[:, 0:32], ptl[0:w, t % 2, n, :], vhl[par % 2][0:w, n, p, 0:32], start=False,
                                           stop=(n == MC - 1))
                        mm.then_inc(av_done, 1)

                    def fold_rows(par):
                        pe.wait_ge(u_done, 1 + k0 + (par + 1) * PAIRS)
                        for n in range(KC):
                            for a in range(2):
                                mm = pe.matmul(pF[:, n, :], u[:, par % 2, a, 4 * n:4 * n + 4, :].rearrange("p a c -> p (a c)"), fold,
                                               start=(a == 0), stop=(a == 1))
                        mm.then_inc(f_mm, 1)

                    def beside_piece(t, half):
                        i = beside(t, half)
                        par = t // PAIRS
                        if i is not None and not (last and par):
                            piece(b + par + 1, 1 - par, i, pK, 0)

                    for t in range(T2 + 3 if last else T2):
                        now, before = t < T2, least + 1 <= t <= T2
                        if now:
                            scores(t, 0)
                            scores(t, 1)
                        if t - 3 >= least and (t - 3) % PAIRS == PAIRS - 1:
                            fold_rows((t - 3) // PAIRS)
                        if before:
                            turn_probs(t - 1, 0)
                        beside_piece(t, 0)
                        if now:
                            scores(t, 2)
                            scores(t, 3)
                        if before:
                            turn_probs(t - 1, 1)
                            turn_probs(t - 1, 2)
                        if least + 2 <= t <= T2 + 1:
                            values(t - 2)
                        beside_piece(t, 1)
                        if before:
                            turn_probs(t - 1, 3)

                for n in range(KC):
                    for c in range(KC):
                        mm = pe.matmul(pT[:, n, :], m.late["x1_wq"][:, c, P * n:P * n + P], m.xnT[:, c, :], start=(c == 0),
                                       stop=(c == KC - 1))
                    mm.then_inc(q_mm, 1)
                for i in range(NP):
                    piece(0, 0, i, pS[:, BANK * (i % 4):BANK * (i % 4) + BANK], 3)
                pe.wait_ge(kv_lo, 1 + NP)
                pe.wait_ge(q_done, KC)
                bodies(pe, body)

            @block.scalar
            def _(act):
                for s in (exp_done, hi_done, kv_hi, f_done):
                    act.sem_inc(s, 1)

                def piece(b, par, i, src, ahead):
                    act.wait_ge(kv_mm, 1 + b * NP + i + 1)
                    kind, n, x = PIECES[i]
                    if kind == "k":
                        s, z = SEG[x]
                        if x == 0 and ahead:
                            for p in range(4 * n, 4 * n + 4):
                                act.wait_ge(ks_in[p], b * 64)
                        act.activation(kh[:, n, s:s + z], src[:, 0:z], ACT.Identity,
                                       bias=m.late["x1_bk"][:, n:n + 1]).then_inc(kv_hi, 1)
                    else:
                        r = min(P, M - P * x[0])
                        act.activation(vhl[par][0:r, x[0]:x[-1] + 1, :, 0:32], src[0:r, 0:D * len(x)].rearrange(
                            "p (c a e) -> p c a e", a=PAIRS, e=32), ACT.Copy).then_inc(kv_hi, 1)

                def body(b, first, last):
                    k0 = b * PAIRS
                    least = 0 if first else -9

                    def high_probs(t, g):
                        cs = TGRP[g][1]
                        n = 4 * t + g
                        w = min(P, M - P * cs[0])
                        if g == 0:
                            act.wait_ge(av_done, 1 + k0 + max(t - 1, least))
                        act.wait_ge(t_done, 1 + (k0 + t) * NG + g + 1)
                        act.activation(pth[0:w, t % 2, cs[0]:cs[-1] + 1, :], pT[0:w, n % 2, 0:P * len(cs)].rearrange(
                            "p (c r) -> p c r", r=P), ACT.Copy).then_inc(hi_done, 1)

                    def beside_piece(t, half):
                        i = beside(t, half)
                        par = t // PAIRS
                        if i is not None and not (last and par):
                            if i == NKP:
                                act.wait_ge(av_done, 1 + k0 + par * PAIRS)
                            piece(b + par + 1, 1 - par, i, pK, True)

                    for t in range(T2 + 3 if last else T2):
                        now, before = t < T2, least + 1 <= t <= T2
                        if t - 3 >= least and (t - 3) % PAIRS == PAIRS - 1:
                            par = (t - 3) // PAIRS
                            act.wait_ge(f_mm, 1 + b + par + 1)
                            for n in range(KC):
                                act.activation(oT[:, n, bass.ds((b + par) * NQ, NQ)], pF[:, n, :], ACT.Identity,
                                               bias=m.late["x1_bv"][:, n:n + 1]).then_inc(f_done, 1)
                        if before:
                            high_probs(t - 1, 0)
                        beside_piece(t, 0)
                        if before:
                            high_probs(t - 1, 1)
                            high_probs(t - 1, 2)
                        if now:
                            act.wait_ge(nmax_done, 1 + k0 + t + 1)
                            act.wait_ge(t_done, 1 + (k0 + max(t - 1, least)) * NG)
                            act.wait_ge(rinv_done, 1 + k0 + max(t - 1, least))
                            act.activation(prob[:, t % 2, :], pS[:, 0:M], ACT.Exp, bias=nmax[:, t % 2:t % 2 + 1], scale=SCALE,
                                           accum_out=rsum[:, t % 2:t % 2 + 1]).then_inc(exp_done, 1)
                        beside_piece(t, 1)
                        if before:
                            high_probs(t - 1, 3)

                for n in range(KC):
                    act.wait_ge(q_mm, n + 1)
                    act.activation(qT[:, n, :], pT[:, n, :], ACT.Identity, bias=m.late["x1_bq"][:, n:n + 1]).then_inc(q_done, 1)
                for n in range(KC):
                    act.wait_ge(q_done, n + 1)
                    for e in range(2):
                        act.activation(qch[:, n, :, e, :], by_batch(qT[:, n, :]), ACT.Copy,
                                       scale=parity[:, e:e + 1]).then_inc(qch_done, 1)
                for i in range(NP):
                    piece(0, 0, i, pS[:, BANK * (i % 4):BANK * (i % 4) + BANK], False)
                bodies(act, body)

            @block.vector
            def _(dve):
                for s in (lo_done, mx_done, nmax_done, rinv_done, u_done, kv_lo):
                    dve.sem_inc(s, 1)

                def piece(b, par, i, src):
                    dve.wait_ge(kv_hi, 1 + b * NP + i + 1)
                    kind, n, x = PIECES[i]
                    if kind == "k":
                        s, z = SEG[x]
                        dve.scalar_tensor_tensor(kl[:, n, s:s + z], src[:, 0:z], m.late["x1_bk"][:, n:n + 1],
                                                 kh[:, n, s:s + z], ALU.add, ALU.subtract).then_inc(kv_lo, 1)
                    else:
                        r = min(P, M - P * x[0])
                        v = vhl[par][0:r, x[0]:x[-1] + 1, :, :]
                        dve.tensor_tensor(v[:, :, :, 32:64], src[0:r, 0:D * len(x)].rearrange(
                            "p (c a e) -> p c a e", a=PAIRS, e=32), v[:, :, :, 0:32], ALU.subtract).then_inc(kv_lo, 1)

                def body(b, first, last):
                    k0 = b * PAIRS
                    least = 0 if first else -9

                    def low_probs(t, g):
                        cs = TGRP[g][1]
                        n = 4 * t + g
                        w = min(P, M - P * cs[0])
                        dve.wait_ge(hi_done, 1 + (k0 + t) * NG + g + 1)
                        dve.tensor_tensor(ptl[0:w, t % 2, cs[0]:cs[-1] + 1, :], pT[0:w, n % 2, 0:P * len(cs)].rearrange(
                            "p (c r) -> p c r", r=P), pth[0:w, t % 2, cs[0]:cs[-1] + 1, :], ALU.subtract).then_inc(lo_done, 1)

                    def maxima(t, half):
                        a, z = (0, 2 * BANK) if half == 0 else (2 * BANK, M)
                        dve.wait_ge(s_done, 1 + (k0 + t) * 2 + half + 1)
                        dve.tensor_reduce(mx[:, half:half + 1], pS[:, a:z], AX_X, ALU.max, negate=True).then_inc(mx_done, 1)

                    def beside_piece(t, half):
                        i = beside(t, half)
                        par = t // PAIRS
                        if i is not None and not (last and par):
                            piece(b + par + 1, 1 - par, i, pK)

                    for t in range(T2 + 3 if last else T2):
                        now, before = t < T2, least + 1 <= t <= T2
                        if now:
                            maxima(t, 0)
                        if before:
                            low_probs(t - 1, 0)
                        if now:
                            maxima(t, 1)
                            dve.wait_ge(mx_done, 1 + (k0 + t + 1) * 2)
                            dve.tensor_scalar(nmax[:, t % 2:t % 2 + 1], mx[:, 0:1], mx[:, 1:2], SCALE, ALU.min,
                                              ALU.mult).then_inc(nmax_done, 1)
                        beside_piece(t, 0)
                        if before:
                            s = (t - 1) % 2
                            dve.wait_ge(exp_done, 1 + k0 + t)
                            dve.wait_ge(u_done, 1 + k0 + max(t - 2, least))
                            dve.reciprocal(rinv[:, s:s + 1], rsum[:, s:s + 1]).then_inc(rinv_done, 1)
                        if least + 2 <= t <= T2 + 1:
                            par, p, s = (t - 2) // PAIRS, (t - 2) % PAIRS, t % 2
                            dve.wait_ge(rinv_done, 1 + k0 + t - 1)
                            dve.wait_ge(av_done, 1 + k0 + t - 1)
                            if p == 0:
                                dve.wait_ge(f_mm, 1 + (b if first else b + par - 1))
                            dve.scalar_tensor_tensor(u[:, par % 2, :, p, :], pU.rearrange("p (a c) -> p a c", a=2),
                                                     rinv[:, s:s + 1], rowmask, ALU.mult, ALU.mult).then_inc(u_done, 1)
                        if before:
                            low_probs(t - 1, 1)
                            low_probs(t - 1, 2)
                        beside_piece(t, 1)
                        if before:
                            low_probs(t - 1, 3)

                for n in range(KC):
                    for e in range(2):
                        dve.wait_ge(qch_done, 2 * n + e + 1)
                        dve.scalar_tensor_tensor(qcl[:, n, :, e, :], by_batch(qT[:, n, :]), parity[:, e:e + 1],
                                                 qch[:, n, :, e, :], ALU.mult, ALU.subtract).then_inc(qcl_done, 1)
                for i in range(NP):
                    piece(0, 0, i, pS[:, BANK * (i % 4):BANK * (i % 4) + BANK])
                bodies(dve, body)


def l1x(nc, m, d, c0):
    with ExitStack() as ctx:
        sb, ps, sem = names(nc, ctx)
        oT = sb("x1_oT", [P, KC, TOK])
        c0.hl.append(Parts(sb, "x1_ctx1", False))
        l1x_tiles(nc, m, d, c0, oT)
        project(nc, m, "xp", oT, m.late["x1_wo"], m.late["x1_bo"][:, :])


MAGIC = 1.5 * 2 ** 23


class QuantWeights:
    def __init__(self, sb, sem):
        self.wq = sb("ff_wq", [P, KC, FF], BF16)
        self.wo = sb("ff_woq", [P, FC, D], BF16)
        self.am = sb("ff_am", [P, 2, FC])
        self.rs = sb("ff_rs", [P, 2, FC])
        self.dq = sb("ff_dq", [P, 2, FC])
        self.w1 = sb("ff_w1", [P, FC, D])
        self.w2 = sb("ff_w2", [P, FC, D])
        self.w1q = sb("ff_w1q", [P, FC, D], BF16)
        self.idb = sb("ff_idb", [P, P], BF16)
        self.chain, self.chain2, self.id_done, self.w_t, self.w_c, self.scaled, self.wo_done = (
            sem("ff_" + n) for n in ("chain", "chain2", "id_done", "w_t", "w_c", "scaled", "wo_done"))

    def scales(self, dve, m):
        loaded(m, dve, "ff")
        link = chained(dve, self.chain)
        am, rs, dq = self.am, self.rs, self.dq
        for n, w in ((0, m.late["ff_w_in"]), (1, m.late["ff_w_out"])):
            link(dve.tensor_reduce(am[:, n, :], w[:, :, :], AX_X, ALU.max, apply_absolute_value=True))
            link(dve.tensor_scalar(am[:, n, :], am[:, n, :], 1e-8, None, ALU.max))
            link(dve.reciprocal(rs[:, n, :], am[:, n, :]))
            link(dve.tensor_scalar(rs[:, n, :], rs[:, n, :], 127.0, None, ALU.mult))
            link(dve.tensor_scalar(dq[:, n, :], am[:, n, :], 1 / 127.0, None, ALU.mult))

    def scale(self, act, m, n):
        w, o = ((m.late["ff_w_in"], self.w1), (m.late["ff_w_out"], self.w2))[n]
        act.wait_ge(self.chain, 5 * n + 4)
        for c in range(FC):
            act.activation(o[:, c, :], w[:, c, :], ACT.Copy, scale=self.rs[:, n, c:c + 1]).then_inc(self.scaled, 1)

    def round(self, dve, pW):
        w1, w2, half = self.w1, self.w2, FC // 2
        dve.wait_ge(self.scaled, 2 * FC)
        link = chained(dve, self.chain2)
        for n in range(2):
            c = slice(half * n, half * n + half)
            link(dve.tensor_scalar(w1[:, c, :], w1[:, c, :], 127.0, -128.0, ALU.min, ALU.max))
            link(dve.tensor_scalar(self.w1q[:, c, :], w1[:, c, :], MAGIC, MAGIC, ALU.add, ALU.subtract))
        for n in range(2):
            c = slice(half * n, half * n + half)
            link(dve.tensor_scalar(w2[:, c, :], w2[:, c, :], 127.0, -128.0, ALU.min, ALU.max))
            dve.tensor_scalar(self.wo[:, c, :], w2[:, c, :], MAGIC, MAGIC, ALU.add, ALU.subtract).then_inc(self.wo_done, 1)
        for h in range(2):
            dve.wait_ge(self.w_t, h + 1)
            dve.tensor_copy(self.wq[:, :, BANK * h:BANK * h + BANK], pW[:, h, :, :]).then_inc(self.w_c, 1)

    def turn(self, pe, pW):
        pe.wait_ge(self.id_done, 1)
        for h in range(2):
            pe.wait_ge(self.chain2, 2 * (h + 1))
            for c in range(KC):
                for a in range(4):
                    mm = pe.transpose(pW[:, h, c, P * a:P * a + P], self.w1q[:, 4 * h + a, P * c:P * c + P], self.idb[:, :])
            mm.then_inc(self.w_t, 1)


def l1_attn(nc, m, d, w):
    with ExitStack() as ctx:
        sb, ps, sem = names(nc, ctx)
        x2 = sb("a1_x2", [P, TT, D])
        x2T = sb("a1_x2T", [P, KC, TOK])
        layer_norm(nc, m, "ln4b", m.xn, x2, x2T, (m.late["a1_gamma"][:, :], m.late["a1_beta"][:, :], "a1"))
        qk = sb("a1_qk", [P, TT, 2 * D])
        kT = sb("a1_kT", [P, KC, TOK])
        qT = sb("a1_qT", [P, KC, TOK])
        vhl = sb("a1_vhl", [P, TT, H, 32], BF16)
        gates = sb("a1_gates", [P, TT, 2 * H])
        o = sb("a1_o", [P, TT, D])
        with ExitStack() as c2:
            sb2, ps2, sem2 = names(nc, c2)
            sq = sb2("a1_sq", [P, TT, 2 * D])
            ss = sb2("a1_ss", [P, TT, 2 * H])
            qg = sb2("a1_qg", [P, TT, 2 * D])
            gg = sb2("a1_gg", [P, TT, 2 * H])
            nrm = sb2("a1_nrm", [P, TT, 2 * H])
            vg = sb2("a1_vg", [P, TT, D])
            pqk = ps2("a1_pqk", [P, TT, BANK])
            pv = ps2("a1_pv", [P, TT, BANK])
            qk_mm, v_mm, qk_done, chain, nrm_done, sig_done, turned, copied, v_hi, v_lo, sq_done, ss_done, qg_done, gg_done = (
                sem2("a1_" + n) for n in ("qk_mm", "v_mm", "qk_done", "chain", "nrm_done", "sig_done", "turned",
                                          "copied", "v_hi", "v_lo", "sq_done", "ss_done", "qg_done",
                                          "gg_done"))

            def by_head(a, n):
                return a.rearrange("p t (h e) -> p t h e", h=n)

            with nc.Block() as block:
                @block.tensor
                def _(pe):
                    for t in range(TT):
                        s = slice(P * t, P * t + P)
                        for c in range(KC):
                            mm = pe.matmul(pqk[:, t, :], x2T[:, c, s], m.late["a1_wqk"][:, c, :], start=(c == 0), stop=(c == KC - 1))
                        mm.then_inc(qk_mm, 1)
                    for t in range(TT):
                        s = slice(P * t, P * t + P)
                        for c in range(KC):
                            mm = pe.matmul(pv[:, t, 0:D], m.xnT[:, c, s], m.late["a1_wv"][:, c, :], start=(c == 0), stop=(c == KC - 1))
                        mm.then_inc(v_mm, 1)
                    pe.wait_ge(chain, 4)
                    for n in range(4):
                        for t in range(TT):
                            mm = pe.transpose(pqk[:, n, P * t:P * t + P], qk[:, t, P * n:P * n + P], m.ident[:, :])
                        mm.then_inc(turned, 1)

                @block.scalar
                def _(act):
                    for t in range(TT):
                        act.wait_ge(qk_mm, t + 1)
                        act.activation(qk[:, t, :], pqk[:, t, :], ACT.Copy).then_inc(qk_done, 1)
                        act.activation(sq[:, t, :], pqk[:, t, :], ACT.Square).then_inc(sq_done, 1)
                    w.scale(act, m, 0)
                    act.wait_ge(ss_done, TT)
                    act.activation(nrm[:, :, :], ss[:, :, :], ACT.Sqrt).then_inc(nrm_done, 1)
                    w.scale(act, m, 1)
                    act.wait_ge(chain, 3)
                    act.activation(gates[:, :, :], gg[:, :, :], ACT.Sigmoid).then_inc(sig_done, 1)
                    for n in range(4):
                        act.wait_ge(turned, n + 1)
                        o_ = (qT if n < 2 else kT)[:, n % 2, :]
                        act.activation(o_, pqk[:, n, :], ACT.Copy).then_inc(copied, 1)
                    act.wait_ge(chain, 6)
                    for t in range(TT):
                        act.activation(vhl[:, t, :, 0:16], by_head(vg[:, :, :], H)[:, t], ACT.Copy).then_inc(v_hi, 1)

                @block.vector
                def _(dve):
                    w.scales(dve, m)
                    inv = nrm
                    q4 = by_head(qk[:, :, :], 2 * H)
                    link = chained(dve, chain)
                    for t in range(TT):
                        dve.wait_ge(sq_done, t + 1)
                        ins = dve.tensor_reduce(ss[:, t, :], sq[:, t, :].rearrange("p (h e) -> p h e", e=16), AX_X, ALU.add)
                        ins.then_inc(ss_done, 1)
                    for t in range(TT):
                        dve.wait_ge(qg_done, t + 1)
                        dve.tensor_reduce(gg[:, t, :], qg[:, t, :].rearrange("p (h e) -> p h e", e=16), AX_X,
                                          ALU.add).then_inc(gg_done, 1)
                    dve.wait_ge(nrm_done, 1)
                    link(dve.tensor_scalar(nrm[:, :, :], nrm[:, :, :], 1e-12, None, ALU.max))
                    link(dve.reciprocal(inv[:, :, :], nrm[:, :, :]))
                    dve.wait_ge(gg_done, TT)
                    link(dve.tensor_tensor(gg[:, :, :], gg[:, :, :], inv[:, :, :], ALU.mult))
                    link(dve.tensor_tensor(q4, q4, inv[:, :, :].unsqueeze(3).broadcast_to([P, TT, 2 * H, 16]), ALU.mult))
                    dve.wait_ge(sig_done, 1)
                    dve.wait_ge(v_mm, TT)
                    link(dve.tensor_scalar(gates[:, :, :], gates[:, :, :], 0.75, 0.25, ALU.mult, ALU.add))
                    link(dve.tensor_tensor(
                         by_head(vg[:, :, :], H), pv[:, :, 0:D].rearrange("p t (h e) -> p t h e", h=H),
                         gates[:, :, H:2 * H].unsqueeze(3).broadcast_to([P, TT, H, 16]), ALU.mult))
                    for t in range(2):
                        dve.wait_ge(v_hi, t + 1)
                        dve.tensor_tensor(vhl[:, t, :, 16:32], by_head(vg[:, :, :], H)[:, t], vhl[:, t, :, 0:16],
                                          ALU.subtract).then_inc(v_lo, 1)

                @block.gpsimd
                def _(pool):
                    pool.tensor_copy(w.idb[:, :], m.ident[:, :]).then_inc(w.id_done, 1)
                    pool.wait_ge(w.id_done, 1)
                    for t in range(TT):
                        pool.wait_ge(qk_done, t + 1)
                        pool.tensor_tensor(qg[:, t, :], qk[:, t, :], m.late["a1_g"][:, :], ALU.mult).then_inc(qg_done, 1)
                    v4 = by_head(vg[:, :, :], H)
                    for t in range(2, TT):
                        pool.wait_ge(v_hi, t + 1)
                        pool.tensor_tensor(vhl[:, t, :, 16:32], v4[:, t], vhl[:, t, :, 0:16], ALU.subtract).then_inc(v_lo, 1)
        heads16(nc, m, "ah", qT, kT, vhl, o, lambda t: gates[:, t, 0:H].unsqueeze(2).broadcast_to([P, H, 16]), None)
        project(nc, m, "ap", kT, m.late["a1_wo"], m.late["a1_bo"][:, :], src=o, w=w)


def l1_ffn(nc, m, d, w):
    with ExitStack() as ctx:
        sb, ps, sem = names(nc, ctx)
        wq, wo, dq = w.wq, w.wo, w.dq
        xq = sb("ff_xq", [P, TT, D])
        xh = sb("ff_xh", [P, KC, TOK], BF16)
        xl = sb("ff_xl", [P, KC, TOK], BF16)
        hid = sb("ff_hid", [P, FC, TOK])
        cols = sb("ff_cols", [P, 8])
        hmax = sb("ff_hmax", [P, FC])
        top = sb("ff_top", [1, 2])
        sc = sb("ff_sc", [P, 2, 2])
        dqx = sb("ff_dqx", [P, FC])
        pM = ps("ff_pM", [P, BANK])
        pXT = ps("ff_pXT", [P, KC, BANK])
        pH = ps("ff_pH", [P, 2, BANK])
        chain, m_mm, turned, xhi, h_mm, h_done, hm_done, x_mm = (
            sem("fg_" + n) for n in ("chain", "m_mm", "turned", "xhi", "h_mm", "h_done", "hm_done", "x_mm"))
        steps = [0]

        def largest(dve, link, column, k):
            dve.wait_ge(m_mm, 2 * k + 1)
            link(dve.tensor_reduce(top[0:1, k:k + 1], pM[0:1, 0:P], AX_X, ALU.max))
            link(dve.tensor_scalar(top[0:1, k:k + 1], top[0:1, k:k + 1], 1e-8, None, ALU.max))
            dve.wait_ge(m_mm, 2 * k + 2)
            link(dve.tensor_copy(cols[:, 2 + k:3 + k], pM[:, P:P + 1]))
            link(dve.reciprocal(sc[:, k, 0:1], cols[:, 2 + k:3 + k]))
            link(dve.tensor_scalar(sc[:, k, 0:1], sc[:, k, 0:1], 32767.0, None, ALU.mult))
            link(dve.tensor_scalar(sc[:, k, 1:2], cols[:, 2 + k:3 + k], 1 / 32767.0, None, ALU.mult))

        C_AMAX, C_TOP, C_XQ = 1, 3, 10
        with nc.Block() as block:
            @block.vector
            def _(dve):
                def link(ins):
                    steps[0] += 1
                    ins.then_inc(chain, 1)
                    dve.wait_ge(chain, steps[0])

                link(dve.tensor_reduce(cols[:, 0:1], m.xn[:, :, :].rearrange("p t f -> p (t f)"), AX_X, ALU.max,
                                       apply_absolute_value=True))
                largest(dve, link, 0, 0)
                link(dve.tensor_scalar(xq[:, :, :], m.xn[:, :, :], sc[:, 0, 0:1], 32767.0, ALU.mult, ALU.min))
                link(dve.tensor_scalar(xq[:, :, :], xq[:, :, :], -32768.0, MAGIC, ALU.max, ALU.add))
                link(dve.tensor_scalar(xq[:, :, :], xq[:, :, :], MAGIC, None, ALU.subtract))
                assert steps[0] == C_XQ
                link(dve.tensor_scalar(dqx[:, :], dq[:, 0, :], sc[:, 0, 1:2], None, ALU.mult))
                for c in range(KC):
                    dve.wait_ge(xhi, c + 1)
                    link(dve.tensor_tensor(xl[:, c, :], pXT[:, c, :], xh[:, c, :], ALU.subtract))
                link(dve.tensor_tensor(m.x[:, :, :], m.x[:, :, :], m.late["ff_b_out"][:, :].unsqueeze(1).broadcast_to([P, TT, D]),
                                       ALU.add))
                for n in range(FC):
                    dve.wait_ge(h_done, n + 1)
                    dve.tensor_reduce(hmax[:, n:n + 1], hid[:, n, :], AX_X, ALU.max, apply_absolute_value=True).then_inc(
                        hm_done, 1)
                dve.wait_ge(hm_done, FC)
                link(dve.tensor_reduce(cols[:, 1:2], hmax[:, :], AX_X, ALU.max))

            @block.scalar
            def _(act):
                for c in range(KC):
                    act.wait_ge(turned, c + 1)
                    act.activation(xh[:, c, :], pXT[:, c, :], ACT.Copy).then_inc(xhi, 1)
                act.wait_ge(chain, C_XQ + 1)
                for n in range(FC):
                    act.wait_ge(h_mm, n + 1)
                    act.activation(hid[:, n, :], pH[:, n % 2, :], ACT.Gelu, bias=m.late["ff_b_in"][:, n:n + 1],
                                   scale=dqx[:, n:n + 1]).then_inc(h_done, 1)

            @block.tensor
            def _(pe):
                pe.wait_ge(chain, C_AMAX)
                pe.transpose(pM[0:1, 0:P], cols[:, 0:1], m.ident[:, :]).then_inc(m_mm, 1)
                pe.wait_ge(chain, C_TOP)
                pe.matmul(pM[:, P:P + 1], m.ones_row, top[0:1, 0:1], start=True, stop=True).then_inc(m_mm, 1)
                pe.wait_ge(chain, C_XQ)
                for c in range(KC):
                    for t in range(TT):
                        mm = pe.transpose(pXT[:, c, P * t:P * t + P], xq[:, t, P * c:P * c + P], m.ident[:, :])
                    mm.then_inc(turned, 1)
                pe.wait_ge(chain, C_XQ + 1 + KC)
                for n in range(FC):
                    if n >= 2:
                        pe.wait_ge(h_done, n - 1)
                    for a in range(4):
                        c, xx = a // 2, (xh, xl)[a % 2]
                        mm = pe.matmul(pH[:, n % 2, :], wq[:, c, P * n:P * n + P], xx[:, c, :], start=(a == 0), stop=(a == 3))
                    mm.then_inc(h_mm, 1)
        pX = ps("ff_pX", [P, 2, BANK])
        chain2, x_done, hh_done, hl_done = (sem("fh_" + n) for n in ("chain", "x_done", "hh_done", "hl_done"))
        hh = sb("ff_hh", [P, FC, TOK], BF16)
        hl = sb("ff_hl", [P, FC, TOK], BF16)
        C_HID = 6
        with nc.Block() as block:
            @block.vector
            def _(dve):
                done = [0]

                def link(ins):
                    done[0] += 1
                    ins.then_inc(chain2, 1)
                    dve.wait_ge(chain2, done[0])

                largest(dve, link, 1, 1)
                for n in range(0, FC, 2):
                    for k, (a, b2, op0, op1) in enumerate(((sc[:, 1, 0:1], 32767.0, ALU.mult, ALU.min),
                                                           (-32768.0, MAGIC, ALU.max, ALU.add), (MAGIC, None, ALU.subtract, ALU.mult))):
                        for c in (n, n + 1):
                            if k:
                                dve.wait_ge(chain2, C_HID + 3 * n + 2 * k + c - n - 1)
                            dve.tensor_scalar(hid[:, c, :], hid[:, c, :], a, dq[:, 1, c:c + 1] if b2 is None else b2,
                                              op0, op1).then_inc(chain2, 1)
                for t in range(TT):
                    dve.wait_ge(x_mm, t + 1)
                    dve.scalar_tensor_tensor(m.x[:, t, :], (pX if t < 2 else pXT)[:, t % 2, 0:D], sc[:, 1, 1:2], m.x[:, t, :],
                                             ALU.mult, ALU.add).then_inc(x_done, 1)

            @block.tensor
            def _(pe):
                pe.transpose(pM[0:1, 0:P], cols[:, 1:2], m.ident[:, :]).then_inc(m_mm, 1)
                pe.wait_ge(chain2, 2)
                pe.matmul(pM[:, P:P + 1], m.ones_row, top[0:1, 1:2], start=True, stop=True).then_inc(m_mm, 1)
                for n in range(FC):
                    pe.wait_ge(hh_done, n + 1)
                    pe.wait_ge(hl_done, n + 1)
                    for t in range(TT):
                        for part in (hh, hl):
                            mm = pe.matmul((pX if t < 2 else pXT)[:, t % 2, 0:D], part[:, n, P * t:P * t + P], wo[:, n, :],
                                           start=(n == 0 and part is hh), stop=(n == FC - 1 and part is hl))
                        if n == FC - 1:
                            mm.then_inc(x_mm, 1)

            @block.scalar
            def _(act):
                for n in range(FC):
                    act.wait_ge(chain2, C_HID + 3 * (n - n % 2) + 5 + n % 2)
                    act.activation(hh[:, n, :], hid[:, n, :], ACT.Copy).then_inc(hh_done, 1)

            @block.gpsimd
            def _(pool):
                for n in range(FC):
                    pool.wait_ge(hh_done, n + 1)
                    pool.tensor_tensor(hl[:, n, :], hid[:, n, :], hh[:, n, :], ALU.subtract).then_inc(hl_done, 1)


LATE = {
    "gl_wq": [P, KC, D], "gl_wkv": [P, KC, 2 * D], "gl_wf": [P, KC, 96], "gl_g1": [P, KC, 16], "gl_g2": [16, D],
    "gl_lnw": [P, D], "gl_wo": [P, KC, D], "gl_scanmask": [P, TOK],
    "x1_wq": [P, KC, D], "x1_bq": [P, KC], "x1_wkv": [P, 2, 2 * D], "x1_bk": [P, KC], "x1_bv": [P, KC],
    "x1_wo": [P, KC, D], "x1_bo": [1, D],
    "a1_wqk": [P, KC, 2 * D], "a1_wv": [P, KC, D], "a1_wo": [P, KC, D], "a1_bo": [1, D], "a1_gamma": [P, D],
    "a1_beta": [P, D], "a1_g": [P, 2 * D],
    "ff_w_in": [P, FC, D], "ff_w_out": [P, FC, D], "ff_b_in": [P, FC], "ff_b_out": [P, D],
    "mo_gate": [P, KC, E], "mo_wg": [P, E, KC, I], "mo_wu": [P, E, KC, I], "mo_wd": [P, E, D],
}


def load_weights(m, d, sp, layer):
    for name, shape in LATE.items():
        if name.startswith(layer):
            rank = len(shape)
            t = m.late[name]
            sp.dma_start(t[:, :] if rank == 2 else t[:, :, :] if rank == 3 else t[:, :, :, :],
                         d[name]).then_inc(m.weights_in[layer], 16)
            m.weights_n[layer] += 16


def room_for_weights(m, sb, layer):
    m.weights_n[layer] = 0
    m.late.update({name: sb("w_" + name, shape) for name, shape in LATE.items() if name.startswith(layer)})


def clear_semaphores(nc):
    done = sorted(nc.released_uncleared_semaphores)
    runs, start = [], None
    for n, s in enumerate(done):
        start = s if start is None else start
        if n + 1 == len(done) or done[n + 1] != s + 1:
            runs.append(range(start, s + 1))
            start = None
    with nc.Block() as block:
        @block.gpsimd
        def _(pool):
            for r in runs:
                pool.sem_clear(r)


def build(nc, d, out):
    with ExitStack() as ctx:
        sb, ps, sem = names(nc, ctx)
        m = Shared()
        m.x_loaded, m.const_loaded, m.w0_loaded, m.onehot_made, m.stored = (
            sem(n) for n in ("x_loaded", "const_loaded", "w0_loaded", "onehot_made", "stored"))
        m.weights_in = {layer: sem(layer + "_weights_in") for layer in ("gl", "mo", "x1", "a1", "ff")}
        m.weights_n = {}
        m.x = sb("x", [P, TT, D])
        m.xn = sb("xn", [P, TT, D])
        m.xnT = sb("xnT", [P, KC, TOK])
        m.ident = sb("ident", [P, P])
        m.onehot = sb("onehot", [96, H, P], BF16)
        m.maskneg = sb("maskneg", [P, BANK])
        m.mask05 = sb("mask05", [P, BANK])
        m.small = sb("small", [P, SMALL["n"]])
        m.eps = m.small[:, SMALL["eps"]:SMALL["eps"] + 1]
        m.one = m.small[:, SMALL["ones"]:SMALL["ones"] + 1]
        m.tanh_bias = m.small[:, SMALL["tanh"]:SMALL["tanh"] + 1]
        m.ones_row = m.small[0:1, SMALL["ones"]:SMALL["ones"] + P]
        m.const_n, m.w0_n = 32, 80
        m.late = {"onehot": m.onehot}
        for layer in ("gl", "x1"):
            room_for_weights(m, sb, layer)
        with ExitStack() as c2:
            sb2, _, _ = names(nc, c2)
            m.wv0 = sb2("wv0", [P, 2, 1024])
            m.wo0 = sb2("wo0", [P, PAIRS, D])
            m.bo0 = sb2("bo0", [1, D])
            m.quA = sb2("quA", [P, 2, B, PAIRS, P], BF16)
            m.quB = sb2("quB", [P, B, PAIRS, P], BF16)
            with ExitStack() as c3:
                c0 = context0(nc, c3)
                with ExitStack() as c4:
                    sb4, _, _ = names(nc, c4)
                    c0.wq = sb4("wq0", [P, KC, 1024])
                    c0.wk = sb4("wk0", [P, PAIRS, D])
                    layer_norm(nc, m, "ln0", m.x, m.xn, m.xnT, start=lambda sp: load_inputs(sp, m, d, c0))
                    l0x_queries(nc, m, d, c0)
                m.wvh, m.wvl = (names(nc, c3)[0](n, [P, 2, 1024], BF16) for n in ("wv0h", "wv0l"))
                l0x_attention(nc, m, d, c0)
                l0x_output(nc, m, d)
        with ExitStack() as c2:
            sb2, _, sem2 = names(nc, c2)
            early = ContextL1(sb2, sem2)
            with ExitStack() as c3:
                room_for_weights(m, names(nc, c3)[0], "mo")
                layer_norm(nc, m, "ln1", m.x, m.xn, m.xnT, start=lambda sp: load_weights(m, d, sp, "mo"))
                l0_gla(nc, m, d)
                layer_norm(nc, m, "ln2", m.x, m.xn, m.xnT)
                l0_moe(nc, m, d, early)
            clear_semaphores(nc)
            layer_norm(nc, m, "ln3", m.x, m.xn, m.xnT)
            l1x(nc, m, d, early)
        with ExitStack() as c2:
            sb2, _, sem2 = names(nc, c2)
            room_for_weights(m, sb2, "a1")
            room_for_weights(m, sb2, "ff")
            w = QuantWeights(sb2, sem2)
            layer_norm(nc, m, "ln4", m.x, m.xn, m.xnT,
                       start=lambda sp: [load_weights(m, d, sp, layer) for layer in ("a1", "ff")])
            l1_attn(nc, m, d, w)
            layer_norm(nc, m, "ln5", m.x, m.xn, None)
            l1_ffn(nc, m, d, w)
        with nc.Block() as block:
            @block.sync
            def _(sp):
                sp.wait_ge(m.w0_loaded, m.w0_n)
                sp.dma_start(out, m.x[:, :, :]).then_inc(m.stored, 16)
                sp.wait_ge(m.stored, 16)


SMALL = {"eps": 0, "ones": 1, "hmask": 129, "desc": 137, "tanh": 145, "rowmask": 146, "fold": 210, "onehot": 274, "parity": 290,
         "n": 292}


def layouts(v):
    f = np.float32
    c = np.ascontiguousarray

    def rows(w, n=P):
        w = np.asarray(w)
        return c(w.reshape(-1, n, w.shape[1]).transpose(1, 0, 2))

    a = {}
    a["x"] = rows(v["x"].reshape(TOK, D))
    ctx = v["ctx_768"]
    pad = np.zeros((B, MC * P, DC), f)
    pad[:, :M] = ctx
    a["ctxn"] = c(pad.reshape(B, MC, P, DC).transpose(0, 2, 1, 3))
    a["ctxT"] = c(ctx.transpose(0, 2, 1))
    a["wq0"] = rows(v["L0_xattn_Wq"])
    wkT = v["L0_xattn_Wk"].T
    a["wk0"] = rows(np.concatenate([wkT, wkT[:, P:]], axis=1))
    wv = v["L0_xattn_Wv"]
    a["wv0"] = c(np.stack([wv[:P], np.concatenate([wv[P:], wv[P:]])], axis=1))
    a["wo0"] = rows(v["L0_xattn_Wo"])
    a["bo0"] = c(v["L0_xattn_bo"][None])
    a["ident"] = np.eye(P, dtype=f)
    s, t = np.arange(P)[:, None], np.arange(P)[None]
    same = s // NQ == t // NQ
    a["maskneg"] = np.tile(np.where(same & (s <= t), 0, -1e30).astype(f), (1, 4))
    a["mask05"] = np.tile(np.where(same, 0.5, 0).astype(f), (1, 4))
    small = np.zeros((P, SMALL["n"]), f)
    small[:, SMALL["eps"]] = 1e-5
    small[:, SMALL["ones"]:SMALL["ones"] + P] = 1
    small[:, SMALL["hmask"]:SMALL["hmask"] + 8] = np.arange(P)[:, None] // 16 == np.arange(8)
    small[:, SMALL["desc"]:SMALL["desc"] + E] = E - np.arange(E)
    small[:, SMALL["tanh"]] = -15.0 * 0.27
    r = np.arange(P)[:, None]
    small[:, SMALL["rowmask"]:SMALL["rowmask"] + 64] = r // NQ == np.arange(64) % 32 // 16
    small[:, SMALL["fold"]:SMALL["fold"] + NQ] = r % NQ == np.arange(NQ)
    small[:, SMALL["onehot"]:SMALL["onehot"] + H] = r % 32 == np.arange(H)
    small[:, SMALL["parity"]:SMALL["parity"] + 2] = r // 16 % 2 == np.arange(2)
    a["small"] = small

    gl = {n: v["L0_attn_" + n] for n in ("Wq", "Wk", "Wv", "Wf", "Wg1", "Wg2", "ln_w", "Wo")}
    a["gl_wq"] = rows(gl["Wq"].T)
    a["gl_wkv"] = rows(np.concatenate([gl["Wk"].T, gl["Wv"].T], axis=1))
    wf = np.zeros((D, 96), f)
    for n in range(3):
        wf[:, 32 * n:32 * n + 16] = gl["Wf"].T
    a["gl_wf"] = rows(wf)
    a["gl_g1"] = rows(gl["Wg1"].T)
    a["gl_g2"] = c(gl["Wg2"].T)
    a["gl_lnw"] = c(np.broadcast_to(gl["ln_w"], (P, D)))
    a["gl_wo"] = rows(gl["Wo"].T)
    a["gl_scanmask"] = np.tile((np.arange(TOK) % NQ != 0).astype(f), (P, 1))
    a["mo_gate"] = rows(v["L0_ffn_gate_w"].T)
    for n, w in (("mo_wg", "w_gate"), ("mo_wu", "w_up")):
        a[n] = c(v["L0_ffn_" + w].reshape(E, I, KC, P).transpose(3, 0, 2, 1))
    a["mo_wd"] = c(v["L0_ffn_w_down"].transpose(2, 0, 1))

    def cols(b, n=P):
        return c(np.asarray(b).reshape(-1, n).T)

    x1 = {n: v["L1_xattn_" + n] for n in ("Wq", "bq", "Wkv", "bkv", "Wo", "bo")}
    ik = (np.arange(H)[:, None] * 32 + np.arange(16)).ravel()
    a["x1_wq"] = rows(x1["Wq"].T)
    a["x1_bq"] = cols(x1["bq"])
    wkv = x1["Wkv"][np.concatenate([ik, ik + 16])].T
    a["x1_wkv"] = c(np.stack([wkv[:P], np.concatenate([wkv[P:], wkv[P:]])], axis=1))
    a["x1_bk"] = cols(x1["bkv"][ik])
    a["x1_bv"] = cols(x1["bkv"][ik + 16])
    a["x1_wo"] = rows(x1["Wo"].T)
    a["x1_bo"] = c(x1["bo"][None])
    a1 = {n: v["L1_attn_" + n] for n in ("w_q", "w_k", "w_v", "g_q", "g_k", "w_o", "b_o", "gamma", "beta")}
    a["a1_wqk"] = rows(np.concatenate([a1["w_q"], a1["w_k"]], axis=1))
    a["a1_wv"] = rows(a1["w_v"])
    a["a1_wo"] = rows(a1["w_o"])
    a["a1_bo"] = c(a1["b_o"][None])
    for n in ("gamma", "beta"):
        a["a1_" + n] = c(np.broadcast_to(a1[n], (P, D)))
    a["a1_g"] = c(np.broadcast_to(np.concatenate([np.tile(a1["g_q"], H), np.tile(a1["g_k"], H)]), (P, 2 * D)))
    a["ff_w_in"] = rows(v["L1_ffn_W_in"].T)
    a["ff_w_out"] = rows(v["L1_ffn_W_out"])
    a["ff_b_in"] = cols(v["L1_ffn_b_in"])
    a["ff_b_out"] = c(np.broadcast_to(v["L1_ffn_b_out"], (P, D)))
    return a


def kernel(**inputs):
    import concourse.bacc as _bacc
    from concourse.bass_utils import run_bass_kernel_spmd as _run

    arrays = layouts({k: np.asarray(v) for k, v in inputs.items()})
    nc = _bacc.Bacc("TRN2", target_bir_lowering=False, num_devices=1)
    d = {n: nc.dram_tensor(f"in_{n}", a.shape, mybir.dt.from_np(a.dtype), kind="ExternalInput").ap()
         for n, a in arrays.items()}
    out = nc.dram_tensor("out_x", (P, TT, D), F32, kind="ExternalOutput").ap()
    build(nc, d, out)
    r = _run(nc, [{f"in_{n}": a for n, a in arrays.items()}], core_ids=[0])
    y = np.asarray(r.results[0]["out_x"])
    return y.transpose(1, 0, 2).reshape(B, NQ, D)
```
